# Optimizing a Trainium2 kernel written in Bass

```python
import numpy as np
import jax
import jax.numpy as jnp

def _softmax(x, axis=-1):
    return jax.nn.softmax(x, axis=axis)

def _gelu(x):
    return jax.nn.gelu(x, approximate=True)

def _silu(x):
    return jax.nn.silu(x)

def _sigmoid(x):
    return jax.nn.sigmoid(x)

def _layernorm(x, axis=-1, eps=1e-05):
    m = jnp.mean(x, axis=axis, keepdims=True)
    v = jnp.var(x, axis=axis, keepdims=True)
    return (x - m) / jnp.sqrt(v + eps)

def _scatter_add(tgt, idx, src, axis=0):
    return tgt.at[idx].add(src)

def _segment_sum(src, seg, n):
    return jax.ops.segment_sum(src, seg, n)
kernel_name = 'mk_gnn_resnorm_d4_gnn_r8_45ff23'

def setup_inputs(seed: int=0):
    np.random.seed(seed)
    _w = jnp.asarray

    def _rec_inputs():
        import jax
        import jax.numpy as jnp
        _gk = jax.random.key(seed)
        x = -8.776e-05 + 1 * jax.random.normal(jax.random.fold_in(_gk, 1), (2500, 256), jnp.float32)
        src = jax.random.randint(jax.random.fold_in(_gk, 2), (80000,), 0, 2500, jnp.int32)
        dst = jax.random.randint(jax.random.fold_in(_gk, 3), (80000,), 0, 2500, jnp.int32)
        _o = jnp.argsort(dst, stable=True)
        src = src[_o]
        dst = dst[_o]
        edge_attr_384 = -4.94225e-05 + 0.999873 * jax.random.normal(jax.random.fold_in(_gk, 11), (80000, 384), jnp.float32)
        edge_attr_64 = 0.000312547 + 1.00004 * jax.random.normal(jax.random.fold_in(_gk, 12), (80000, 64), jnp.float32)
        edge_weight = jax.random.uniform(jax.random.fold_in(_gk, 14), (80000,), jnp.float32, 0.0, 0.999998)
        return (x, src, dst, edge_attr_384, edge_attr_64, edge_weight)
    x, src, dst, edge_attr_384, edge_attr_64, edge_weight = _rec_inputs()

    def _L0_gnn_setup():
        import jax, jax.numpy as jnp
        import numpy as np
        N_NODES = 2500
        key = jax.random.key(seed)
        k1, k2, k3, k4 = jax.random.split(key, 4)
        d = 256
        E = 40000
        x = jax.random.normal(k1, (N_NODES, d), dtype=jnp.float32)
        edge_index = jax.random.randint(k2, (2, E), 0, N_NODES, dtype=jnp.int64)
        limit = float(np.sqrt(6.0 / (d + d)))
        W_l = jax.random.uniform(k3, (d, d), dtype=jnp.float32, minval=-limit, maxval=limit)
        W_r = jax.random.uniform(k4, (d, d), dtype=jnp.float32, minval=-limit, maxval=limit)
        b_r = jnp.zeros((d,), dtype=jnp.float32)
        return {'x': x, 'edge_index': edge_index, 'W_l': W_l, 'W_r': W_r, 'b_r': b_r}
    _L0_gnn_all = _L0_gnn_setup()
    _L0_gnn_in = {k: v for k, v in _L0_gnn_all.items() if k in ('W_l', 'W_r', 'b_r')}
    del _L0_gnn_all

    def _L1_gnn_setup():
        import jax, jax.numpy as jnp
        import numpy as np
        N_NODES = 1250
        N_EDGES = 37500
        IN_FEAT = 256
        OUT_FEAT = 256
        EDGE_DIM = 384
        GRID_SIZE = 4
        SPLINE_ORDER = 3

        def _make_grid(in_features, grid_size=GRID_SIZE, k=SPLINE_ORDER, lo=-1.0, hi=1.0):
            h = (hi - lo) / grid_size
            g = jnp.arange(-k, grid_size + k + 1, dtype=jnp.float32) * h + lo
            return jnp.broadcast_to(g, (in_features, g.shape[0]))

        def _b_splines(x, grid, k=SPLINE_ORDER):
            xe = x[..., None]
            bases = ((xe >= grid[:, :-1]) & (xe < grid[:, 1:])).astype(x.dtype)
            for j in range(1, k + 1):
                left = (xe - grid[:, :-(j + 1)]) / (grid[:, j:-1] - grid[:, :-(j + 1)])
                right = (grid[:, j + 1:] - xe) / (grid[:, j + 1:] - grid[:, 1:-j])
                bases = left * bases[..., :-1] + right * bases[..., 1:]
            return bases
        key = jax.random.key(seed)
        ks = jax.random.split(key, 10)
        n_coef = GRID_SIZE + SPLINE_ORDER
        return {'x': jax.random.normal(ks[0], (N_NODES, IN_FEAT), jnp.float32), 'edge_attr': jax.random.normal(ks[1], (N_EDGES, EDGE_DIM), jnp.float32), 'edge_index': jax.random.randint(ks[2], (2, N_EDGES), 0, N_NODES, jnp.int64), 'W_edge': jax.random.normal(ks[3], (OUT_FEAT, EDGE_DIM), jnp.float32) * 0.03, 'b_edge': jnp.zeros((OUT_FEAT,), jnp.float32), 'W_node': jax.random.normal(ks[4], (OUT_FEAT, IN_FEAT), jnp.float32) * 0.03, 'b_node': jnp.zeros((OUT_FEAT,), jnp.float32), 'base_weight': jax.random.normal(ks[5], (OUT_FEAT, OUT_FEAT), jnp.float32) * 0.05, 'spline_weight': jax.random.normal(ks[6], (OUT_FEAT, OUT_FEAT, n_coef), jnp.float32) * 0.05, 'spline_scaler': jax.random.normal(ks[7], (OUT_FEAT, OUT_FEAT), jnp.float32) * 0.1 + 1.0}
    _L1_gnn_all = _L1_gnn_setup()
    _L1_gnn_in = {k: v for k, v in _L1_gnn_all.items() if k in ('W_edge', 'b_edge', 'W_node', 'b_node', 'base_weight', 'spline_weight', 'spline_scaler')}
    del _L1_gnn_all

    def _L2_gnn_setup():
        import jax, jax.numpy as jnp
        import numpy as np
        MIN_NORM = 1e-15
        BALL_EPS = 1e-05
        C = 1.0
        N_NODES, N_EDGES, D_IN, D_OUT = (5000, 40000, 256, 256)

        def _sqnorm(x):
            return jnp.sum(x * x, axis=-1, keepdims=True)

        def _norm(x):
            return jnp.maximum(jnp.sqrt(_sqnorm(x)), MIN_NORM)

        def _artanh(x):
            return jnp.arctanh(jnp.clip(x, -1.0 + 1e-07, 1.0 - 1e-07))

        def _lam(x, c):
            return jnp.maximum(2.0 / jnp.maximum(1.0 - c * _sqnorm(x), MIN_NORM), MIN_NORM)

        def mobius_add(x, y, c):
            x2, y2 = (_sqnorm(x), _sqnorm(y))
            xy = jnp.sum(x * y, axis=-1, keepdims=True)
            num = (1.0 + 2.0 * c * xy + c * y2) * x + (1.0 - c * x2) * y
            den = 1.0 + 2.0 * c * xy + c * c * x2 * y2
            return num / jnp.maximum(den, MIN_NORM)

        def expmap0(u, c):
            sc = jnp.sqrt(c)
            un = _norm(u)
            return jnp.tanh(sc * un) * u / (sc * un)

        def logmap0(p, c):
            sc = jnp.sqrt(c)
            pn = _norm(p)
            return _artanh(sc * pn) * p / (sc * pn)

        def expmap(u, base, c):
            sc = jnp.sqrt(c)
            un = _norm(u)
            second = jnp.tanh(sc * _lam(base, c) * un / 2.0) * u / (sc * un)
            return mobius_add(base, second, c)

        def logmap(p, base, c):
            sub = mobius_add(-base, p, c)
            sn = _norm(sub)
            sc = jnp.sqrt(c)
            return 2.0 / (sc * _lam(base, c)) * _artanh(sc * sn) * sub / sn

        def mobius_matvec(W, x, c):
            sc = jnp.sqrt(c)
            xn = _norm(x)
            mx = x @ W.T
            mxn = _norm(mx)
            res = jnp.tanh(mxn / xn * _artanh(sc * xn)) * mx / (mxn * sc)
            is_zero = jnp.all(mx == 0.0, axis=-1, keepdims=True)
            return jnp.where(is_zero, jnp.zeros_like(res), res)

        def project(x, c):
            n = _norm(x)
            maxn = (1.0 - BALL_EPS) / jnp.sqrt(c)
            return jnp.where(n > maxn, x / n * maxn, x)
        key = jax.random.key(seed)
        k1, k2, k3, k4, k5 = jax.random.split(key, 5)
        x_tan = 0.2 * jax.random.normal(k1, (N_NODES, D_IN), jnp.float32)
        x = project(expmap0(x_tan, C), C)
        bound = 0.05 * float(np.sqrt(6.0 / (D_IN + D_OUT)))
        weight = jax.random.uniform(k2, (D_OUT, D_IN), jnp.float32, -bound, bound)
        bias = 0.01 * jax.random.normal(k3, (D_OUT,), jnp.float32)
        edge_index = jax.random.randint(k4, (2, N_EDGES), 0, N_NODES, dtype=jnp.int32)
        edge_weight = jax.random.uniform(k5, (N_EDGES,), jnp.float32)
        return {'x': x, 'weight': weight, 'bias': bias, 'edge_index': edge_index, 'edge_weight': edge_weight}
    _L2_gnn_all = _L2_gnn_setup()
    _L2_gnn_in = {k: v for k, v in _L2_gnn_all.items() if k in ('weight', 'bias')}
    del _L2_gnn_all

    def _L3_gnn_setup():
        import jax, jax.numpy as jnp
        import numpy as np
        N, E, H, DE = (1250, 31250, 256, 64)
        EPS = 1e-05

        def _lin_init(k, fan_in, shape):
            s = 1.0 / np.sqrt(fan_in)
            return jax.random.uniform(k, shape, jnp.float32, -s, s)
        key = jax.random.key(seed)
        ks = jax.random.split(key, 12)
        x = jax.random.normal(ks[0], (N, H), jnp.float32)
        edge_index = jax.random.randint(ks[1], (2, E), 0, N)
        edge_attr = jax.random.normal(ks[2], (E, DE), jnp.float32)
        d_in = H + DE
        W1 = _lin_init(ks[3], d_in, (d_in, H))
        b1 = _lin_init(ks[4], d_in, (H,))
        W2 = _lin_init(ks[5], H, (H, H))
        b2 = _lin_init(ks[6], H, (H,))
        Wg = _lin_init(ks[7], d_in, (d_in, H))
        bg = _lin_init(ks[8], d_in, (H,))
        gamma = jnp.ones((H,), jnp.float32)
        beta = jnp.zeros((H,), jnp.float32)
        return {'x': x, 'edge_index': edge_index, 'edge_attr': edge_attr, 'W1': W1, 'b1': b1, 'W2': W2, 'b2': b2, 'Wg': Wg, 'bg': bg, 'gamma': gamma, 'beta': beta}
    _L3_gnn_all = _L3_gnn_setup()
    _L3_gnn_in = {k: v for k, v in _L3_gnn_all.items() if k in ('W1', 'b1', 'W2', 'b2', 'Wg', 'bg', 'gamma', 'beta')}
    del _L3_gnn_all
    return {'x': x, 'src': src, 'dst': dst, 'edge_attr_384': edge_attr_384, 'edge_attr_64': edge_attr_64, 'edge_weight': edge_weight, 'L0_gnn_W_l': _L0_gnn_in['W_l'], 'L0_gnn_W_r': _L0_gnn_in['W_r'], 'L0_gnn_b_r': _L0_gnn_in['b_r'], 'L1_gnn_W_edge': _L1_gnn_in['W_edge'], 'L1_gnn_b_edge': _L1_gnn_in['b_edge'], 'L1_gnn_W_node': _L1_gnn_in['W_node'], 'L1_gnn_b_node': _L1_gnn_in['b_node'], 'L1_gnn_base_weight': _L1_gnn_in['base_weight'], 'L1_gnn_spline_weight': _L1_gnn_in['spline_weight'], 'L1_gnn_spline_scaler': _L1_gnn_in['spline_scaler'], 'L2_gnn_weight': _L2_gnn_in['weight'], 'L2_gnn_bias': _L2_gnn_in['bias'], 'L3_gnn_W1': _L3_gnn_in['W1'], 'L3_gnn_b1': _L3_gnn_in['b1'], 'L3_gnn_W2': _L3_gnn_in['W2'], 'L3_gnn_b2': _L3_gnn_in['b2'], 'L3_gnn_Wg': _L3_gnn_in['Wg'], 'L3_gnn_bg': _L3_gnn_in['bg'], 'L3_gnn_gamma': _L3_gnn_in['gamma'], 'L3_gnn_beta': _L3_gnn_in['beta']}

def reference(x, src, dst, edge_attr_384, edge_attr_64, edge_weight, L0_gnn_W_l, L0_gnn_W_r, L0_gnn_b_r, L1_gnn_W_edge, L1_gnn_b_edge, L1_gnn_W_node, L1_gnn_b_node, L1_gnn_base_weight, L1_gnn_spline_weight, L1_gnn_spline_scaler, L2_gnn_weight, L2_gnn_bias, L3_gnn_W1, L3_gnn_b1, L3_gnn_W2, L3_gnn_b2, L3_gnn_Wg, L3_gnn_bg, L3_gnn_gamma, L3_gnn_beta):
    import jax
    import jax.numpy as jnp

    def _L0_gnn_ref(x, edge_index, W_l, W_r, b_r):
        import jax, jax.numpy as jnp
        import numpy as np
        N_NODES = 2500
        src, dst = (edge_index[0], edge_index[1])
        messages = x[src]
        sums = jax.ops.segment_sum(messages, dst, num_segments=N_NODES)
        counts = jax.ops.segment_sum(jnp.ones_like(dst, dtype=x.dtype), dst, num_segments=N_NODES)
        aggr = sums / jnp.maximum(counts, 1.0)[:, None]
        out = aggr @ W_l.T + x @ W_r.T + b_r
        return out

    def _L1_gnn_ref(x, edge_attr, edge_index, W_edge, b_edge, W_node, b_node, base_weight, spline_weight, spline_scaler):
        import jax, jax.numpy as jnp
        import numpy as np
        N_NODES = 1250
        N_EDGES = 37500
        IN_FEAT = 256
        OUT_FEAT = 256
        EDGE_DIM = 384
        GRID_SIZE = 4
        SPLINE_ORDER = 3

        def _make_grid(in_features, grid_size=GRID_SIZE, k=SPLINE_ORDER, lo=-1.0, hi=1.0):
            h = (hi - lo) / grid_size
            g = jnp.arange(-k, grid_size + k + 1, dtype=jnp.float32) * h + lo
            return jnp.broadcast_to(g, (in_features, g.shape[0]))

        def _b_splines(x, grid, k=SPLINE_ORDER):
            xe = x[..., None]
            bases = ((xe >= grid[:, :-1]) & (xe < grid[:, 1:])).astype(x.dtype)
            for j in range(1, k + 1):
                left = (xe - grid[:, :-(j + 1)]) / (grid[:, j:-1] - grid[:, :-(j + 1)])
                right = (grid[:, j + 1:] - xe) / (grid[:, j + 1:] - grid[:, 1:-j])
                bases = left * bases[..., :-1] + right * bases[..., 1:]
            return bases
        e = edge_attr @ W_edge.T + b_edge
        h = x @ W_node.T + b_node
        row, col = (edge_index[0], edge_index[1])
        msg = e * h[row]
        agg = jax.ops.segment_sum(msg, col, num_segments=x.shape[0])
        grid = _make_grid(OUT_FEAT)
        base = jax.nn.silu(agg) @ base_weight.T
        sp = _b_splines(agg, grid)
        scaled_w = spline_weight * spline_scaler[..., None]
        spline_out = jnp.einsum('nik,oik->no', sp, scaled_w)
        return base + spline_out

    def _L2_gnn_ref(x, weight, bias, edge_index, edge_weight):
        import jax, jax.numpy as jnp
        import numpy as np
        MIN_NORM = 1e-15
        BALL_EPS = 1e-05
        C = 1.0
        N_NODES, N_EDGES, D_IN, D_OUT = (5000, 40000, 256, 256)

        def _sqnorm(x):
            return jnp.sum(x * x, axis=-1, keepdims=True)

        def _norm(x):
            return jnp.maximum(jnp.sqrt(_sqnorm(x)), MIN_NORM)

        def _artanh(x):
            return jnp.arctanh(jnp.clip(x, -1.0 + 1e-07, 1.0 - 1e-07))

        def _lam(x, c):
            return jnp.maximum(2.0 / jnp.maximum(1.0 - c * _sqnorm(x), MIN_NORM), MIN_NORM)

        def mobius_add(x, y, c):
            x2, y2 = (_sqnorm(x), _sqnorm(y))
            xy = jnp.sum(x * y, axis=-1, keepdims=True)
            num = (1.0 + 2.0 * c * xy + c * y2) * x + (1.0 - c * x2) * y
            den = 1.0 + 2.0 * c * xy + c * c * x2 * y2
            return num / jnp.maximum(den, MIN_NORM)

        def expmap0(u, c):
            sc = jnp.sqrt(c)
            un = _norm(u)
            return jnp.tanh(sc * un) * u / (sc * un)

        def logmap0(p, c):
            sc = jnp.sqrt(c)
            pn = _norm(p)
            return _artanh(sc * pn) * p / (sc * pn)

        def expmap(u, base, c):
            sc = jnp.sqrt(c)
            un = _norm(u)
            second = jnp.tanh(sc * _lam(base, c) * un / 2.0) * u / (sc * un)
            return mobius_add(base, second, c)

        def logmap(p, base, c):
            sub = mobius_add(-base, p, c)
            sn = _norm(sub)
            sc = jnp.sqrt(c)
            return 2.0 / (sc * _lam(base, c)) * _artanh(sc * sn) * sub / sn

        def mobius_matvec(W, x, c):
            sc = jnp.sqrt(c)
            xn = _norm(x)
            mx = x @ W.T
            mxn = _norm(mx)
            res = jnp.tanh(mxn / xn * _artanh(sc * xn)) * mx / (mxn * sc)
            is_zero = jnp.all(mx == 0.0, axis=-1, keepdims=True)
            return jnp.where(is_zero, jnp.zeros_like(res), res)

        def project(x, c):
            n = _norm(x)
            maxn = (1.0 - BALL_EPS) / jnp.sqrt(c)
            return jnp.where(n > maxn, x / n * maxn, x)
        c = jnp.float32(C)
        N = x.shape[0]
        src, dst = (edge_index[0], edge_index[1])
        x_src = x[src]
        x_dst = x[dst]
        msg = logmap(x_src, x_dst, c)
        msg = msg * edge_weight[:, None]
        agg = jax.ops.segment_sum(msg, dst, num_segments=N)
        u = expmap(agg, x, c)
        h = mobius_matvec(weight, u, c)
        b_ball = expmap0(jnp.broadcast_to(bias, h.shape), c)
        h = mobius_add(h, b_ball, c)
        h_tan = jax.nn.relu(logmap0(h, c))
        h = expmap0(h_tan, c)
        return project(h, c)

    def _L3_gnn_ref(x, edge_index, edge_attr, W1, b1, W2, b2, Wg, bg, gamma, beta):
        import jax, jax.numpy as jnp
        import numpy as np
        N, E, H, DE = (1250, 31250, 256, 64)
        EPS = 1e-05

        def _lin_init(k, fan_in, shape):
            s = 1.0 / np.sqrt(fan_in)
            return jax.random.uniform(k, shape, jnp.float32, -s, s)
        src, dst = (edge_index[0], edge_index[1])
        ei = jnp.concatenate([x[src], edge_attr], axis=-1)
        core = jnp.maximum(ei @ W1 + b1, 0.0) @ W2 + b2
        gate = jax.nn.sigmoid(ei @ Wg + bg)
        msg = gate * core
        agg = jax.ops.segment_sum(msg, dst, num_segments=x.shape[0])
        out = agg + x
        mu = jnp.mean(out, axis=-1, keepdims=True)
        var = jnp.var(out, axis=-1, keepdims=True)
        out = (out - mu) * jax.lax.rsqrt(var + EPS) * gamma + beta
        return out
    edge_index = jnp.stack([src, dst])
    x = _layernorm(x + _L0_gnn_ref(x, edge_index, L0_gnn_W_l, L0_gnn_W_r, L0_gnn_b_r), axis=-1)
    x = _layernorm(x + _L1_gnn_ref(x, edge_attr_384, edge_index, L1_gnn_W_edge, L1_gnn_b_edge, L1_gnn_W_node, L1_gnn_b_node, L1_gnn_base_weight, L1_gnn_spline_weight, L1_gnn_spline_scaler), axis=-1)
    x = _layernorm(x + _L2_gnn_ref(x, L2_gnn_weight, L2_gnn_bias, edge_index, edge_weight), axis=-1)
    x = _layernorm(x + _L3_gnn_ref(x, edge_index, edge_attr_64, L3_gnn_W1, L3_gnn_b1, L3_gnn_W2, L3_gnn_b2, L3_gnn_Wg, L3_gnn_bg, L3_gnn_gamma, L3_gnn_beta), axis=-1)
    return x

_drawn_inputs = setup_inputs


def setup_inputs(seed=0):
    import zlib

    import numpy as np

    out = dict(_drawn_inputs(seed))
    spreads = {'L0_gnn_b_r': (0.0, 0.1),
     'L1_gnn_b_edge': (0.0, 0.1),
     'L1_gnn_b_node': (0.0, 0.1),
     'L3_gnn_gamma': (1.0, 0.2),
     'L3_gnn_beta': (0.0, 0.1)}
    factors = {'edge_weight': 8.0, 'L2_gnn_weight': 4.524, 'L2_gnn_bias': 8.0, 'L3_gnn_bg': 6.498}
    for name, (base, spread) in spreads.items():
        noise = np.random.default_rng([zlib.crc32(name.encode()), seed]).standard_normal(out[name].shape)
        drawn = base * np.exp(spread * noise) if base else spread * noise
        out[name] = jnp.asarray(drawn.astype(out[name].dtype))
    for name, factor in factors.items():
        out[name] = (out[name] * factor).astype(out[name].dtype)
    return out
```

```python
from contextlib import ExitStack

import concourse.bass as bass
from concourse import mybir

FP32 = mybir.dt.float32
BF16 = mybir.dt.bfloat16
I32 = mybir.dt.int32
ALU = mybir.AluOpType
ACT = mybir.ActivationFunctionType

P = 128
N = 2500
E = 80000
D = 256
DC = D // P
DE1 = 384
KC1 = DE1 // P
DE3 = 64
W = -(-N // P)
TAIL = N - (W - 1) * P
T = E // P
STEPS = T + W - 1
SC = -(-STEPS // P)
SP_ = SC * P
AW = D + 1
LN_EPS = 1e-5
INPUTS = ("x", "src", "dst", "edge_weight", "wl_t", "wr_t", "b_r", "wn_t", "b_node", "we_t", "b_edge", "ea1", "base_t", "scaler_t",
          "spline_t", "w2l_t", "l2_bias", "ea3", "w1", "b1", "w2_in", "b2_in", "wg", "bg", "gamma_in", "beta_in")
NB = 7


def rounds(eng, n):
    yield 0
    with eng.Fori(1, n) as i:
        yield i


def wait(eng, sem, value):
    if not isinstance(value, int) or value > 0:
        eng.wait_ge(sem, value)


class Chain:

    def __init__(self, eng, sem):
        self.eng, self.sem, self.n, self.r = eng, sem, 0, 0

    def __call__(self, ins):
        ins.then_inc(self.sem, 1)
        self.n += 1
        self.eng.wait_ge(self.sem, self.r + self.n)

    def loop(self, count, per):
        base = self.n
        with self.eng.Fori(0, count) as i:
            self.r, self.n = i * per + base, 0
            yield i
            assert self.n == per, self.n
        self.r, self.n = 0, base + count * per


class Parts:

    def __init__(self, args, out):
        (self.x, self.src, self.dst, self.edge_weight, self.wl_t, self.wr_t, self.b_r, self.wn_t, self.b_node, self.we_t,
         self.b_edge, self.ea1, self.base_t, self.scaler_t, self.spline_t, self.w2l_t, self.l2_bias, self.ea3, self.w1, self.b1,
         self.w2_in, self.b2_in, self.wg, self.bg, self.gamma_in, self.beta_in) = (args[name] for name in INPUTS)
        self.out = out


def at(t, i, width=None):
    cols = slice(None) if width is None else slice(0, width)
    if isinstance(i, int):
        return t[:, i, cols]
    return t[:, bass.DynSlice(i, 1), cols].rearrange("p o f -> p (o f)")


def col(t, i):
    return t[:, bass.DynSlice(i, 1)]


def setup(nc, k, sb, ps, sem):
    k.iota = sb("iota", [P, P], FP32)
    k.ident = sb("ident", [P, P], FP32)
    k.ones = sb("ones", [P, P], FP32)
    k.xs = sb("xs", [P, W, AW], FP32)
    k.stats = sb("stats", [P, W, 6], FP32)
    k.agg = sb("agg", [P, W, AW], FP32)
    k.src_t = sb("src_t", [P, SP_], I32)
    k.dst_t = sb("dst_t", [P, SP_], I32)
    k.rel_t = sb("rel_t", [P, SP_], FP32)
    k.ew_t = sb("ew_t", [P, SP_], FP32)
    k.tile_row = sb("tile_row", [1, SP_], I32)
    k.win_row = sb("win_row", [1, SP_], I32)
    k.wl, k.wr, k.wn, k.wbase, k.scaler, k.w2l, k.w2 = (
        sb(n, [P, DC, D], FP32) for n in ("wl", "wr", "wn", "wbase", "scaler", "w2l", "w2"))
    k.we = sb("we", [P, KC1, D], FP32)
    k.wsp = sb("wsp", [P, NB, DC, D], FP32)
    k.w13 = sb("w13", [P, DC, 2 * D], FP32)
    k.we3 = sb("we3", [DE3, 2 * D], FP32)
    k.w1b, k.wgb = k.we3[:, 0:D], k.we3[:, D:2 * D]
    k.br, k.bn, k.be, k.bias2, k.b2, k.gamma, k.beta = (
        sb(n, [P, D], FP32) for n in ("br", "bn", "be", "bias2", "b2b", "gamma", "beta"))
    k.b13 = sb("b13", [P, 2 * D], FP32)
    weights = [(k.wl, k.wl_t), (k.wr, k.wr_t), (k.wn, k.wn_t), (k.we, k.we_t), (k.wbase, k.base_t), (k.scaler, k.scaler_t),
               (k.w2l, k.w2l_t), (k.w2, k.w2_in), (k.w13[:, :, 0:D], k.w1[0:D, :]), (k.w13[:, :, D:2 * D], k.wg[0:D, :])]
    biases = [(k.br[:, :], k.b_r), (k.bn[:, :], k.b_node), (k.be[:, :], k.b_edge), (k.bias2[:, :], k.l2_bias), (k.b2[:, :], k.b2_in),
              (k.gamma[:, :], k.gamma_in), (k.beta[:, :], k.beta_in), (k.b13[:, 0:D], k.b1), (k.b13[:, D:2 * D], k.bg)]

    QT = T // (T // 5)
    TP = T // QT
    ctx = ExitStack()
    def tmp(name, shape, dt):
        return ctx.enter_context(nc.sbuf_tensor(name, shape, dt))
    with ctx:
        dst_tiles = tmp("dst_tiles", [TP, QT, P], I32)
        last_win = tmp("last_win", [TP, QT], I32)
        last_pos = tmp("last_pos", [TP, QT], FP32)
        tile_id = tmp("tile_id", [TP, QT], FP32)
        step_row = tmp("step_row", [P, SP_], FP32)
        step_col = tmp("step_col", [P, SC], FP32)
        part = tmp("part", [P, 1], FP32)
        passed = tmp("passed", [TP, QT, SP_], FP32)
        tile_f = tmp("tile_f", [1, SP_], FP32)
        win_f = tmp("win_f", [1, SP_], FP32)
        tcol_f = tmp("tcol_f", [P, SC], FP32)
        tcol = tmp("tcol", [P, SC], I32)
        wcol = tmp("wcol", [P, SC], FP32)
        dst_s = tmp("dst_s", [P, SC, P], I32)
        src_s = tmp("src_s", [P, SC, P], I32)
        ew_s = tmp("ew_s", [P, SC, P], FP32)
        conv = tmp("conv", [P, 4, SC, P], FP32)
        pcount = ctx.enter_context(nc.psum_tensor("pcount", [P, 2, 512], FP32))
        ptile = ctx.enter_context(nc.psum_tensor("ptile", [P, SC], FP32))
        ptr = ctx.enter_context(nc.psum_tensor("ptr", [P, 4, P], FP32))
        loaded = sem("setup_loaded")
        xs_zero = sem("xs_zero")
        dst_loaded = sem("dst_loaded")
        iotas = sem("iotas")
        passed_ready = sem("passed_ready")
        counted = sem("counted")
        tcol_ready = sem("tcol_ready")
        rows_in = sem("rows_in")
        conv_ready = sem("conv_ready")
        turned = sem("turned")
        taken = sem("taken")
        ch = sem("setup_chain")
        with nc.Block() as block:
            @block.sync
            def _(sp):
                sp.dma_start(dst_tiles[:, :, :], k.dst.rearrange("(p q e) -> p q e", q=QT, e=P)).then_inc(dst_loaded, 16)
                sp.dma_start(k.xs[:, 0:W - 1, 0:D], k.x[0:(W - 1) * P, :].rearrange("(w p) f -> p w f", p=P)).then_inc(loaded, 16)
                sp.wait_ge(xs_zero, 1)
                sp.dma_start(k.xs[0:TAIL, W - 1, 0:D], k.x[(W - 1) * P:N, :]).then_inc(loaded, 16)
                n = 2
                for dst, src in weights:
                    sp.dma_start(dst[:, :, :], src.rearrange("(c p) o -> p c o", p=P)).then_inc(loaded, 16)
                    n += 1
                for kk in range(NB):
                    sp.dma_start(k.wsp[:, kk, :, :], k.spline_t[kk].rearrange("(c p) o -> p c o", p=P)).then_inc(loaded, 16)
                    n += 1
                for dst, src in ((k.w1b, k.w1[D:D + DE3, :]), (k.wgb, k.wg[D:D + DE3, :])):
                    sp.dma_start(dst, src).then_inc(loaded, 16)
                    n += 1
                for dst, src in biases:
                    sp.dma_start(dst, src[None, :].broadcast_to([P, D])).then_inc(loaded, 16)
                    n += 1
                sp.wait_ge(loaded, 16 * n)

            @block.gpsimd
            def _(pool):
                nc.gpsimd.iota(k.iota[:, :], [[1, P]], base=0, channel_multiplier=0, allow_small_or_imprecise_dtypes=True).then_inc(iotas, 1)
                nc.gpsimd.iota(part[:, :], [[1, 1]], base=0, channel_multiplier=1, allow_small_or_imprecise_dtypes=True).then_inc(iotas, 1)
                nc.gpsimd.iota(tile_id[:, :], [[1, QT]], base=0, channel_multiplier=QT, allow_small_or_imprecise_dtypes=True).then_inc(iotas, 1)
                nc.gpsimd.iota(step_row[:, :], [[1, SP_]], base=0, channel_multiplier=0, allow_small_or_imprecise_dtypes=True).then_inc(iotas, 1)
                nc.gpsimd.iota(step_col[:, :], [[P, SC]], base=0, channel_multiplier=1, allow_small_or_imprecise_dtypes=True).then_inc(iotas, 1)
                pool.wait_ge(tcol_ready, 1)
                n = 0
                for c in range(SC):
                    for rows, table in ((dst_s, k.dst), (src_s, k.src), (ew_s, k.edge_weight)):
                        nc.gpsimd.indirect_dma_start(rows[:, c, :], None, table.rearrange("(t e) -> t e", e=P),
                                                     bass.IndirectOffsetOnAxis(tcol[:, c:c + 1], 0)).then_inc(rows_in, 16)
                        n += 1
                pool.wait_ge(rows_in, 16 * n)

            @block.vector
            def _(dve):
                link = Chain(dve, ch)
                nc.vector.memset(k.xs[:, W - 1, :], 0.0).then_inc(xs_zero, 1)
                nc.vector.memset(k.ones[:, :], 1.0)
                link(nc.vector.memset(k.agg[:, :, :], 0.0))
                dve.wait_ge(iotas, 5)
                nc.vector.tensor_scalar(k.ident[:, :], k.iota[:, :], part[:, 0:1], None, ALU.is_equal)
                dve.wait_ge(dst_loaded, 16)
                link(nc.vector.tensor_scalar(last_win[:, :], dst_tiles[:, :, P - 1], 7, None, ALU.logical_shift_right))
                link(nc.vector.tensor_copy(last_pos[:, :], last_win[:, :]))
                link(nc.vector.tensor_tensor(last_pos[:, :], last_pos[:, :], tile_id[:, :], ALU.add))
                for q in range(QT):
                    last = nc.vector.tensor_scalar(passed[:, q, :], step_row[0:TP, :], last_pos[:, q:q + 1], None, ALU.is_gt)
                last.then_inc(passed_ready, 1)
                dve.wait_ge(counted, 1)
                last_tile = float(T - 1)
                link(nc.vector.tensor_scalar(tcol_f[:, :], ptile[:, :], last_tile, None, ALU.min))
                nc.vector.tensor_copy(tcol[:, :], tcol_f[:, :]).then_inc(tcol_ready, 1)
                link(nc.vector.tensor_tensor(wcol[:, :], step_col[:, :], tcol_f[:, :], ALU.subtract))
                link(nc.vector.tensor_scalar(wcol[:, :], wcol[:, :], float(P), None, ALU.mult))
                half = SP_ // 2
                nc.vector.tensor_scalar(tile_f[:, 0:half], pcount[0:1, 0, 0:half], last_tile, None, ALU.min)
                link(nc.vector.tensor_scalar(tile_f[:, half:], pcount[0:1, 1, 0:half], last_tile, None, ALU.min))
                nc.vector.tensor_copy(k.tile_row[:, :], tile_f[:, :])
                link(nc.vector.tensor_tensor(win_f[:, :], step_row[0:1, :], tile_f[:, :], ALU.subtract))
                link(nc.vector.tensor_scalar(win_f[:, :], win_f[:, :], float(W - 1), None, ALU.min))
                link(nc.vector.tensor_copy(k.win_row[:, :], win_f[:, :]))
                dve.wait_ge(rows_in, 16 * 3 * SC)
                for c in range(SC):
                    nc.vector.tensor_copy(conv[:, 0, c, :], src_s[:, c, :])
                    nc.vector.tensor_copy(conv[:, 1, c, :], dst_s[:, c, :])
                    nc.vector.tensor_scalar(conv[:, 2, c, :], dst_s[:, c, :], wcol[:, c:c + 1], None, ALU.subtract)
                    nc.vector.tensor_copy(conv[:, 3, c, :], ew_s[:, c, :]).then_inc(conv_ready, 1)
                for c in range(SC):
                    cols = slice(c * P, (c + 1) * P)
                    dve.wait_ge(turned, c + 1)
                    nc.vector.tensor_copy(k.src_t[:, cols], ptr[:, 0, :])
                    nc.vector.tensor_copy(k.dst_t[:, cols], ptr[:, 1, :])
                    nc.vector.tensor_copy(k.rel_t[:, cols], ptr[:, 2, :])
                    nc.vector.tensor_copy(k.ew_t[:, cols], ptr[:, 3, :]).then_inc(taken, 1)

            @block.tensor
            def _(pe):
                pe.wait_ge(passed_ready, 1)
                for h in range(2):
                    for q in range(QT):
                        nc.tensor.matmul(pcount[:, h, 0:SP_ // 2], k.ones[0:TP, :], passed[:, q, h * SP_ // 2:(h + 1) * SP_ // 2],
                                         start=(q == 0), stop=(q == QT - 1))
                for c in range(SC):
                    for q in range(QT):
                        last = nc.tensor.matmul(ptile[:, c:c + 1], passed[:, q, c * P:(c + 1) * P], k.ones[0:TP, 0:1],
                                                start=(q == 0), stop=(q == QT - 1))
                last.then_inc(counted, 1)
                for c in range(SC):
                    pe.wait_ge(conv_ready, c + 1)
                    if c:
                        pe.wait_ge(taken, c)
                    for t in range(4):
                        last = nc.tensor.transpose(ptr[:, t, :], conv[:, t, c, :], k.ident[:, :])
                    last.then_inc(turned, 1)


def set_indices(nc, act, n_rounds, slots, idx, table, idx_set, used):
    for i in rounds(act, n_rounds):
        for j in range(slots):
            wait(act, used, i * slots + j + 1 - slots)
            nc.scalar.activation(idx[:, j:j + 1], col(table, i * slots + j), ACT.Copy).then_inc(idx_set, 1)


def gather(nc, pool, n_rounds, slots, idx, idx_set, issued, rows, table, gathered):
    for i in rounds(pool, n_rounds):
        for j in range(slots):
            pool.wait_ge(idx_set, i * slots + j + 1)
            pool.sem_inc(issued, 1)
            nc.gpsimd.indirect_dma_start(rows[:, j, :], None, table, bass.IndirectOffsetOnAxis(idx[:, j:j + 1], 0)
                                         ).then_inc(gathered[j], 16)


def edges_mean(nc, k, sb, ps, sem):
    R = 7
    LAG = 3
    ROUNDS = STEPS // R
    ctx = ExitStack()
    with ctx:
        rows = ctx.enter_context(nc.sbuf_tensor("l0_rows", [P, R, AW], FP32))
        hot = ctx.enter_context(nc.sbuf_tensor("l0_hot", [P, R, P], FP32))
        idx = ctx.enter_context(nc.sbuf_tensor("l0_idx", [P, R], I32))
        seg = [ctx.enter_context(nc.psum_tensor(f"l0_seg{j}", [P, 512], FP32)) for j in range(R)]
        ones_set = sem("l0_ones_set")
        idx_set = sem("l0_idx_set")
        issued = sem("l0_issued")
        gathered = [sem(f"l0_gathered{j}") for j in range(R)]
        hot_ready = sem("l0_hot_ready")
        summed = sem("l0_summed")
        added = sem("l0_added")
        with nc.Block() as block:
            @block.gpsimd
            def _(pool):
                pool.wait_ge(ones_set, 1)
                gather(nc, pool, ROUNDS, R, idx, idx_set, issued, rows[:, :, 0:D], k.x, gathered)

            @block.scalar
            def _(act):
                set_indices(nc, act, ROUNDS, R, idx, k.src_t, idx_set, summed)

            @block.vector
            def _(dve):
                nc.vector.memset(rows[:, :, D:AW], 1.0).then_inc(ones_set, 1)

                def add(s, j):
                    dve.wait_ge(summed, s + 1)
                    wait(dve, added, s)
                    w = dve.value_load(k.win_row[0:1, bass.DynSlice(s, 1)], min_val=0, max_val=W - 1)
                    nc.vector.tensor_tensor(at(k.agg, w), at(k.agg, w), seg[j][:, 0:AW], ALU.add).then_inc(added, 1)

                for i in rounds(dve, ROUNDS):
                    for j in range(R):
                        s = i * R + j
                        wait(dve, summed, s + 1 - R)
                        nc.vector.tensor_scalar(hot[:, j, :], k.iota[:, :], col(k.rel_t, s), None, ALU.is_equal).then_inc(hot_ready, 1)
                        if not isinstance(i, int) or s >= LAG:
                            add(s - LAG, (j - LAG) % R)
                for s in range(STEPS - LAG, STEPS):
                    add(s, s % R)

            @block.tensor
            def _(pe):
                for i in rounds(pe, ROUNDS):
                    for j in range(R):
                        s = i * R + j
                        wait(pe, added, s + 1 - R)
                        pe.wait_ge(hot_ready, s + 1)
                        pe.wait_ge(gathered[j], 16 * i + 16)
                        nc.tensor.matmul(seg[j][:, 0:AW], hot[:, j, :], rows[:, j, :], start=True, stop=True).then_inc(summed, 1)


def nodes_mean(nc, k, sb, ps, sem):
    ctx = ExitStack()
    with ctx:
        def tmp(name, shape, dt=FP32):
            return ctx.enter_context(nc.sbuf_tensor(name, shape, dt))
        rc = tmp("n0_rc", [P, W])
        mean = tmp("n0_mean", [P, D])
        opT = tmp("n0_opT", [P, 4, P])
        turn = ctx.enter_context(nc.psum_tensor("n0_turn", [P, 4, P], FP32))
        prod = ctx.enter_context(nc.psum_tensor("n0_prod", [P, 512], FP32))
        row = tmp("n0_row", [P, D])
        mean_ready, brought, turned, copied, multiplied, ch = (
            sem("n0_" + n) for n in ("mean_ready", "brought", "turned", "copied", "multiplied", "ch"))
        with nc.Block() as block:
            @block.vector
            def _(dve):
                link = Chain(dve, ch)
                link(nc.vector.tensor_scalar(rc[:, :], k.agg[:, :, D], 1.0, None, ALU.max))
                link(nc.vector.reciprocal(rc[:, :], rc[:, :]))
                for w in link.loop(W, 3):
                    nc.vector.tensor_scalar(mean[:, :], at(k.agg, w, D), col(rc, w), None, ALU.mult).then_inc(mean_ready, 1)
                    dve.wait_ge(multiplied, w + 1)
                    link(nc.vector.tensor_tensor(at(k.xs, w, D), at(k.xs, w, D), prod[:, 0:D], ALU.add))
                    link(nc.vector.tensor_tensor(at(k.xs, w, D), at(k.xs, w, D), k.br[:, :], ALU.add))
                    link(nc.vector.bn_stats(at(k.stats, w), at(k.xs, w, D)))
                link(nc.vector.memset(k.agg[:, :, :], 0.0))

            @block.tensor
            def _(pe):
                for w in rounds(pe, W):
                    pe.wait_ge(mean_ready, w + 1)
                    pe.wait_ge(brought, w + 1)
                    for c in range(DC):
                        nc.tensor.transpose(turn[:, c, :], mean[:, c * P:(c + 1) * P], k.ident[:, :])
                    for c in range(DC):
                        last = nc.tensor.transpose(turn[:, DC + c, :], row[:, c * P:(c + 1) * P], k.ident[:, :])
                    last.then_inc(turned, 1)
                    pe.wait_ge(copied, w + 1)
                    for c in range(2 * DC):
                        last = nc.tensor.matmul(prod[:, 0:D], opT[:, c, :], (k.wl if c < DC else k.wr)[:, c % DC, :],
                                                start=(c == 0), stop=(c == 2 * DC - 1))
                    last.then_inc(multiplied, 1)

            @block.gpsimd
            def _(pool):
                for w in rounds(pool, W):
                    wait(pool, turned, w)
                    nc.gpsimd.tensor_copy(row[:, :], at(k.xs, w, D)).then_inc(brought, 1)

            @block.scalar
            def _(act):
                with act.Fori(0, W) as w:
                    act.wait_ge(turned, w + 1)
                    nc.scalar.activation(opT[:, :, :], turn[:, :, :], ACT.Copy).then_inc(copied, 1)
        layernorm(nc, k, sem, "n0", k.wn, k.bn, D, k.h)


def layernorm(nc, k, sem, tag, weight, bias, width, table):
    ctx = ExitStack()
    with ctx:
        def tmp(name, shape, dt=FP32):
            return ctx.enter_context(nc.sbuf_tensor(tag + name, shape, dt))
        rstd = tmp("_rstd", [P, W])
        mv = tmp("_mv", [P, W, 2])
        ch, rooted, normed = (sem(f"{tag}_{n}") for n in ("lch", "rooted", "normed"))
        with nc.Block() as block:
            @block.scalar
            def _(act):
                act.wait_ge(ch, 2)
                nc.scalar.activation(rstd[:, :], rstd[:, :], ACT.Sqrt).then_inc(rooted, 1)

            @block.vector
            def _(dve):
                link = Chain(dve, ch)
                for w in range(W):
                    last = nc.vector.bn_aggr(mv[:, w, :], k.stats[:, w, :])
                link(last)
                link(nc.vector.tensor_scalar(rstd[:, :], mv[:, :, 1], LN_EPS, None, ALU.add))
                dve.wait_ge(rooted, 1)
                link(nc.vector.reciprocal(rstd[:, :], rstd[:, :]))
                with dve.Fori(0, W) as w:
                    nc.vector.tensor_scalar(at(k.xs, w, D), at(k.xs, w, D), mv[:, bass.DynSlice(w, 1), 0], col(rstd, w),
                                            ALU.subtract, ALU.mult).then_inc(normed, 1)
    if weight is not None:
        project(nc, k, sem, tag, weight, bias, width, table)


def project(nc, k, sem, tag, weight, bias, width, table):
    ctx = ExitStack()
    with ctx:
        def tmp(name, shape, dt=FP32):
            return ctx.enter_context(nc.sbuf_tensor(tag + name, shape, dt))
        opT = tmp("_lnT", [P, 2, DC, P])
        row = tmp("_lrow", [P, 2, D])
        made = tmp("_made", [P, W, width])
        turn = [ctx.enter_context(nc.psum_tensor(f"{tag}_lturn{b}", [P, DC, P], FP32)) for b in range(2)]
        prod = [ctx.enter_context(nc.psum_tensor(f"{tag}_lprod{b}", [P, 512], FP32)) for b in range(2)]
        brought, turned, copied, multiplied, added, stored = (
            sem(f"{tag}_{n}") for n in ("lbrought", "lturned", "lcopied", "lmult", "ladded", "stored"))
        with nc.Block() as block:
            @block.scalar
            def _(act):
                with act.Fori(0, W // 2) as i:
                    for b in range(2):
                        act.wait_ge(turned, i * 2 + b + 1)
                        nc.scalar.activation(opT[:, b, :, :], turn[b][:, :, :], ACT.Copy).then_inc(copied, 1)

            @block.vector
            def _(dve):
                with dve.Fori(0, W // 2) as i:
                    for b in range(2):
                        w = i * 2 + b
                        dve.wait_ge(multiplied, w + 1)
                        nc.vector.tensor_tensor(at(made, w), prod[b][:, 0:width], bias[:, 0:width], ALU.add).then_inc(added, 1)

            @block.gpsimd
            def _(pool):
                for i in rounds(pool, W // 2):
                    for b in range(2):
                        w = i * 2 + b
                        wait(pool, turned, w - 1)
                        nc.gpsimd.tensor_copy(row[:, b, :], at(k.xs, w, D)).then_inc(brought, 1)

            @block.tensor
            def _(pe):
                for i in rounds(pe, W // 2):
                    for b in range(2):
                        w = i * 2 + b
                        wait(pe, copied, w - 1)
                        pe.wait_ge(brought, w + 1)
                        for c in range(DC):
                            last = nc.tensor.transpose(turn[b][:, c, :], row[:, b, c * P:(c + 1) * P], k.ident[:, :])
                        last.then_inc(turned, 1)
                        pe.wait_ge(copied, w + 1)
                        wait(pe, added, w - 1)
                        for c in range(DC):
                            last = nc.tensor.matmul(prod[b][:, 0:width], opT[:, b, c, :], weight[:, c, :], start=(c == 0), stop=(c == DC - 1))
                        last.then_inc(multiplied, 1)

            @block.sync
            def _(sp):
                sp.wait_ge(added, W)
                sp.dma_start(table.rearrange("(w p) f -> p w f", p=P), made[:, :, :]).then_inc(stored, 16)
                sp.wait_ge(stored, 16)


def accumulate(nc, k, dve, s, seg, width, summed, added):
    dve.wait_ge(summed, s + 1)
    wait(dve, added, s)
    w = dve.value_load(k.win_row[0:1, bass.DynSlice(s, 1)], min_val=0, max_val=W - 1)
    nc.vector.tensor_tensor(at(k.agg, w, width), at(k.agg, w, width), seg[:, 0:width], ALU.add).then_inc(added, 1)


def edges_spline(nc, k, sb, ps, sem):
    R = 4
    LAG = 3
    ROUNDS = STEPS // R
    ctx = ExitStack()
    with ctx:
        def tmp(name, shape, dt=FP32):
            return ctx.enter_context(nc.sbuf_tensor(name, shape, dt))
        rows = tmp("l1_rows", [P, R, D])
        attr = tmp("l1_attr", [P, R, KC1, P])
        hot = tmp("l1_hot", [P, R, P])
        edge = tmp("l1_edge", [P, R, D])
        msg = tmp("l1_msg", [P, R, D])
        idx = tmp("l1_idx", [P, R], I32)
        prod = [ctx.enter_context(nc.psum_tensor(f"l1_prod{j}", [P, 512], FP32)) for j in range(R)]
        seg = [ctx.enter_context(nc.psum_tensor(f"l1_seg{j}", [P, 512], FP32)) for j in range(R)]
        gathered = [sem(f"l1_gathered{j}") for j in range(R)]
        attr_in = [sem(f"l1_attr_in{j}") for j in range(R)]
        idx_set, issued, hot_ready, multiplied, biased, msg_ready, summed, added = (
            sem("l1_" + n) for n in ("idx_set", "issued", "hot_ready", "multiplied", "biased", "msg_ready", "summed", "added"))
        with nc.Block() as block:
            @block.sync
            def _(sp):
                for i in rounds(sp, ROUNDS):
                    for j in range(R):
                        s = i * R + j
                        wait(sp, multiplied, s + 1 - R)
                        t = sp.value_load(k.tile_row[0:1, bass.DynSlice(s, 1)], min_val=0, max_val=T - 1)
                        sp.dma_start(attr[:, j, :, :], k.ea1[bass.DynSlice(t, 1), :, :, :].rearrange("o p c e -> (o p) c e")
                                     ).then_inc(attr_in[j], 16)

            @block.gpsimd
            def _(pool):
                gather(nc, pool, ROUNDS, R, idx, idx_set, issued, rows, k.h, gathered)

            @block.scalar
            def _(act):
                set_indices(nc, act, ROUNDS, R, idx, k.src_t, idx_set, msg_ready)

            @block.vector
            def _(dve):
                def message(s, j):
                    dve.wait_ge(multiplied, s + 1)
                    nc.vector.tensor_tensor(edge[:, j, :], prod[j][:, 0:D], k.be[:, :], ALU.add).then_inc(biased, 1)
                    dve.wait_ge(gathered[j], (s - j) // R * 16 + 16 if isinstance(s, int) else (s - j) * (16 // R) + 16)
                    dve.wait_ge(biased, s + 1)
                    nc.vector.tensor_tensor(msg[:, j, :], edge[:, j, :], rows[:, j, :], ALU.mult).then_inc(msg_ready, 1)

                for i in rounds(dve, ROUNDS):
                    for j in range(R):
                        s = i * R + j
                        wait(dve, summed, s + 1 - R)
                        nc.vector.tensor_scalar(hot[:, j, :], k.iota[:, :], col(k.rel_t, s), None, ALU.is_equal).then_inc(hot_ready, 1)
                        message(s, j)
                        if not isinstance(i, int) or s >= LAG:
                            accumulate(nc, k, dve, s - LAG, seg[(j - LAG) % R], D, summed, added)
                for s in range(STEPS - LAG, STEPS):
                    accumulate(nc, k, dve, s, seg[s % R], D, summed, added)

            @block.tensor
            def _(pe):
                def segment(s, j):
                    pe.wait_ge(msg_ready, s + 1)
                    pe.wait_ge(hot_ready, s + 1)
                    nc.tensor.matmul(seg[j][:, 0:D], hot[:, j, :], msg[:, j, :], start=True, stop=True).then_inc(summed, 1)

                for i in rounds(pe, ROUNDS):
                    for j in range(R):
                        s = i * R + j
                        pe.wait_ge(attr_in[j], i * 16 + 16)
                        wait(pe, msg_ready, s + 1 - R)
                        for c in range(KC1):
                            last = nc.tensor.matmul(prod[j][:, 0:D], attr[:, j, c, :], k.we[:, c, :], start=(c == 0), stop=(c == KC1 - 1))
                        last.then_inc(multiplied, 1)
                        if not isinstance(i, int) or s >= 1:
                            wait(pe, added, s + 1 - R)
                            segment(s - 1, (j - 1) % R)
                pe.wait_ge(added, STEPS - R)
                segment(STEPS - 1, R - 1)


def nodes_spline(nc, k, sb, ps, sem):
    ctx = ExitStack()
    with ctx:
        def tmp(name, shape, dt=FP32):
            return ctx.enter_context(nc.sbuf_tensor(name, shape, dt))
        centre = tmp("n1_centre", [P, NB])
        row = tmp("n1_row", [P, 2, D])
        aggT = tmp("n1_aggT", [P, 2, D])
        siluT = tmp("n1_siluT", [P, 2, D])
        near = tmp("n1_near", [P, 2, NB, D])
        far = tmp("n1_far", [P, 2, NB, D])
        sq = tmp("n1_sq", [P, 2, NB, D])
        sqn = tmp("n1_sqn", [P, 2, NB, D])
        basis = tmp("n1_basis", [P, 2, NB, D])
        turn = [ctx.enter_context(nc.psum_tensor(f"n1_turn{b}", [P, D], FP32)) for b in range(2)]
        prod = [ctx.enter_context(nc.psum_tensor(f"n1_prod{b}", [P, 512], FP32)) for b in range(2)]
        (brought, turned, aggT_in, silu_in, dist_in, near_in, far_in, sq_in, cube_in, basis_in, multiplied, xs_in, centred, ch,
         scaled) = (sem("n1_" + n) for n in (
             "brought", "turned", "aggT_in", "silu_in", "dist_in", "near_in", "far_in", "sq_in", "cube_in", "basis_in",
             "multiplied", "xs_in", "centred", "ch", "scaled"))
        with nc.Block() as block:
            @block.gpsimd
            def _(pool):
                for i in rounds(pool, W // 2):
                    for b in range(2):
                        w = i * 2 + b
                        wait(pool, turned, w - 1)
                        nc.gpsimd.tensor_copy(row[:, b, :], at(k.agg, w, D)).then_inc(brought, 1)

            @block.scalar
            def _(act):
                act.wait_ge(centred, 1)
                for i in rounds(act, W // 2):
                    for b in range(2):
                        w = i * 2 + b
                        act.wait_ge(turned, w + 1)
                        wait(act, multiplied, w - 1)
                        nc.scalar.activation(siluT[:, b, :], turn[b][:, :], ACT.Silu).then_inc(silu_in, 1)
                        wait(act, basis_in, w - 1)
                        for n in range(NB):
                            last = nc.scalar.activation(near[:, b, n, :], turn[b][:, :], ACT.Abs, bias=centre[:, n:n + 1], scale=2.0)
                        last.then_inc(dist_in, 1)
                        act.wait_ge(near_in, w + 1)
                        nc.scalar.activation(sq[:, b, :, :], far[:, b, :, :], ACT.Square)
                        nc.scalar.activation(sqn[:, b, :, :], near[:, b, :, :], ACT.Square).then_inc(sq_in, 1)

            @block.vector
            def _(dve):
                link = Chain(dve, ch)
                link(nc.vector.tensor_scalar(centre[:, :], k.iota[:, 0:NB], -1.0, 3.0, ALU.mult, ALU.add))
                nc.vector.tensor_copy(centre[:, :], centre[:, :]).then_inc(centred, 1)
                for n in range(NB):
                    last = nc.vector.scalar_tensor_tensor(k.wsp[:, n, :, :], k.wsp[:, n, :, :], 1.0 / 6.0, k.scaler[:, :, :], ALU.mult, ALU.mult)
                last.then_inc(scaled, 1)

                def take(w, b):
                    dve.wait_ge(multiplied, w + 1)
                    nc.vector.tensor_tensor(at(k.xs, w, D), at(k.xs, w, D), prod[b][:, 0:D], ALU.add).then_inc(xs_in, 1)
                    dve.wait_ge(xs_in, w + 1)
                    nc.vector.bn_stats(at(k.stats, w), at(k.xs, w, D))

                for i in rounds(dve, W // 2):
                    for b in range(2):
                        w = i * 2 + b
                        dve.wait_ge(dist_in, w + 1)
                        wait(dve, multiplied, w - 1)
                        nc.vector.tensor_scalar(far[:, b, :, :], near[:, b, :, :], 2.0, 2.0, ALU.min, ALU.subtract).then_inc(far_in, 1)
                        dve.wait_ge(far_in, w + 1)
                        nc.vector.tensor_scalar(near[:, b, :, :], near[:, b, :, :], 1.0, 1.0, ALU.min, ALU.subtract).then_inc(near_in, 1)
                        dve.wait_ge(sq_in, w + 1)
                        nc.vector.tensor_tensor(sq[:, b, :, :], sq[:, b, :, :], far[:, b, :, :], ALU.mult)
                        nc.vector.scalar_tensor_tensor(sqn[:, b, :, :], sqn[:, b, :, :], 4.0, near[:, b, :, :], ALU.mult, ALU.mult).then_inc(cube_in, 1)
                        dve.wait_ge(cube_in, w + 1)
                        nc.vector.tensor_tensor(basis[:, b, :, :], sqn[:, b, :, :], sq[:, b, :, :], ALU.subtract).then_inc(basis_in, 1)
                        if not isinstance(i, int) or w >= 1:
                            take(w - 1, 1 - b)
                take(W - 1, 1)
                link(nc.vector.memset(k.agg[:, :, :], 0.0))

            @block.tensor
            def _(pe):
                pe.wait_ge(scaled, 1)

                def turn_rows(w, b):
                    pe.wait_ge(brought, w + 1)
                    wait(pe, silu_in, w - 1)
                    wait(pe, dist_in, w - 1)
                    for c in range(DC):
                        last = nc.tensor.transpose(turn[b][:, c * P:(c + 1) * P], row[:, b, c * P:(c + 1) * P], k.ident[:, :])
                    last.then_inc(turned, 1)

                def multiply(w, b):
                    pe.wait_ge(silu_in, w + 1)
                    wait(pe, xs_in, w - 1)
                    for c in range(DC):
                        nc.tensor.matmul(prod[b][:, 0:D], siluT[:, b, c * P:(c + 1) * P], k.wbase[:, c, :], start=(c == 0), stop=False)
                    pe.wait_ge(basis_in, w + 1)
                    for n in range(NB):
                        for c in range(DC):
                            last = nc.tensor.matmul(prod[b][:, 0:D], basis[:, b, n, c * P:(c + 1) * P], k.wsp[:, n, c, :],
                                                    start=False, stop=(n == NB - 1 and c == DC - 1))
                    last.then_inc(multiplied, 1)

                turn_rows(0, 0)
                for i in rounds(pe, W // 2 - 1):
                    for b in range(2):
                        w = i * 2 + b
                        turn_rows(w + 1, 1 - b)
                        multiply(w, b)
                turn_rows(W - 1, 1)
                multiply(W - 2, 0)
                multiply(W - 1, 1)
    layernorm(nc, k, sem, "n1", None, None, 0, None)


MIN_NORM = 1e-15
BALL_EPS = 1e-5
Z_MAX = 1.0 - 1e-7
ROOT_MIN = 2.0 ** -60


class Linked:

    def __init__(self, eng, sem, per):
        self.eng, self.sem, self.per = eng, sem, per

    def start(self, h):
        self.base, self.n = h * self.per, 0

    def __call__(self, ins):
        ins.then_inc(self.sem, 1)
        self.n += 1
        assert self.n <= self.per
        self.eng.wait_ge(self.sem, self.base + self.n)


def norms(nc, k, sem):
    normed, stored = sem("x2_normed"), sem("x2_stored")
    with nc.sbuf_tensor("x2_junk", [P, 2, D], FP32) as junk, nc.Block() as block:
        @block.scalar
        def _(act):
            for w in range(W):
                wait(act, normed, w - 1)
                nc.scalar.activation(junk[:, w % 2, :], k.xs[:, w, 0:D], ACT.Square, accum_out=k.xs[:, w, D:AW]).then_inc(normed, 1)

        @block.sync
        def _(sp):
            sp.wait_ge(normed, W)
            sp.dma_start(k.x2_table.rearrange("(w p) f -> p w f", p=P), k.xs[:, :, :]).then_inc(stored, 16)
            sp.wait_ge(stored, 16)


def edges_ball(nc, k, sb, ps, sem):
    H = 7
    R = 2 * H
    ROUNDS = STEPS // R
    LAG = H + 2
    ctx = ExitStack()
    with ctx:
        def tmp(name, shape, dt=FP32):
            return ctx.enter_context(nc.sbuf_tensor(name, shape, dt))
        rows = tmp("l2_rows", [P, R, AW])
        hot = tmp("l2_hot", [P, R, P])
        hotT = tmp("l2_hotT", [P, 2, P])
        scaled = tmp("l2_scaled", [P, 2, D])
        junk = tmp("l2_junk", [P, 2, D])
        idx = tmp("l2_idx", [P, R], I32)
        dot, dst2, gap, q, den, rden, prod2, root, rroot, sn, z, la, lb, g, kb, fsrc, fdst = (
            tmp("l2_" + n, [P, 2, H]) for n in ("dot", "dst2", "gap", "q", "den", "rden", "prod2", "root", "rroot", "sn", "z",
                                                "la", "lb", "g", "kb", "fsrc", "fdst"))
        turn = [ctx.enter_context(nc.psum_tensor(f"l2_turn{j}", [P, 512], FP32)) for j in range(2)]
        base = [ctx.enter_context(nc.psum_tensor(f"l2_base{j}", [P, 512], FP32)) for j in range(2)]
        seg = [ctx.enter_context(nc.psum_tensor(f"l2_seg{j}", [P, 512], FP32)) for j in range(2)]
        gathered = [sem(f"l2_gathered{j}") for j in range(R)]
        (idx_set, issued, hot_ready, turned, hotT_in, expanded, dotted, scaled_in, summed, added, squared, logq_in, root_in,
         z_in, logs_in, factors_in, cha, chb, chc) = (sem("l2_" + n) for n in (
             "idx_set", "issued", "hot_ready", "turned", "hotT_in", "expanded", "dotted", "scaled_in", "summed", "added",
             "squared", "logq_in", "root_in", "z_in", "logs_in", "factors_in", "cha", "chb", "chc"))

        def ticks(eng):
            for i in rounds(eng, ROUNDS):
                for b in range(2):
                    for j in range(H):
                        yield i * R + b * H + j, i, b, j

        with nc.Block() as block:
            @block.gpsimd
            def _(pool):
                for s, i, b, j in ticks(pool):
                    slot = b * H + j
                    wait(pool, scaled_in, s + 1 - R)
                    nc.gpsimd.tensor_copy(idx[:, slot:slot + 1], col(k.src_t, s)).then_inc(idx_set, 1)
                    pool.wait_ge(idx_set, s + 1)
                    pool.sem_inc(issued, 1)
                    nc.gpsimd.indirect_dma_start(rows[:, slot, :], None, k.x2_table, bass.IndirectOffsetOnAxis(idx[:, slot:slot + 1], 0)
                                                 ).then_inc(gathered[slot], 16)

            @block.scalar
            def _(act):
                def copy_hot(s, slot):
                    act.wait_ge(turned, s + 1)
                    wait(act, expanded, s - 1)
                    nc.scalar.activation(hotT[:, slot % 2, :], turn[slot % 2][:, 0:P], ACT.Copy).then_inc(hotT_in, 1)

                def scale_rows(s, h, slot):
                    b, j = slot // H, slot % H
                    act.wait_ge(factors_in, h + 1)
                    wait(act, summed, s - 1)
                    nc.scalar.activation(scaled[:, slot % 2, :], rows[:, slot, 0:D], ACT.Copy, scale=fsrc[:, b, j:j + 1]).then_inc(scaled_in, 1)

                def roots(h, b):
                    act.wait_ge(squared, h + 1)
                    nc.scalar.activation(root[:, b, :], q[:, b, :], ACT.Ln).then_inc(logq_in, 1)
                    act.wait_ge(logq_in, h + 1)
                    nc.scalar.activation(root[:, b, :], root[:, b, :], ACT.Exp, scale=0.5).then_inc(root_in, 1)

                def logs(h, b):
                    act.wait_ge(z_in, h + 1)
                    nc.scalar.activation(la[:, b, :], z[:, b, :], ACT.Ln, bias=1.0, scale=1.0)
                    nc.scalar.activation(lb[:, b, :], z[:, b, :], ACT.Ln, bias=1.0, scale=-1.0).then_inc(logs_in, 1)

                copy_hot(0, 0)
                copy_hot(1, 1)
                for s, i, b, j in ticks(act):
                    h = i * 2 + b
                    slot = b * H + j
                    copy_hot(s + 2, (slot + 2) % R)
                    if not isinstance(i, int) or s >= LAG:
                        scale_rows(s - LAG, h - 1 if j >= 2 else h - 2, (slot - LAG) % R)
                    if j == H - 1:
                        roots(h, b)
                    if j == 0 and (not isinstance(i, int) or h >= 1):
                        logs(h - 1, 1 - b)
                logs(STEPS // H - 1, 1)
                for s in range(STEPS - LAG, STEPS):
                    scale_rows(s, s // H, s % R)

            @block.vector
            def _(dve):
                A, B, C = Linked(dve, cha, 9), Linked(dve, chb, 5), Linked(dve, chc, 7)
                V = nc.vector

                def one_hot(s, slot):
                    wait(dve, summed, s + 1 - R)
                    V.tensor_scalar(hot[:, slot, :], k.iota[:, :], col(k.rel_t, s), None, ALU.is_equal).then_inc(hot_ready, 1)

                def inner(s, i, slot):
                    b, j = slot // H, slot % H
                    dve.wait_ge(gathered[slot], i * 16 + 16)
                    dve.wait_ge(expanded, s + 1)
                    wait(dve, dotted, s - 1)
                    V.tensor_tensor_reduce(out=junk[:, slot % 2, :], in0=rows[:, slot, 0:D], in1=base[slot % 2][:, 0:D], scale=1.0, scalar=0.0,
                                           op0=ALU.mult, op1=ALU.add, accum_out=dot[:, b, j:j + 1])
                    V.tensor_copy(dst2[:, b, j:j + 1], base[slot % 2][:, D:AW]).then_inc(dotted, 1)

                def before_root(h, b):
                    A.start(h)
                    src2 = rows[:, b * H:(b + 1) * H, D]
                    dve.wait_ge(dotted, h * H + H)
                    A(V.scalar_tensor_tensor(gap[:, b, :], dot[:, b, :], -2.0, src2, ALU.mult, ALU.add))
                    A(V.tensor_tensor(prod2[:, b, :], dst2[:, b, :], src2, ALU.mult))
                    A(V.tensor_tensor(q[:, b, :], gap[:, b, :], dst2[:, b, :], ALU.add))
                    A(V.scalar_tensor_tensor(den[:, b, :], dot[:, b, :], -2.0, prod2[:, b, :], ALU.mult, ALU.add))
                    A(V.tensor_scalar(q[:, b, :], q[:, b, :], 0.0, None, ALU.max))
                    A(V.tensor_scalar(den[:, b, :], den[:, b, :], 1.0, 0.0, ALU.add, ALU.max))
                    A(V.tensor_tensor(q[:, b, :], q[:, b, :], den[:, b, :], ALU.mult))
                    V.tensor_scalar(q[:, b, :], q[:, b, :], ROOT_MIN, None, ALU.max).then_inc(squared, 1)
                    A(V.tensor_scalar(den[:, b, :], den[:, b, :], MIN_NORM, None, ALU.max))
                    A(V.reciprocal(rden[:, b, :], den[:, b, :]))

                def after_root(h, b):
                    B.start(h)
                    dve.wait_ge(root_in, h + 1)
                    B(V.reciprocal(rroot[:, b, :], root[:, b, :]))
                    B(V.tensor_tensor(rroot[:, b, :], rroot[:, b, :], q[:, b, :], ALU.mult))
                    B(V.tensor_tensor(root[:, b, :], root[:, b, :], rroot[:, b, :], ALU.add))
                    B(V.scalar_tensor_tensor(sn[:, b, :], root[:, b, :], 0.5, rden[:, b, :], ALU.mult, ALU.mult))
                    B(V.tensor_scalar(sn[:, b, :], sn[:, b, :], MIN_NORM, None, ALU.max))
                    V.tensor_scalar(z[:, b, :], sn[:, b, :], Z_MAX, None, ALU.min).then_inc(z_in, 1)

                def factors(h, b):
                    C.start(h)
                    dve.wait_ge(logs_in, h + 1)
                    C(V.tensor_tensor(g[:, b, :], la[:, b, :], lb[:, b, :], ALU.subtract))
                    C(V.reciprocal(rroot[:, b, :], sn[:, b, :]))
                    C(V.tensor_tensor(g[:, b, :], g[:, b, :], rroot[:, b, :], ALU.mult))
                    C(V.scalar_tensor_tensor(g[:, b, :], g[:, b, :], 0.5, rden[:, b, :], ALU.mult, ALU.mult))
                    C(V.tensor_tensor(g[:, b, :], g[:, b, :], k.ew_t[:, bass.DynSlice(h * H, H)], ALU.mult))
                    C(V.tensor_scalar(kb[:, b, :], dst2[:, b, :], -1.0, 1.0, ALU.mult, ALU.add))
                    C(V.scalar_tensor_tensor(fdst[:, b, :], gap[:, b, :], 1.0, g[:, b, :], ALU.add, ALU.mult))
                    V.tensor_tensor(fsrc[:, b, :], g[:, b, :], kb[:, b, :], ALU.mult).then_inc(factors_in, 1)

                for s in range(3):
                    one_hot(s, s)
                for s, i, b, j in ticks(dve):
                    h = i * 2 + b
                    slot = b * H + j
                    one_hot(s + 3, (slot + 3) % R)
                    inner(s, i, slot)
                    if not isinstance(i, int) or s >= LAG + 1:
                        accumulate(nc, k, dve, s - LAG - 1, seg[(slot - LAG - 1) % 2], AW, summed, added)
                    if j == H - 1:
                        before_root(h, b)
                    if not isinstance(i, int) or h >= 1:
                        if j == 0:
                            after_root(h - 1, 1 - b)
                        if j == 1:
                            factors(h - 1, 1 - b)
                after_root(STEPS // H - 1, 1)
                factors(STEPS // H - 1, 1)
                for s in range(STEPS - LAG - 1, STEPS):
                    accumulate(nc, k, dve, s, seg[s % 2], AW, summed, added)

            @block.tensor
            def _(pe):
                def turn_hot(s, slot):
                    pe.wait_ge(hot_ready, s + 1)
                    wait(pe, hotT_in, s - 1)
                    nc.tensor.transpose(turn[slot % 2][:, 0:P], hot[:, slot, :], k.ident[:, :]).then_inc(turned, 1)

                def expand(s, slot):
                    w = pe.value_load(k.win_row[0:1, bass.DynSlice(s, 1)], min_val=0, max_val=W - 1)
                    pe.wait_ge(hotT_in, s + 1)
                    wait(pe, dotted, s - 1)
                    nc.tensor.matmul(base[slot % 2][:, 0:AW], hotT[:, slot % 2, :], at(k.xs, w), start=True, stop=True).then_inc(expanded, 1)

                def segment(s, slot):
                    b, j = slot // H, slot % H
                    pe.wait_ge(scaled_in, s + 1)
                    wait(pe, added, s - 1)
                    nc.tensor.matmul(seg[slot % 2][:, 0:D], hot[:, slot, :], scaled[:, slot % 2, :], start=True, stop=True)
                    nc.tensor.matmul(seg[slot % 2][:, D:AW], hot[:, slot, :], fdst[:, b, j:j + 1], start=True, stop=True).then_inc(summed, 1)

                turn_hot(0, 0)
                turn_hot(1, 1)
                expand(0, 0)
                for s, i, b, j in ticks(pe):
                    slot = b * H + j
                    turn_hot(s + 2, (slot + 2) % R)
                    expand(s + 1, (slot + 1) % R)
                    if not isinstance(i, int) or s >= LAG:
                        segment(s - LAG, (slot - LAG) % R)
                for s in range(STEPS - LAG, STEPS):
                    segment(s, s % R)


def nodes_ball(nc, k, sb, ps, sem):
    ctx = ExitStack()
    with ctx:
        def tmp(name, shape, dt=FP32):
            return ctx.enter_context(nc.sbuf_tensor(name, shape, dt))
        mx = tmp("n2_mx", [P, W, D])
        uT = tmp("n2_uT", [P, 2, D])
        junk = tmp("n2_junk", [P, 2, D])
        bball = tmp("n2_bball", [P, D])
        part = tmp("n2_part", [P, 2, D])
        S = {n: tmp("n2_" + n, [P, W]) for n in (
            "s2", "xm", "il", "r", "un", "t1", "t2", "q", "y2", "xy", "den", "c1", "c2", "xn2", "mb", "mxn2", "xn", "mxn", "z", "la",
            "lb", "f", "d1", "d2", "hn2", "r2", "al", "sr", "e")}
        bs = {n: tmp("n2_b" + n, [P, 1]) for n in ("n2", "n", "t", "y2")}
        turn = [ctx.enter_context(nc.psum_tensor(f"n2_turn{b}", [P, D], FP32)) for b in range(2)]
        prod = [ctx.enter_context(nc.psum_tensor(f"n2_prod{b}", [P, 512], FP32)) for b in range(2)]
        (ch, args_ready, function_in, combined, s2_in, u_in, turned, uT_in, multiplied, mx_in, h_in, relu_in, r2_in, xn2_in, hn2_in, part_in) = (
            sem("n2_" + n) for n in ("ch", "args_ready", "function_in", "combined", "s2_in", "u_in", "turned", "uT_in", "multiplied",
                                     "mx_in", "h_in", "relu_in", "r2_in", "xn2_in", "hn2_in", "part_in"))

        def v(name):
            return S[name][:, :]

        with nc.Block() as block:
            @block.vector
            def _(dve):
                link = Chain(dve, ch)
                V = nc.vector

                def tt(out, a, b, op):
                    link(V.tensor_tensor(v(out), v(a), v(b), op))

                def ts(out, a, s1, s2, op0, op1=None):
                    link(V.tensor_scalar(v(out), v(a), s1, s2, op0, op1) if op1 is not None else V.tensor_scalar(v(out), v(a), s1, None, op0))

                def rec(out, a):
                    link(V.reciprocal(v(out), v(a)))

                def by_scalar(n):
                    dve.sem_inc(args_ready, 1)
                    dve.wait_ge(function_in, n)

                def artanh2(out, a, n):
                    ts("z", a, Z_MAX, None, ALU.min)
                    by_scalar(n)
                    tt(out, "la", "lb", ALU.subtract)

                x2 = k.xs[:, :, D]
                for w in range(W):
                    V.scalar_tensor_tensor(k.agg[:, w, 0:D], k.xs[:, w, 0:D], k.agg[:, w, D:AW], k.agg[:, w, 0:D], ALU.mult, ALU.subtract
                                           ).then_inc(combined, 1)
                    dve.wait_ge(combined, w + 1)
                    wait(dve, part_in, w - 1)
                    V.tensor_tensor_reduce(out=part[:, w % 2, :], in0=k.xs[:, w, 0:D], in1=k.agg[:, w, 0:D], scale=1.0, scalar=0.0,
                                           op0=ALU.mult, op1=ALU.add, accum_out=S["xm"][:, w:w + 1]).then_inc(part_in, 1)
                link(V.tensor_scalar(v("il"), x2, -1.0, 1.0, ALU.mult, ALU.add))
                link(V.tensor_copy(v("t2"), v("il")))
                ts("il", "il", MIN_NORM, None, ALU.max)
                rec("il", "il")
                ts("r", "il", 2.0, MIN_NORM, ALU.mult, ALU.max)
                rec("il", "r")
                ts("il", "il", 2.0, None, ALU.mult)
                dve.wait_ge(s2_in, W)
                by_scalar(1)
                tt("un", "un", "il", ALU.mult)
                ts("un", "un", MIN_NORM, None, ALU.max)
                tt("r", "r", "un", ALU.mult)
                by_scalar(2)
                tt("q", "q", "il", ALU.mult)
                rec("un", "un")
                tt("q", "q", "un", ALU.mult)
                tt("y2", "q", "q", ALU.mult)
                tt("y2", "y2", "s2", ALU.mult)
                tt("xy", "q", "xm", ALU.mult)
                ts("xy", "xy", -2.0, 1.0, ALU.mult, ALU.add)
                link(V.tensor_tensor(v("den"), x2, v("y2"), ALU.mult))
                tt("den", "den", "xy", ALU.add)
                ts("den", "den", MIN_NORM, None, ALU.max)
                rec("den", "den")
                tt("c1", "xy", "y2", ALU.add)
                tt("c1", "c1", "den", ALU.mult)
                tt("c2", "t2", "q", ALU.mult)
                tt("c2", "c2", "den", ALU.mult)
                for w in range(W):
                    V.tensor_scalar(part[:, w % 2, :], k.agg[:, w, 0:D], S["c2"][:, w:w + 1], None, ALU.mult).then_inc(combined, 1)
                    dve.wait_ge(combined, W + w + 1)
                    V.scalar_tensor_tensor(k.agg[:, w, 0:D], k.xs[:, w, 0:D], S["c1"][:, w:w + 1], part[:, w % 2, :], ALU.mult, ALU.subtract
                                           ).then_inc(u_in, 1)
                link(V.tensor_tensor_reduce(out=part[:, 0, :], in0=k.bias2[:, :], in1=k.bias2[:, :], scale=1.0, scalar=0.0,
                                            op0=ALU.mult, op1=ALU.add, accum_out=bs["n2"][:, :]))
                by_scalar(3)
                link(V.tensor_scalar(bs["n"][:, :], bs["n"][:, :], MIN_NORM, None, ALU.max))
                by_scalar(4)
                link(V.reciprocal(bs["n"][:, :], bs["n"][:, :]))
                link(V.tensor_tensor(bs["t"][:, :], bs["t"][:, :], bs["n"][:, :], ALU.mult))
                link(V.tensor_scalar(bball[:, :], k.bias2[:, :], bs["t"][:, 0:1], None, ALU.mult))
                link(V.tensor_tensor(bs["y2"][:, :], bs["t"][:, :], bs["t"][:, :], ALU.mult))
                link(V.tensor_tensor(bs["y2"][:, :], bs["y2"][:, :], bs["n2"][:, :], ALU.mult))
                for w in range(W):
                    dve.wait_ge(mx_in, w + 1)
                    dve.wait_ge(part_in, W + w - 1)
                    V.tensor_tensor_reduce(out=part[:, w % 2, :], in0=mx[:, w, :], in1=bball[:, :], scale=1.0, scalar=0.0,
                                           op0=ALU.mult, op1=ALU.add, accum_out=S["mb"][:, w:w + 1]).then_inc(part_in, 1)
                dve.wait_ge(part_in, 2 * W)
                by_scalar(5)
                ts("xn", "xn", MIN_NORM, None, ALU.max)
                ts("mxn", "mxn", MIN_NORM, None, ALU.max)
                artanh2("f", "xn", 6)
                rec("xn", "xn")
                tt("f", "f", "xn", ALU.mult)
                tt("f", "f", "mxn", ALU.mult)
                by_scalar(7)
                rec("mxn", "mxn")
                tt("f", "f", "mxn", ALU.mult)
                tt("xn2", "f", "f", ALU.mult)
                tt("xn2", "xn2", "mxn2", ALU.mult)
                tt("xy", "f", "mb", ALU.mult)
                ts("xy", "xy", 2.0, 1.0, ALU.mult, ALU.add)
                link(V.scalar_tensor_tensor(v("den"), v("xn2"), bs["y2"][:, 0:1], v("xy"), ALU.mult, ALU.add))
                ts("den", "den", MIN_NORM, None, ALU.max)
                rec("den", "den")
                link(V.scalar_tensor_tensor(v("d1"), v("xy"), bs["y2"][:, 0:1], v("f"), ALU.add, ALU.mult))
                tt("d1", "d1", "den", ALU.mult)
                ts("d2", "xn2", -1.0, 1.0, ALU.mult, ALU.add)
                tt("d2", "d2", "den", ALU.mult)
                for w in range(W):
                    V.tensor_scalar(part[:, w % 2, :], bball[:, :], S["d2"][:, w:w + 1], None, ALU.mult).then_inc(combined, 1)
                    dve.wait_ge(combined, 2 * W + w + 1)
                    V.scalar_tensor_tensor(mx[:, w, :], mx[:, w, :], S["d1"][:, w:w + 1], part[:, w % 2, :], ALU.mult, ALU.add).then_inc(h_in, 1)
                dve.wait_ge(r2_in, W)
                by_scalar(8)
                ts("xn", "xn", MIN_NORM, None, ALU.max)
                artanh2("al", "xn", 9)
                rec("xn", "xn")
                link(V.scalar_tensor_tensor(v("al"), v("al"), 0.5, v("xn"), ALU.mult, ALU.mult))
                tt("mxn", "al", "sr", ALU.mult)
                ts("mxn", "mxn", MIN_NORM, None, ALU.max)
                by_scalar(10)
                rec("mxn", "mxn")
                tt("e", "e", "mxn", ALU.mult)
                tt("e", "e", "al", ALU.mult)
                tt("xn", "e", "sr", ALU.mult)
                ts("xn", "xn", MIN_NORM, None, ALU.max)
                rec("xn", "xn")
                ts("xn", "xn", 1.0 - BALL_EPS, 1.0, ALU.mult, ALU.min)
                tt("e", "e", "xn", ALU.mult)
                for w in range(W):
                    V.scalar_tensor_tensor(k.xs[:, w, 0:D], k.agg[:, w, 0:D], S["e"][:, w:w + 1], k.xs[:, w, 0:D], ALU.mult, ALU.add).then_inc(combined, 1)
                    dve.wait_ge(combined, 3 * W + w + 1)
                    last = V.bn_stats(k.stats[:, w, :], k.xs[:, w, 0:D])
                link(last)
                link(V.memset(k.agg[:, :, :], 0.0))

            @block.tensor
            def _(pe):
                for w in range(W):
                    b = w % 2
                    pe.wait_ge(u_in, w + 1)
                    wait(pe, uT_in, w - 1)
                    for c in range(DC):
                        last = nc.tensor.transpose(turn[b][:, c * P:(c + 1) * P], k.agg[:, w, c * P:(c + 1) * P], k.ident[:, :])
                    last.then_inc(turned, 1)
                    pe.wait_ge(uT_in, w + 1)
                    wait(pe, mx_in, w - 1)
                    for c in range(DC):
                        last = nc.tensor.matmul(prod[b][:, 0:D], uT[:, b, c * P:(c + 1) * P], k.w2l[:, c, :], start=(c == 0), stop=(c == DC - 1))
                    last.then_inc(multiplied, 1)

            @block.scalar
            def _(act):
                function = nc.scalar.activation

                def square_sum(w, row, name):
                    return function(junk[:, w % 2, :], row, ACT.Square, accum_out=S[name][:, w:w + 1])

                for w in range(W):
                    act.wait_ge(combined, w + 1)
                    wait(act, s2_in, w - 1)
                    square_sum(w, k.agg[:, w, 0:D], "s2").then_inc(s2_in, 1)
                act.wait_ge(args_ready, 1)
                function(v("un"), v("s2"), ACT.Sqrt).then_inc(function_in, 1)
                act.wait_ge(args_ready, 2)
                function(v("q"), v("r"), ACT.Tanh, scale=0.5).then_inc(function_in, 1)
                for w in range(W):
                    act.wait_ge(u_in, w + 1)
                    act.wait_ge(mx_in, w) if w else act.wait_ge(s2_in, W)
                    square_sum(w, k.agg[:, w, 0:D], "xn2").then_inc(xn2_in, 1)
                    act.wait_ge(turned, w + 1)
                    wait(act, multiplied, w - 1)
                    function(uT[:, w % 2, :], turn[w % 2][:, :], ACT.Copy).then_inc(uT_in, 1)
                    act.wait_ge(multiplied, w + 1)
                    function(mx[:, w, :], prod[w % 2][:, 0:D], ACT.Copy)
                    act.wait_ge(xn2_in, w + 1)
                    square_sum(w, prod[w % 2][:, 0:D], "mxn2").then_inc(mx_in, 1)
                act.wait_ge(args_ready, 3)
                function(bs["n"][:, :], bs["n2"][:, :], ACT.Sqrt).then_inc(function_in, 1)
                act.wait_ge(args_ready, 4)
                function(bs["t"][:, :], bs["n"][:, :], ACT.Tanh).then_inc(function_in, 1)
                act.wait_ge(args_ready, 5)
                function(v("xn"), v("xn2"), ACT.Sqrt)
                function(v("mxn"), v("mxn2"), ACT.Sqrt).then_inc(function_in, 1)
                act.wait_ge(args_ready, 6)
                function(v("la"), v("z"), ACT.Ln, bias=1.0, scale=1.0)
                function(v("lb"), v("z"), ACT.Ln, bias=1.0, scale=-1.0).then_inc(function_in, 1)
                act.wait_ge(args_ready, 7)
                function(v("f"), v("f"), ACT.Tanh, scale=0.5).then_inc(function_in, 1)
                for w in range(W):
                    act.wait_ge(h_in, w + 1)
                    wait(act, hn2_in, w - 1)
                    square_sum(w, mx[:, w, :], "hn2").then_inc(hn2_in, 1)
                    function(k.agg[:, w, 0:D], mx[:, w, :], ACT.Relu).then_inc(relu_in, 1)
                for w in range(W):
                    act.wait_ge(relu_in, w + 1)
                    wait(act, r2_in, w - 1) if w else act.wait_ge(hn2_in, W)
                    square_sum(w, k.agg[:, w, 0:D], "r2").then_inc(r2_in, 1)
                act.wait_ge(args_ready, 8)
                function(v("xn"), v("hn2"), ACT.Sqrt)
                function(v("sr"), v("r2"), ACT.Sqrt).then_inc(function_in, 1)
                act.wait_ge(args_ready, 9)
                function(v("la"), v("z"), ACT.Ln, bias=1.0, scale=1.0)
                function(v("lb"), v("z"), ACT.Ln, bias=1.0, scale=-1.0).then_inc(function_in, 1)
                act.wait_ge(args_ready, 10)
                function(v("e"), v("mxn"), ACT.Tanh).then_inc(function_in, 1)
    layernorm(nc, k, sem, "n2", k.w13, k.b13, 2 * D, k.p_table)


def edges_gate(nc, k, sb, ps, sem):
    R = 4
    LAG = 3
    ROUNDS = STEPS // R
    ctx = ExitStack()
    with ctx:
        def tmp(name, shape, dt=FP32):
            return ctx.enter_context(nc.sbuf_tensor(name, shape, dt))
        rows = tmp("l3_rows", [P, R, 2 * D])
        attr = tmp("l3_attr", [DE3, R, P])
        hot = tmp("l3_hot", [P, R, P])
        hidT = tmp("l3_hidT", [P, 2, D])
        gsum = tmp("l3_gsum", [P, 2, D])
        gate = tmp("l3_gate", [P, 2, D])
        core = tmp("l3_core", [P, 2, D])
        msg = tmp("l3_msg", [P, 2, D])
        idx = tmp("l3_idx", [P, R], I32)
        p_hid, p_gate, p_core, seg = ([ctx.enter_context(nc.psum_tensor(f"l3_p{n}{j}", [P, 512], FP32)) for j in range(2)] for n in range(4))
        gathered = [sem(f"l3_gathered{j}") for j in range(R)]
        attr_in = [sem(f"l3_attr_in{j}") for j in range(R)]
        (idx_set, issued, hot_ready, hid_made, gate_made, hid_in, gsum_in, gate_in, core_made, core_in, msg_ready, summed, added) = (
            sem("l3_" + n) for n in ("idx_set", "issued", "hot_ready", "hid_made", "gate_made", "hid_in", "gsum_in", "gate_in",
                                     "core_made", "core_in", "msg_ready", "summed", "added"))
        with nc.Block() as block:
            @block.sync
            def _(sp):
                for i in rounds(sp, ROUNDS):
                    for j in range(R):
                        s = i * R + j
                        wait(sp, gate_made, s + 1 - R)
                        t = sp.value_load(k.tile_row[0:1, bass.DynSlice(s, 1)], min_val=0, max_val=T - 1)
                        sp.dma_start(attr[:, j, :], k.ea3[bass.DynSlice(t, 1), :, :].rearrange("o p e -> (o p) e")).then_inc(attr_in[j], 16)

            @block.gpsimd
            def _(pool):
                for i in rounds(pool, ROUNDS):
                    for j in range(R):
                        s = i * R + j
                        wait(pool, gsum_in, s + 1 - R)
                        nc.gpsimd.tensor_copy(idx[:, j:j + 1], col(k.src_t, s)).then_inc(idx_set, 1)
                        pool.wait_ge(idx_set, s + 1)
                        pool.sem_inc(issued, 1)
                        nc.gpsimd.indirect_dma_start(rows[:, j, :], None, k.p_table, bass.IndirectOffsetOnAxis(idx[:, j:j + 1], 0)
                                                     ).then_inc(gathered[j], 16)

            @block.scalar
            def _(act):
                for i in rounds(act, ROUNDS):
                    for j in range(R):
                        s = i * R + j
                        act.wait_ge(hid_made, s + 1)
                        wait(act, core_made, s - 1)
                        nc.scalar.activation(hidT[:, j % 2, :], p_hid[j % 2][:, 0:D], ACT.Relu).then_inc(hid_in, 1)
                        act.wait_ge(gsum_in, s + 1)
                        wait(act, msg_ready, s - 1)
                        nc.scalar.activation(gate[:, j % 2, :], gsum[:, j % 2, :], ACT.Sigmoid).then_inc(gate_in, 1)

            @block.vector
            def _(dve):
                V = nc.vector

                def take_core(s, b):
                    dve.wait_ge(core_made, s + 1)
                    V.tensor_tensor(core[:, b, :], p_core[b][:, 0:D], k.b2[:, :], ALU.add).then_inc(core_in, 1)

                def message(s, b):
                    dve.wait_ge(core_in, s + 1)
                    dve.wait_ge(gate_in, s + 1)
                    wait(dve, summed, s - 1)
                    V.tensor_tensor(msg[:, b, :], core[:, b, :], gate[:, b, :], ALU.mult).then_inc(msg_ready, 1)

                for i in rounds(dve, ROUNDS):
                    for j in range(R):
                        s = i * R + j
                        later = not isinstance(i, int)
                        if later or s >= 1:
                            take_core(s - 1, (j - 1) % 2)
                        wait(dve, summed, s + 1 - R)
                        V.tensor_scalar(hot[:, j, :], k.iota[:, :], col(k.rel_t, s), None, ALU.is_equal).then_inc(hot_ready, 1)
                        if later or s >= 1:
                            message(s - 1, (j - 1) % 2)
                        dve.wait_ge(gate_made, s + 1)
                        wait(dve, gate_in, s - 1)
                        V.tensor_tensor(gsum[:, j % 2, :], p_gate[j % 2][:, 0:D], rows[:, j, D:2 * D], ALU.add).then_inc(gsum_in, 1)
                        if later or s >= LAG:
                            accumulate(nc, k, dve, s - LAG, seg[(j - LAG) % 2], D, summed, added)
                take_core(STEPS - 1, 1)
                message(STEPS - 1, 1)
                for s in range(STEPS - LAG, STEPS):
                    accumulate(nc, k, dve, s, seg[s % 2], D, summed, added)

            @block.tensor
            def _(pe):
                mm = nc.tensor.matmul

                def hidden_and_gate(s, i, j):
                    b = j % 2
                    pe.wait_ge(gathered[j], i * 16 + 16)
                    pe.wait_ge(attr_in[j], i * 16 + 16)
                    wait(pe, hid_in, s - 1)
                    for c in range(DC):
                        f = slice(c * P, (c + 1) * P)
                        mm(p_hid[b][:, f], k.w1b[:, f], attr[:, j, :], start=True, stop=False)
                        last = mm(p_hid[b][:, f], rows[:, j, f], k.ident[:, :], start=False, stop=True)
                    last.then_inc(hid_made, 1)
                    wait(pe, gsum_in, s - 1)
                    mm(p_gate[b][:, 0:D], attr[:, j, :], k.wgb, start=True, stop=True).then_inc(gate_made, 1)

                def times_w2(s, b):
                    pe.wait_ge(hid_in, s + 1)
                    wait(pe, core_in, s - 1)
                    for c in range(DC):
                        last = mm(p_core[b][:, 0:D], hidT[:, b, c * P:(c + 1) * P], k.w2[:, c, :], start=(c == 0), stop=(c == DC - 1))
                    last.then_inc(core_made, 1)

                def segment(s, j):
                    b = j % 2
                    pe.wait_ge(msg_ready, s + 1)
                    wait(pe, added, s - 1)
                    mm(seg[b][:, 0:D], hot[:, j, :], msg[:, b, :], start=True, stop=True).then_inc(summed, 1)

                for i in rounds(pe, ROUNDS):
                    for j in range(R):
                        s = i * R + j
                        hidden_and_gate(s, i, j)
                        if not isinstance(i, int) or s >= 1:
                            times_w2(s - 1, (j - 1) % 2)
                        if not isinstance(i, int) or s >= 2:
                            segment(s - 2, (j - 2) % R)
                times_w2(STEPS - 1, 1)
                segment(STEPS - 2, R - 2)
                segment(STEPS - 1, R - 1)


def nodes_gate(nc, k, sb, ps, sem):
    ctx = ExitStack()
    with ctx:
        mv = ctx.enter_context(nc.sbuf_tensor("n3a_mv", [P, W, 2], FP32))
        rstd = ctx.enter_context(nc.sbuf_tensor("n3a_rstd", [P, W], FP32))
        ch, var_in, root_in = (sem("n3_" + n) for n in ("ch", "var_in", "root_in"))
        with nc.Block() as block:
            @block.scalar
            def _(act):
                act.wait_ge(var_in, 1)
                nc.scalar.activation(rstd[:, :], rstd[:, :], ACT.Sqrt).then_inc(root_in, 1)

            @block.vector
            def _(dve):
                V = nc.vector
                link = Chain(dve, ch)
                for w in link.loop(W, 1):
                    link(V.tensor_tensor(at(k.agg, w, D), at(k.agg, w, D), at(k.xs, w, D), ALU.add))
                    V.bn_stats(at(k.stats, w), at(k.agg, w, D))
                link(V.memset(rstd[:, :], LN_EPS))
                for w in range(W):
                    last = V.bn_aggr(mv[:, w, :], k.stats[:, w, :])
                link(last)
                V.tensor_tensor(rstd[:, :], mv[:, :, 1], rstd[:, :], ALU.add).then_inc(var_in, 1)
                dve.wait_ge(root_in, 1)
                link(V.reciprocal(rstd[:, :], rstd[:, :]))
                for w in link.loop(W, 4):
                    link(V.tensor_scalar(at(k.agg, w, D), at(k.agg, w, D), mv[:, bass.DynSlice(w, 1), 0], col(rstd, w), ALU.subtract, ALU.mult))
                    link(V.tensor_tensor(at(k.agg, w, D), at(k.agg, w, D), k.gamma[:, :], ALU.mult))
                    link(V.tensor_tensor(at(k.agg, w, D), at(k.agg, w, D), k.beta[:, :], ALU.add))
                    link(V.tensor_tensor(at(k.xs, w, D), at(k.xs, w, D), at(k.agg, w, D), ALU.add))
                    V.bn_stats(at(k.stats, w), at(k.xs, w, D))
    layernorm(nc, k, sem, "n3", None, None, 0, None)


def finish(nc, k, sem, src):
    out_stored = sem("out_stored")
    with nc.Block() as block:
        @block.sync
        def _(sp):
            sp.dma_start(k.out[0:(W - 1) * P, :].rearrange("(w p) f -> p w f", p=P), src[:, 0:W - 1, 0:D]).then_inc(out_stored, 16)
            sp.dma_start(k.out[(W - 1) * P:N, :], src[0:TAIL, W - 1, 0:D]).then_inc(out_stored, 16)
            sp.wait_ge(out_stored, 32)


def gnn_kernel(nc, args, out):
    k = Parts(args, out)
    ctx = ExitStack()
    with ctx:
        def sb(name, shape, dt):
            return ctx.enter_context(nc.sbuf_tensor(name, shape, dt))

        def ps(name, shape, dt):
            return ctx.enter_context(nc.psum_tensor(name, shape, dt))

        live = []

        def sem(name):
            live.append(nc.alloc_semaphore(name))
            return live[-1]

        def phase(build, *more):
            build(nc, k, *more)
            nc.clear_and_free_semaphores(live)
            nc.all_engine_barrier()
            live.clear()
        k.h = nc.dram_tensor("h_table", (W * P, D), FP32).ap()
        k.x2_table = nc.dram_tensor("x2_table", (W * P, AW), FP32).ap()
        k.p_table = nc.dram_tensor("p_table", (W * P, 2 * D), FP32).ap()
        phase(setup, sb, ps, sem)
        phase(edges_mean, sb, ps, sem)
        phase(nodes_mean, sb, ps, sem)
        phase(edges_spline, sb, ps, sem)
        phase(nodes_spline, sb, ps, sem)
        phase(norms, sem)
        phase(edges_ball, sb, ps, sem)
        phase(nodes_ball, sb, ps, sem)
        phase(edges_gate, sb, ps, sem)
        phase(nodes_gate, sb, ps, sem)
        phase(finish, sem, k.xs)


def kernel(x, src, dst, edge_attr_384, edge_attr_64, edge_weight, L0_gnn_W_l, L0_gnn_W_r, L0_gnn_b_r, L1_gnn_W_edge,
           L1_gnn_b_edge, L1_gnn_W_node, L1_gnn_b_node, L1_gnn_base_weight, L1_gnn_spline_weight, L1_gnn_spline_scaler,
           L2_gnn_weight, L2_gnn_bias, L3_gnn_W1, L3_gnn_b1, L3_gnn_W2, L3_gnn_b2, L3_gnn_Wg, L3_gnn_bg, L3_gnn_gamma,
           L3_gnn_beta):
    import numpy as np
    import concourse.bacc as bacc
    from concourse.bass_utils import run_bass_kernel_spmd

    ins = {
        "x": x, "src": src, "dst": dst, "edge_weight": edge_weight,
        "wl_t": np.asarray(L0_gnn_W_l).T, "wr_t": np.asarray(L0_gnn_W_r).T, "b_r": L0_gnn_b_r,
        "wn_t": np.asarray(L1_gnn_W_node).T, "b_node": L1_gnn_b_node, "we_t": np.asarray(L1_gnn_W_edge).T, "b_edge": L1_gnn_b_edge,
        "ea1": np.asarray(edge_attr_384).reshape(T, P, KC1, P).transpose(0, 3, 2, 1),
        "base_t": np.asarray(L1_gnn_base_weight).T, "scaler_t": np.asarray(L1_gnn_spline_scaler).T,
        "spline_t": np.asarray(L1_gnn_spline_weight).transpose(2, 1, 0),
        "w2l_t": np.asarray(L2_gnn_weight).T, "l2_bias": L2_gnn_bias,
        "ea3": np.asarray(edge_attr_64).reshape(T, P, DE3).transpose(0, 2, 1),
        "w1": L3_gnn_W1, "b1": L3_gnn_b1, "w2_in": L3_gnn_W2, "b2_in": L3_gnn_b2, "wg": L3_gnn_Wg, "bg": L3_gnn_bg,
        "gamma_in": L3_gnn_gamma, "beta_in": L3_gnn_beta,
    }
    nc = bacc.Bacc("TRN2", target_bir_lowering=False, num_devices=1)
    arrays, args = {}, {}
    for name, a in ins.items():
        a = np.ascontiguousarray(a)
        arrays[f"in_{name}"] = a
        args[name] = nc.dram_tensor(f"in_{name}", a.shape, mybir.dt.from_np(a.dtype), kind="ExternalInput").ap()
    out = nc.dram_tensor("out_0", (N, D), FP32, kind="ExternalOutput").ap()
    gnn_kernel(nc, args, out)
    r = run_bass_kernel_spmd(nc, [arrays], core_ids=[0])
    return r.results[0]["out_0"]
```

```python
from contextlib import ExitStack

import concourse.bass as bass
from concourse import mybir

FP32 = mybir.dt.float32
FP32R = mybir.dt.float32r
I32 = mybir.dt.int32
ALU = mybir.AluOpType
ACT = mybir.ActivationFunctionType

P = 128
N = 2500
E = 80000
D = 256
DC = D // P
DE1 = 384
KC1 = DE1 // P
DE3 = 64
W = -(-N // P)
TAIL = N - (W - 1) * P
T = E // P
G = 2
NG = -(-T // G)
PAIRS = NG + W - 1
R = 4
HB = 4
NH = 3
RB = NH * HB
BALL_PAIRS = -(-PAIRS // RB) * RB
assert PAIRS % R == 0
SC = -(-BALL_PAIRS * G // P)
SP_ = SC * P
AW = D + 1
LN_EPS = 1e-5
INPUTS = ("x", "src", "dst", "edge_weight", "wl_t", "wr_t", "b_r", "wn_t", "b_node", "we_t", "b_edge", "ea1", "base_t", "scaler_t",
          "spline_t", "w2l_t", "l2_bias", "ea3", "w1", "b1", "w2_in", "b2_in", "wg", "bg", "gamma_in", "beta_in")
NB = 7


def rounds(eng, n):
    yield 0
    with eng.Fori(1, n) as i:
        yield i


def wait(eng, sem, value):
    if not isinstance(value, int) or value > 0:
        eng.wait_ge(sem, value)


class Chain:

    def __init__(self, eng, sem):
        self.eng, self.sem, self.n, self.r = eng, sem, 0, 0

    def __call__(self, ins):
        ins.then_inc(self.sem, 1)
        self.n += 1
        self.eng.wait_ge(self.sem, self.r + self.n)

    def loop(self, count, per):
        base = self.n
        with self.eng.Fori(0, count) as i:
            self.r, self.n = i * per + base, 0
            yield i
            assert self.n == per, self.n
        self.r, self.n = 0, base + count * per


class Parts:

    def __init__(self, args, out):
        (self.x, self.src, self.dst, self.edge_weight, self.wl_t, self.wr_t, self.b_r, self.wn_t, self.b_node, self.we_t,
         self.b_edge, self.ea1, self.base_t, self.scaler_t, self.spline_t, self.w2l_t, self.l2_bias, self.ea3, self.w1, self.b1,
         self.w2_in, self.b2_in, self.wg, self.bg, self.gamma_in, self.beta_in) = (args[name] for name in INPUTS)
        self.out = out


def at(t, i, width=None):
    cols = slice(None) if width is None else slice(0, width)
    if isinstance(i, int):
        return t[:, i, cols]
    return t[:, bass.DynSlice(i, 1), cols].rearrange("p o f -> p (o f)")


def col(t, i):
    return t[:, bass.DynSlice(i, 1)]


def setup(nc, k, sb, ps, sem):
    k.iota = sb("iota", [P, P], FP32)
    k.ident = sb("ident", [P, P], FP32)
    k.ones = sb("ones", [P, P], FP32)
    k.xs = sb("xs", [P, W, AW], FP32)
    k.stats = sb("stats", [P, W, 6], FP32)
    k.agg = sb("agg", [P, W, AW], FP32)
    k.src_t = sb("src_t", [P, SP_], I32)
    k.rel_t = sb("rel_t", [P, SP_], FP32)
    k.ew_t = sb("ew_t", [P, SP_], FP32)
    k.tile_row = sb("tile_row", [1, SP_], I32)
    k.win_row = sb("win_row", [1, SP_], I32)
    k.wl, k.wr, k.wn, k.wbase, k.scaler, k.w2l, k.w2 = (
        sb(n, [P, DC, D], FP32) for n in ("wl", "wr", "wn", "wbase", "scaler", "w2l", "w2"))
    k.we = sb("we", [P, KC1, D], FP32)
    k.wsp = sb("wsp", [P, NB, DC, D], FP32)
    k.ones_r = sb("ones_r", [P, P], FP32R)
    k.w13 = sb("w13", [P, DC, 2 * D], FP32)
    k.we3 = sb("we3", [P, 2 * D], FP32)
    k.br, k.bn, k.be, k.bias2, k.b2, k.gamma, k.beta = (
        sb(n, [P, D], FP32) for n in ("br", "bn", "be", "bias2", "b2b", "gamma", "beta"))
    k.b13 = sb("b13", [P, 2 * D], FP32)
    weights = [(k.wl, k.wl_t), (k.wr, k.wr_t), (k.wn, k.wn_t), (k.we, k.we_t), (k.wbase, k.base_t), (k.scaler, k.scaler_t),
               (k.w2l, k.w2l_t), (k.w2, k.w2_in), (k.w13[:, :, 0:D], k.w1[0:D, :]), (k.w13[:, :, D:2 * D], k.wg[0:D, :])]
    biases = [(k.br[:, :], k.b_r), (k.bn[:, :], k.b_node), (k.be[:, :], k.b_edge), (k.bias2[:, :], k.l2_bias), (k.b2[:, :], k.b2_in),
              (k.gamma[:, :], k.gamma_in), (k.beta[:, :], k.beta_in), (k.b13[:, 0:D], k.b1), (k.b13[:, D:2 * D], k.bg)]

    QT = -(-(NG - 1) // P)
    TP = (NG - 1) // QT
    assert TP * QT == NG - 1
    ctx = ExitStack()
    def tmp(name, shape, dt):
        return ctx.enter_context(nc.sbuf_tensor(name, shape, dt))
    with ctx:
        dst_tiles = tmp("dst_tiles", [TP, QT, G * P], I32)
        last_win = tmp("last_win", [TP, QT], I32)
        last_pos = tmp("last_pos", [TP, QT], FP32)
        tile_id = tmp("tile_id", [TP, QT], FP32)
        step_row = tmp("step_row", [P, SP_], FP32)
        col_id = tmp("col_id", [P, SC], I32)
        pair_i = tmp("pair_i", [P, SC], I32)
        id_f = tmp("id_f", [P, SC], FP32)
        pair_f = tmp("pair_f", [P, SC], FP32)
        first = tmp("first", [P, SC], FP32)
        bad = tmp("bad", [P, SC], FP32)
        part = tmp("part", [P, 1], FP32)
        passed = tmp("passed", [TP, QT, SP_], FP32)
        tile_f = tmp("tile_f", [1, SP_], FP32)
        win_f = tmp("win_f", [1, SP_], FP32)
        tcol_f = tmp("tcol_f", [P, SC], FP32)
        tcol = tmp("tcol", [P, SC], I32)
        wcol = tmp("wcol", [P, SC], FP32)
        dst_s = tmp("dst_s", [P, SC, P], I32)
        src_s = tmp("src_s", [P, SC, P], I32)
        ew_s = tmp("ew_s", [P, SC, P], FP32)
        conv = tmp("conv", [P, 3, SC, P], FP32)
        pcount = ctx.enter_context(nc.psum_tensor("pcount", [P, 2, 512], FP32))
        ptile = ctx.enter_context(nc.psum_tensor("ptile", [P, SC], FP32))
        ptr = ctx.enter_context(nc.psum_tensor("ptr", [P, 3, P], FP32))
        loaded = sem("setup_loaded")
        xs_zero = sem("xs_zero")
        dst_loaded = sem("dst_loaded")
        iotas = sem("iotas")
        passed_ready = sem("passed_ready")
        counted = sem("counted")
        tcol_ready = sem("tcol_ready")
        rows_in = sem("rows_in")
        conv_ready = sem("conv_ready")
        turned = sem("turned")
        taken = sem("taken")
        ch = sem("setup_chain")
        with nc.Block() as block:
            @block.sync
            def _(sp):
                sp.dma_start(dst_tiles[:, :, :], k.dst[0:(NG - 1) * G * P].rearrange("(p q e) -> p q e", q=QT, e=G * P)).then_inc(dst_loaded, 16)
                sp.dma_start(k.xs[:, 0:W - 1, 0:D], k.x[0:(W - 1) * P, :].rearrange("(w p) f -> p w f", p=P)).then_inc(loaded, 16)
                sp.wait_ge(xs_zero, 1)
                sp.dma_start(k.xs[0:TAIL, W - 1, 0:D], k.x[(W - 1) * P:N, :]).then_inc(loaded, 16)
                n = 2
                for dst, src in weights:
                    sp.dma_start(dst[:, :, :], src.rearrange("(c p) o -> p c o", p=P)).then_inc(loaded, 16)
                    n += 1
                for kk in range(NB):
                    sp.dma_start(k.wsp[:, kk, :, :], k.spline_t[kk].rearrange("(c p) o -> p c o", p=P)).then_inc(loaded, 16)
                    n += 1
                for half in range(2):
                    for cols, src in ((slice(0, D), k.w1), (slice(D, 2 * D), k.wg)):
                        sp.dma_start(k.we3[half * DE3:(half + 1) * DE3, cols], src[D:D + DE3, :]).then_inc(loaded, 16)
                        n += 1
                for dst, src in biases:
                    sp.dma_start(dst, src[None, :].broadcast_to([P, D])).then_inc(loaded, 16)
                    n += 1
                sp.wait_ge(loaded, 16 * n)

            @block.gpsimd
            def _(pool):
                nc.gpsimd.iota(k.iota[:, :], [[1, P]], base=0, channel_multiplier=0, allow_small_or_imprecise_dtypes=True).then_inc(iotas, 1)
                nc.gpsimd.iota(part[:, :], [[1, 1]], base=0, channel_multiplier=1, allow_small_or_imprecise_dtypes=True).then_inc(iotas, 1)
                nc.gpsimd.iota(tile_id[:, :], [[1, QT]], base=0, channel_multiplier=QT, allow_small_or_imprecise_dtypes=True).then_inc(iotas, 1)
                nc.gpsimd.iota(step_row[:, :], [[1, SP_ // G], [0, G]], base=0, channel_multiplier=0, allow_small_or_imprecise_dtypes=True
                               ).then_inc(iotas, 1)
                nc.gpsimd.iota(col_id[:, :], [[P, SC]], base=0, channel_multiplier=1).then_inc(iotas, 1)
                pool.wait_ge(tcol_ready, 1)
                n = 0
                for c in range(SC):
                    for rows, table in ((dst_s, k.dst), (src_s, k.src), (ew_s, k.edge_weight)):
                        nc.gpsimd.indirect_dma_start(rows[:, c, :], None, table.rearrange("(t e) -> t e", e=P),
                                                     bass.IndirectOffsetOnAxis(tcol[:, c:c + 1], 0)).then_inc(rows_in, 16)
                        n += 1
                pool.wait_ge(rows_in, 16 * n)

            @block.vector
            def _(dve):
                link = Chain(dve, ch)
                nc.vector.memset(k.xs[:, W - 1, :], 0.0).then_inc(xs_zero, 1)
                nc.vector.memset(k.ones[:, :], 1.0)
                link(nc.vector.memset(k.agg[:, :, :], 0.0))
                dve.wait_ge(iotas, 5)
                nc.vector.tensor_scalar(k.ident[:, :], k.iota[:, :], part[:, 0:1], None, ALU.is_equal)
                dve.wait_ge(dst_loaded, 16)
                link(nc.vector.tensor_scalar(last_win[:, :], dst_tiles[:, :, G * P - 1], 7, None, ALU.logical_shift_right))
                link(nc.vector.tensor_copy(last_pos[:, :], last_win[:, :]))
                link(nc.vector.tensor_tensor(last_pos[:, :], last_pos[:, :], tile_id[:, :], ALU.add))
                for q in range(QT):
                    last = nc.vector.tensor_scalar(passed[:, q, :], step_row[0:TP, :], last_pos[:, q:q + 1], None, ALU.is_gt)
                last.then_inc(passed_ready, 1)
                dve.wait_ge(counted, 1)
                link(nc.vector.tensor_scalar(pair_i[:, :], col_id[:, :], G.bit_length() - 1, None, ALU.logical_shift_right))
                link(nc.vector.tensor_copy(pair_f[:, :], pair_i[:, :]))
                link(nc.vector.tensor_copy(id_f[:, :], col_id[:, :]))
                link(nc.vector.scalar_tensor_tensor(id_f[:, :], pair_f[:, :], -float(G), id_f[:, :], ALU.mult, ALU.add))
                link(nc.vector.tensor_scalar(first[:, :], ptile[:, :], float(G), None, ALU.mult))
                link(nc.vector.scalar_tensor_tensor(tcol_f[:, :], first[:, :], float(T - G), id_f[:, :], ALU.min, ALU.add))
                nc.vector.tensor_copy(tcol[:, :], tcol_f[:, :]).then_inc(tcol_ready, 1)
                link(nc.vector.tensor_tensor(bad[:, :], tcol_f[:, :], first[:, :], ALU.is_lt))
                link(nc.vector.tensor_tensor(wcol[:, :], pair_f[:, :], ptile[:, :], ALU.subtract))
                link(nc.vector.tensor_scalar(wcol[:, :], wcol[:, :], float(P), None, ALU.mult))
                link(nc.vector.scalar_tensor_tensor(wcol[:, :], bad[:, :], float(W * P), wcol[:, :], ALU.mult, ALU.add))
                half = SP_ // 2
                for h in range(2):
                    cols = slice(h * half, (h + 1) * half)
                    nc.vector.tensor_scalar(tile_f[:, cols], pcount[0:1, h, 0:half], float(G), float(T - G), ALU.mult, ALU.min)
                    link(nc.vector.tensor_tensor(win_f[:, cols], step_row[0:1, cols], pcount[0:1, h, 0:half], ALU.subtract))
                nc.vector.tensor_copy(k.tile_row[:, :], tile_f[:, :])
                link(nc.vector.tensor_scalar(win_f[:, :], win_f[:, :], float(W - 1), None, ALU.min))
                link(nc.vector.tensor_copy(k.win_row[:, :], win_f[:, :]))
                dve.wait_ge(rows_in, 16 * 3 * SC)
                for c in range(SC):
                    nc.vector.tensor_copy(conv[:, 0, c, :], src_s[:, c, :])
                    nc.vector.tensor_scalar(conv[:, 1, c, :], dst_s[:, c, :], wcol[:, c:c + 1], None, ALU.subtract)
                    nc.vector.tensor_copy(conv[:, 2, c, :], ew_s[:, c, :]).then_inc(conv_ready, 1)
                for c in range(SC):
                    cols = slice(c * P, (c + 1) * P)
                    dve.wait_ge(turned, c + 1)
                    nc.vector.tensor_copy(k.src_t[:, cols], ptr[:, 0, :])
                    nc.vector.tensor_copy(k.rel_t[:, cols], ptr[:, 1, :])
                    nc.vector.tensor_copy(k.ew_t[:, cols], ptr[:, 2, :]).then_inc(taken, 1)

            @block.tensor
            def _(pe):
                pe.wait_ge(passed_ready, 1)
                for h in range(2):
                    for q in range(QT):
                        nc.tensor.matmul(pcount[:, h, 0:SP_ // 2], k.ones[0:TP, :], passed[:, q, h * SP_ // 2:(h + 1) * SP_ // 2],
                                         start=(q == 0), stop=(q == QT - 1))
                for c in range(SC):
                    for q in range(QT):
                        last = nc.tensor.matmul(ptile[:, c:c + 1], passed[:, q, c * P:(c + 1) * P], k.ones[0:TP, 0:1],
                                                start=(q == 0), stop=(q == QT - 1))
                last.then_inc(counted, 1)
                for c in range(SC):
                    pe.wait_ge(conv_ready, c + 1)
                    if c:
                        pe.wait_ge(taken, c)
                    for t in range(3):
                        last = nc.tensor.transpose(ptr[:, t, :], conv[:, t, c, :], k.ident[:, :])
                    last.then_inc(turned, 1)


def pairs(eng, n=PAIRS, slots=R):
    for i in rounds(eng, n // slots):
        for j in range(slots):
            yield i * slots + j, i, j


def reached(u, n):
    return not isinstance(u, int) or u >= n


def table_cols(t, u):
    return t[:, bass.DynSlice(u * G, G)]


def window(k, eng, u):
    return eng.value_load(k.win_row[0:1, bass.DynSlice(u * G, 1)], min_val=0, max_val=W - 1)


def set_indices(nc, k, idx, u, j, idx_set):
    nc.scalar.activation(idx[:, j, :], table_cols(k.src_t, u), ACT.Copy).then_inc(idx_set, 1)


def gather_pair(nc, pool, u, j, idx, idx_set, issued, rows, table, gathered):
    pool.wait_ge(idx_set, u + 1)
    pool.sem_inc(issued, 1)
    for e in range(G):
        nc.gpsimd.indirect_dma_start(rows[:, j, e, :], None, table, bass.IndirectOffsetOnAxis(idx[:, j, e:e + 1], 0)
                                     ).then_inc(gathered[j], 16)


def one_hots(nc, k, u, j, hot, hot_ready):
    for e in range(G):
        last = nc.vector.tensor_scalar(hot[:, j, e, :], k.iota[:, :], col(k.rel_t, u * G + e), None, ALU.is_equal)
    last.then_inc(hot_ready, 1)


def accumulate(nc, k, dve, u, seg, width, summed, added):
    dve.wait_ge(summed, u + 1)
    wait(dve, added, u)
    w = window(k, dve, u)
    nc.vector.tensor_tensor(at(k.agg, w, width), at(k.agg, w, width), seg[:, 0:width], ALU.add).then_inc(added, 1)


def edges_mean(nc, k, sb, ps, sem):
    LAG = 2
    ctx = ExitStack()
    with ctx:
        rows = ctx.enter_context(nc.sbuf_tensor("l0_rows", [P, R, G, AW], FP32))
        hot = ctx.enter_context(nc.sbuf_tensor("l0_hot", [P, R, G, P], FP32))
        idx = ctx.enter_context(nc.sbuf_tensor("l0_idx", [P, R, G], I32))
        seg = [ctx.enter_context(nc.psum_tensor(f"l0_seg{j}", [P, 512], FP32)) for j in range(R)]
        gathered = [sem(f"l0_gathered{j}") for j in range(R)]
        ones_set, idx_set, issued, hot_ready, summed, added = (
            sem("l0_" + n) for n in ("ones_set", "idx_set", "issued", "hot_ready", "summed", "added"))
        with nc.Block() as block:
            @block.gpsimd
            def _(pool):
                pool.wait_ge(ones_set, 1)
                for u, i, j in pairs(pool):
                    gather_pair(nc, pool, u, j, idx, idx_set, issued, rows[:, :, :, 0:D], k.x, gathered)

            @block.scalar
            def _(act):
                for u, i, j in pairs(act):
                    wait(act, summed, u + 1 - R)
                    set_indices(nc, k, idx, u, j, idx_set)

            @block.vector
            def _(dve):
                nc.vector.memset(rows[:, :, :, D:AW], 1.0).then_inc(ones_set, 1)
                for u, i, j in pairs(dve):
                    wait(dve, summed, u + 1 - R)
                    one_hots(nc, k, u, j, hot, hot_ready)
                    if reached(u, LAG):
                        accumulate(nc, k, dve, u - LAG, seg[(j - LAG) % R], AW, summed, added)
                for u in range(PAIRS - LAG, PAIRS):
                    accumulate(nc, k, dve, u, seg[u % R], AW, summed, added)

            @block.tensor
            def _(pe):
                for u, i, j in pairs(pe):
                    wait(pe, added, u + 1 - R)
                    pe.wait_ge(hot_ready, u + 1)
                    pe.wait_ge(gathered[j], i * 16 * G + 16 * G)
                    for e in range(G):
                        last = nc.tensor.matmul(seg[j][:, 0:AW], hot[:, j, e, :], rows[:, j, e, :], start=(e == 0), stop=(e == G - 1))
                    last.then_inc(summed, 1)


def nodes_mean(nc, k, sb, ps, sem):
    ctx = ExitStack()
    with ctx:
        def tmp(name, shape, dt=FP32):
            return ctx.enter_context(nc.sbuf_tensor(name, shape, dt))
        rc = tmp("n0_rc", [P, W])
        mean = tmp("n0_mean", [P, D])
        opT = tmp("n0_opT", [P, 4, P])
        turn = ctx.enter_context(nc.psum_tensor("n0_turn", [P, 4, P], FP32))
        prod = ctx.enter_context(nc.psum_tensor("n0_prod", [P, 512], FP32))
        row = tmp("n0_row", [P, D])
        mean_ready, brought, turned, copied, multiplied, ch = (
            sem("n0_" + n) for n in ("mean_ready", "brought", "turned", "copied", "multiplied", "ch"))
        with nc.Block() as block:
            @block.vector
            def _(dve):
                link = Chain(dve, ch)
                link(nc.vector.tensor_scalar(rc[:, :], k.agg[:, :, D], 1.0, None, ALU.max))
                link(nc.vector.reciprocal(rc[:, :], rc[:, :]))
                for w in link.loop(W, 3):
                    nc.vector.tensor_scalar(mean[:, :], at(k.agg, w, D), col(rc, w), None, ALU.mult).then_inc(mean_ready, 1)
                    dve.wait_ge(multiplied, w + 1)
                    link(nc.vector.tensor_tensor(at(k.xs, w, D), at(k.xs, w, D), prod[:, 0:D], ALU.add))
                    link(nc.vector.tensor_tensor(at(k.xs, w, D), at(k.xs, w, D), k.br[:, :], ALU.add))
                    link(nc.vector.bn_stats(at(k.stats, w), at(k.xs, w, D)))
                link(nc.vector.memset(k.agg[:, :, :], 0.0))

            @block.tensor
            def _(pe):
                for w in rounds(pe, W):
                    pe.wait_ge(mean_ready, w + 1)
                    pe.wait_ge(brought, w + 1)
                    for c in range(DC):
                        nc.tensor.transpose(turn[:, c, :], mean[:, c * P:(c + 1) * P], k.ident[:, :])
                    for c in range(DC):
                        last = nc.tensor.transpose(turn[:, DC + c, :], row[:, c * P:(c + 1) * P], k.ident[:, :])
                    last.then_inc(turned, 1)
                    pe.wait_ge(copied, w + 1)
                    for c in range(2 * DC):
                        last = nc.tensor.matmul(prod[:, 0:D], opT[:, c, :], (k.wl if c < DC else k.wr)[:, c % DC, :],
                                                start=(c == 0), stop=(c == 2 * DC - 1))
                    last.then_inc(multiplied, 1)

            @block.gpsimd
            def _(pool):
                for w in rounds(pool, W):
                    wait(pool, turned, w)
                    nc.gpsimd.tensor_copy(row[:, :], at(k.xs, w, D)).then_inc(brought, 1)

            @block.scalar
            def _(act):
                with act.Fori(0, W) as w:
                    act.wait_ge(turned, w + 1)
                    nc.scalar.activation(opT[:, :, :], turn[:, :, :], ACT.Copy).then_inc(copied, 1)
        layernorm(nc, k, sem, "n0", k.wn, k.bn, D, k.h)


def layernorm(nc, k, sem, tag, weight, bias, width, table):
    ctx = ExitStack()
    with ctx:
        def tmp(name, shape, dt=FP32):
            return ctx.enter_context(nc.sbuf_tensor(tag + name, shape, dt))
        rstd = tmp("_rstd", [P, W])
        mv = tmp("_mv", [P, W, 2])
        ch, rooted, normed = (sem(f"{tag}_{n}") for n in ("lch", "rooted", "normed"))
        with nc.Block() as block:
            @block.scalar
            def _(act):
                act.wait_ge(ch, 2)
                nc.scalar.activation(rstd[:, :], rstd[:, :], ACT.Sqrt).then_inc(rooted, 1)

            @block.vector
            def _(dve):
                link = Chain(dve, ch)
                for w in range(W):
                    last = nc.vector.bn_aggr(mv[:, w, :], k.stats[:, w, :])
                link(last)
                link(nc.vector.tensor_scalar(rstd[:, :], mv[:, :, 1], LN_EPS, None, ALU.add))
                dve.wait_ge(rooted, 1)
                link(nc.vector.reciprocal(rstd[:, :], rstd[:, :]))
                with dve.Fori(0, W) as w:
                    nc.vector.tensor_scalar(at(k.xs, w, D), at(k.xs, w, D), mv[:, bass.DynSlice(w, 1), 0], col(rstd, w),
                                            ALU.subtract, ALU.mult).then_inc(normed, 1)
    if weight is not None:
        project(nc, k, sem, tag, weight, bias, width, table)


def project(nc, k, sem, tag, weight, bias, width, table):
    ctx = ExitStack()
    with ctx:
        def tmp(name, shape, dt=FP32):
            return ctx.enter_context(nc.sbuf_tensor(tag + name, shape, dt))
        opT = tmp("_lnT", [P, 2, DC, P])
        row = tmp("_lrow", [P, 2, D])
        made = tmp("_made", [P, W, width])
        turn = [ctx.enter_context(nc.psum_tensor(f"{tag}_lturn{b}", [P, DC, P], FP32)) for b in range(2)]
        prod = [ctx.enter_context(nc.psum_tensor(f"{tag}_lprod{b}", [P, 512], FP32)) for b in range(2)]
        brought, turned, copied, multiplied, added, stored = (
            sem(f"{tag}_{n}") for n in ("lbrought", "lturned", "lcopied", "lmult", "ladded", "stored"))
        with nc.Block() as block:
            @block.scalar
            def _(act):
                with act.Fori(0, W // 2) as i:
                    for b in range(2):
                        act.wait_ge(turned, i * 2 + b + 1)
                        nc.scalar.activation(opT[:, b, :, :], turn[b][:, :, :], ACT.Copy).then_inc(copied, 1)

            @block.vector
            def _(dve):
                with dve.Fori(0, W // 2) as i:
                    for b in range(2):
                        w = i * 2 + b
                        dve.wait_ge(multiplied, w + 1)
                        nc.vector.tensor_tensor(at(made, w), prod[b][:, 0:width], bias[:, 0:width], ALU.add).then_inc(added, 1)

            @block.gpsimd
            def _(pool):
                for i in rounds(pool, W // 2):
                    for b in range(2):
                        w = i * 2 + b
                        wait(pool, turned, w - 1)
                        nc.gpsimd.tensor_copy(row[:, b, :], at(k.xs, w, D)).then_inc(brought, 1)

            @block.tensor
            def _(pe):
                for i in rounds(pe, W // 2):
                    for b in range(2):
                        w = i * 2 + b
                        wait(pe, copied, w - 1)
                        pe.wait_ge(brought, w + 1)
                        for c in range(DC):
                            last = nc.tensor.transpose(turn[b][:, c, :], row[:, b, c * P:(c + 1) * P], k.ident[:, :])
                        last.then_inc(turned, 1)
                        pe.wait_ge(copied, w + 1)
                        wait(pe, added, w - 1)
                        for c in range(DC):
                            last = nc.tensor.matmul(prod[b][:, 0:width], opT[:, b, c, :], weight[:, c, :], start=(c == 0), stop=(c == DC - 1))
                        last.then_inc(multiplied, 1)

            @block.sync
            def _(sp):
                sp.wait_ge(added, W)
                sp.dma_start(table.rearrange("(w p) f -> p w f", p=P), made[:, :, :]).then_inc(stored, 16)
                sp.wait_ge(stored, 16)


def split_bias(nc, k, tag, sem, bias, bias_hl, copies):
    high = sem(tag + "_bias_high")
    done, cleared = sem(tag + "_bias_done"), sem(tag + "_bias_cleared")
    with nc.sbuf_tensor(tag + "_bias_hi", [P, D], FP32R) as hi, nc.Block() as block:
        @block.scalar
        def _(act):
            nc.scalar.activation(k.ones_r[:, :], k.ones[:, :], ACT.Copy)
            nc.scalar.activation(hi[:, :], bias[:, :], ACT.Copy).then_inc(high, 1)
            act.wait_ge(cleared, 1)
            for g in range(copies):
                last = nc.scalar.activation(bias_hl[0:1, g, :], bias[0:1, :], ACT.Copy)
            last.then_inc(done, 1)

        @block.vector
        def _(dve):
            nc.vector.memset(bias_hl[:, :, :].bitcast(FP32), 0.0).then_inc(cleared, 1)
            dve.wait_ge(high, 1)
            dve.wait_ge(cleared, 1)
            for g in range(copies):
                last = nc.vector.tensor_tensor(bias_hl[32:33, g, :], bias[32:33, :], hi[32:33, :].bitcast(FP32), ALU.subtract)
            last.then_inc(done, 1)


def edges_spline(nc, k, sb, ps, sem):
    ctx = ExitStack()
    with ctx:
        def tmp(name, shape, dt=FP32):
            return ctx.enter_context(nc.sbuf_tensor(name, shape, dt))
        rows = tmp("l1_rows", [P, R, G, D])
        attr = tmp("l1_attr", [P, R, G, KC1, P])
        hot = tmp("l1_hot", [P, R, G, P], FP32R)
        msg = tmp("l1_msg", [P, R, G, D])
        high = tmp("l1_high", [P, 2, G, D], FP32R)
        low = tmp("l1_low", [P, 2, G, D], FP32R)
        bias_hl = tmp("l1_bias", [P, G, D], FP32R)
        idx = tmp("l1_idx", [P, R, G], I32)
        split_bias(nc, k, "l1", sem, k.be, bias_hl, G)
        prod = [ctx.enter_context(nc.psum_tensor(f"l1_prod{j}", [P, G, D], FP32)) for j in range(R)]
        seg = [ctx.enter_context(nc.psum_tensor(f"l1_seg{j}", [P, 512], FP32)) for j in range(2)]
        gathered = [sem(f"l1_gathered{j}") for j in range(R)]
        attr_in = [sem(f"l1_attr_in{j}") for j in range(R)]
        idx_set, issued, hot_ready, multiplied, msg_ready, high_in, low_in, summed, added = (
            sem("l1_" + n) for n in ("idx_set", "issued", "hot_ready", "multiplied", "msg_ready", "high_in", "low_in", "summed", "added"))
        with nc.Block() as block:
            @block.sync
            def _(sp):
                for u, i, j in pairs(sp):
                    wait(sp, multiplied, u + 1 - R)
                    t = sp.value_load(k.tile_row[0:1, bass.DynSlice(u * G, 1)], min_val=0, max_val=T - G)
                    sp.dma_start(attr[:, j, :, :, :], k.ea1[bass.DynSlice(t, G), :, :, :].rearrange("g p c e -> p g c e")
                                 ).then_inc(attr_in[j], 16)

            @block.gpsimd
            def _(pool):
                for u, i, j in pairs(pool):
                    gather_pair(nc, pool, u, j, idx, idx_set, issued, rows, k.h, gathered)

            @block.scalar
            def _(act):
                AHEAD = 2

                def split_high(u, j):
                    act.wait_ge(msg_ready, u + 1)
                    wait(act, summed, u - 1)
                    nc.scalar.activation(high[:, j % 2, :, :], msg[:, j, :, :], ACT.Copy).then_inc(high_in, 1)

                for u, i, j in pairs(act):
                    wait(act, msg_ready, u + 1 - R)
                    set_indices(nc, k, idx, u, j, idx_set)
                    if reached(u, AHEAD):
                        split_high(u - AHEAD, (j - AHEAD) % R)
                for u in range(PAIRS - AHEAD, PAIRS):
                    split_high(u, u % R)

            @block.vector
            def _(dve):
                def message(u, i, j):
                    dve.wait_ge(multiplied, u + 1)
                    dve.wait_ge(gathered[j], i * 16 * G + 16 * G)
                    nc.vector.tensor_tensor(msg[:, j, :, :], prod[j][:, :, :], rows[:, j, :, :], ALU.mult).then_inc(msg_ready, 1)

                def split_low(u, j):
                    dve.wait_ge(high_in, u + 1)
                    wait(dve, summed, u - 1)
                    dve.wait_ge(msg_ready, u + 1)
                    nc.vector.tensor_tensor(low[:, j % 2, :, :], msg[:, j, :, :], high[:, j % 2, :, :].bitcast(FP32), ALU.subtract
                                            ).then_inc(low_in, 1)

                for u, i, j in pairs(dve):
                    wait(dve, summed, u + 1 - R)
                    one_hots(nc, k, u, j, hot, hot_ready)
                    message(u, i, j)
                    if reached(u, 1):
                        split_low(u - 1, (j - 1) % R)
                    if reached(u, 3):
                        accumulate(nc, k, dve, u - 3, seg[(j - 3) % 2], D, summed, added)
                split_low(PAIRS - 1, R - 1)
                for u in range(PAIRS - 3, PAIRS):
                    accumulate(nc, k, dve, u, seg[u % 2], D, summed, added)

            @block.tensor
            def _(pe):
                mm = nc.tensor.matmul

                def products(u, i, j):
                    pe.wait_ge(attr_in[j], i * 16 + 16)
                    wait(pe, msg_ready, u + 1 - R)
                    mm(prod[j][:, :, :], k.ones_r[:, :], bias_hl[:, :, :], start=True, stop=False)
                    for e in range(G):
                        for c in range(KC1):
                            last = mm(prod[j][:, e, :], attr[:, j, e, c, :], k.we[:, c, :], start=False, stop=(e == G - 1 and c == KC1 - 1))
                    last.then_inc(multiplied, 1)

                def segment(u, j):
                    pe.wait_ge(low_in, u + 1)
                    pe.wait_ge(high_in, u + 1)
                    pe.wait_ge(hot_ready, u + 1)
                    wait(pe, added, u - 1)
                    for e in range(G):
                        for n, part in enumerate((high, low)):
                            last = mm(seg[j % 2][:, 0:D], hot[:, j, e, :], part[:, j % 2, e, :], start=(e == 0 and n == 0), stop=(e == G - 1 and n == 1))
                    last.then_inc(summed, 1)

                for u, i, j in pairs(pe):
                    products(u, i, j)
                    if reached(u, 2):
                        segment(u - 2, (j - 2) % R)
                segment(PAIRS - 2, R - 2)
                segment(PAIRS - 1, R - 1)


def nodes_spline(nc, k, sb, ps, sem):
    ctx = ExitStack()
    with ctx:
        def tmp(name, shape, dt=FP32):
            return ctx.enter_context(nc.sbuf_tensor(name, shape, dt))
        centre = tmp("n1_centre", [P, NB])
        row = tmp("n1_row", [P, 2, D])
        aggT = tmp("n1_aggT", [P, 2, D])
        siluT = tmp("n1_siluT", [P, 2, D])
        near = tmp("n1_near", [P, 2, NB, D])
        far = tmp("n1_far", [P, 2, NB, D])
        sq = tmp("n1_sq", [P, 2, NB, D])
        sqn = tmp("n1_sqn", [P, 2, NB, D])
        basis = tmp("n1_basis", [P, 2, NB, D])
        turn = [ctx.enter_context(nc.psum_tensor(f"n1_turn{b}", [P, D], FP32)) for b in range(2)]
        prod = [ctx.enter_context(nc.psum_tensor(f"n1_prod{b}", [P, 512], FP32)) for b in range(2)]
        (brought, turned, aggT_in, silu_in, dist_in, near_in, far_in, sq_in, cube_in, basis_in, multiplied, xs_in, centred, ch,
         scaled) = (sem("n1_" + n) for n in (
             "brought", "turned", "aggT_in", "silu_in", "dist_in", "near_in", "far_in", "sq_in", "cube_in", "basis_in",
             "multiplied", "xs_in", "centred", "ch", "scaled"))
        with nc.Block() as block:
            @block.gpsimd
            def _(pool):
                for i in rounds(pool, W // 2):
                    for b in range(2):
                        w = i * 2 + b
                        wait(pool, turned, w - 1)
                        nc.gpsimd.tensor_copy(row[:, b, :], at(k.agg, w, D)).then_inc(brought, 1)

            @block.scalar
            def _(act):
                act.wait_ge(centred, 1)
                for i in rounds(act, W // 2):
                    for b in range(2):
                        w = i * 2 + b
                        act.wait_ge(turned, w + 1)
                        wait(act, multiplied, w - 1)
                        nc.scalar.activation(siluT[:, b, :], turn[b][:, :], ACT.Silu).then_inc(silu_in, 1)
                        wait(act, basis_in, w - 1)
                        for n in range(NB):
                            last = nc.scalar.activation(near[:, b, n, :], turn[b][:, :], ACT.Abs, bias=centre[:, n:n + 1], scale=2.0)
                        last.then_inc(dist_in, 1)
                        act.wait_ge(near_in, w + 1)
                        nc.scalar.activation(sq[:, b, :, :], far[:, b, :, :], ACT.Square)
                        nc.scalar.activation(sqn[:, b, :, :], near[:, b, :, :], ACT.Square).then_inc(sq_in, 1)

            @block.vector
            def _(dve):
                link = Chain(dve, ch)
                link(nc.vector.tensor_scalar(centre[:, :], k.iota[:, 0:NB], -1.0, 3.0, ALU.mult, ALU.add))
                nc.vector.tensor_copy(centre[:, :], centre[:, :]).then_inc(centred, 1)
                for n in range(NB):
                    last = nc.vector.scalar_tensor_tensor(k.wsp[:, n, :, :], k.wsp[:, n, :, :], 1.0 / 6.0, k.scaler[:, :, :], ALU.mult, ALU.mult)
                last.then_inc(scaled, 1)

                def take(w, b):
                    dve.wait_ge(multiplied, w + 1)
                    nc.vector.tensor_tensor(at(k.xs, w, D), at(k.xs, w, D), prod[b][:, 0:D], ALU.add).then_inc(xs_in, 1)
                    dve.wait_ge(xs_in, w + 1)
                    nc.vector.bn_stats(at(k.stats, w), at(k.xs, w, D))

                for i in rounds(dve, W // 2):
                    for b in range(2):
                        w = i * 2 + b
                        dve.wait_ge(dist_in, w + 1)
                        wait(dve, multiplied, w - 1)
                        nc.vector.tensor_scalar(far[:, b, :, :], near[:, b, :, :], 2.0, 2.0, ALU.min, ALU.subtract).then_inc(far_in, 1)
                        dve.wait_ge(far_in, w + 1)
                        nc.vector.tensor_scalar(near[:, b, :, :], near[:, b, :, :], 1.0, 1.0, ALU.min, ALU.subtract).then_inc(near_in, 1)
                        dve.wait_ge(sq_in, w + 1)
                        nc.vector.tensor_tensor(sq[:, b, :, :], sq[:, b, :, :], far[:, b, :, :], ALU.mult)
                        nc.vector.scalar_tensor_tensor(sqn[:, b, :, :], sqn[:, b, :, :], 4.0, near[:, b, :, :], ALU.mult, ALU.mult).then_inc(cube_in, 1)
                        dve.wait_ge(cube_in, w + 1)
                        nc.vector.tensor_tensor(basis[:, b, :, :], sqn[:, b, :, :], sq[:, b, :, :], ALU.subtract).then_inc(basis_in, 1)
                        if not isinstance(i, int) or w >= 1:
                            take(w - 1, 1 - b)
                take(W - 1, 1)
                link(nc.vector.memset(k.agg[:, :, :], 0.0))

            @block.tensor
            def _(pe):
                pe.wait_ge(scaled, 1)

                def turn_rows(w, b):
                    pe.wait_ge(brought, w + 1)
                    wait(pe, silu_in, w - 1)
                    wait(pe, dist_in, w - 1)
                    for c in range(DC):
                        last = nc.tensor.transpose(turn[b][:, c * P:(c + 1) * P], row[:, b, c * P:(c + 1) * P], k.ident[:, :])
                    last.then_inc(turned, 1)

                def multiply(w, b):
                    pe.wait_ge(silu_in, w + 1)
                    wait(pe, xs_in, w - 1)
                    for c in range(DC):
                        nc.tensor.matmul(prod[b][:, 0:D], siluT[:, b, c * P:(c + 1) * P], k.wbase[:, c, :], start=(c == 0), stop=False)
                    pe.wait_ge(basis_in, w + 1)
                    for n in range(NB):
                        for c in range(DC):
                            last = nc.tensor.matmul(prod[b][:, 0:D], basis[:, b, n, c * P:(c + 1) * P], k.wsp[:, n, c, :],
                                                    start=False, stop=(n == NB - 1 and c == DC - 1))
                    last.then_inc(multiplied, 1)

                turn_rows(0, 0)
                for i in rounds(pe, W // 2 - 1):
                    for b in range(2):
                        w = i * 2 + b
                        turn_rows(w + 1, 1 - b)
                        multiply(w, b)
                turn_rows(W - 1, 1)
                multiply(W - 2, 0)
                multiply(W - 1, 1)
    layernorm(nc, k, sem, "n1", None, None, 0, None)


MIN_NORM = 1e-15
BALL_EPS = 1e-5
Z_MAX = 1.0 - 1e-7
ROOT_MIN = 2.0 ** -60


class Linked:

    def __init__(self, eng, sem, per):
        self.eng, self.sem, self.per = eng, sem, per

    def start(self, h):
        self.base, self.n = h * self.per, 0

    def __call__(self, ins):
        ins.then_inc(self.sem, 1)
        self.n += 1
        assert self.n <= self.per
        self.eng.wait_ge(self.sem, self.base + self.n)


def norms(nc, k, sem):
    normed, stored = sem("x2_normed"), sem("x2_stored")
    with nc.sbuf_tensor("x2_junk", [P, 2, D], FP32) as junk, nc.Block() as block:
        @block.scalar
        def _(act):
            for w in range(W):
                wait(act, normed, w - 1)
                nc.scalar.activation(junk[:, w % 2, :], k.xs[:, w, 0:D], ACT.Square, accum_out=k.xs[:, w, D:AW]).then_inc(normed, 1)

        @block.sync
        def _(sp):
            sp.wait_ge(normed, W)
            sp.dma_start(k.x2_table.rearrange("(w p) f -> p w f", p=P), k.xs[:, :, :]).then_inc(stored, 16)
            sp.wait_ge(stored, 16)


def edges_ball(nc, k, sb, ps, sem):
    LAG = HB + 2
    ctx = ExitStack()
    with ctx:
        def tmp(name, shape, dt=FP32):
            return ctx.enter_context(nc.sbuf_tensor(name, shape, dt))
        rows = tmp("l2_rows", [P, RB, G, AW])
        hot = tmp("l2_hot", [P, RB, G, P])
        hotT = tmp("l2_hotT", [P, 2, G, P])
        scaled = tmp("l2_scaled", [P, 2, G, D])
        junk = tmp("l2_junk", [P, 2, D])
        idx = tmp("l2_idx", [P, RB, G], I32)
        dot, dst2, gap, q, den, rden, prod2, root, rroot, sn, z, la, lb, g, kb, fsrc, fdst = (
            tmp("l2_" + n, [P, NH, HB, G]) for n in ("dot", "dst2", "gap", "q", "den", "rden", "prod2", "root", "rroot", "sn", "z",
                                                     "la", "lb", "g", "kb", "fsrc", "fdst"))
        turn = [ctx.enter_context(nc.psum_tensor(f"l2_turn{j}", [P, G, D], FP32)) for j in range(2)]
        base = [ctx.enter_context(nc.psum_tensor(f"l2_base{j}", [P, G, D], FP32)) for j in range(2)]
        seg = [ctx.enter_context(nc.psum_tensor(f"l2_seg{j}", [P, 512], FP32)) for j in range(2)]
        gathered = [sem(f"l2_gathered{j}") for j in range(RB)]
        (idx_set, issued, hot_ready, turned, hotT_in, expanded, product_in, dst2_in, scaled_in, summed, added, squared, logq_in, root_in,
         z_in, logs_in, factors_in, cha, chb, chc) = (sem("l2_" + n) for n in (
             "idx_set", "issued", "hot_ready", "turned", "hotT_in", "expanded", "product_in", "dst2_in", "scaled_in", "summed", "added",
             "squared", "logq_in", "root_in", "z_in", "logs_in", "factors_in", "cha", "chb", "chc"))

        def ticks(eng):
            for u, i, j in pairs(eng, BALL_PAIRS, RB):
                yield u, i, j, i * NH + j // HB, j % HB

        def group_before(h, b):
            return h - 1, (b - 1) % NH

        with nc.Block() as block:
            @block.gpsimd
            def _(pool):
                for u, i, j, h, _ in ticks(pool):
                    gather_pair(nc, pool, u, j, idx, idx_set, issued, rows, k.x2_table, gathered)

            @block.scalar
            def _(act):
                act.preload_act_table_set("natural_log_exp_and_others")
                AHEAD = 4

                def indices(u, j):
                    wait(act, scaled_in, u * G + (1 - RB) * G)
                    set_indices(nc, k, idx, u, j, idx_set)

                def copy_hot(u, j):
                    act.wait_ge(turned, u + 1)
                    wait(act, expanded, u - 1)
                    nc.scalar.activation(hotT[:, j % 2, :, :], turn[j % 2][:, :, 0:P], ACT.Copy).then_inc(hotT_in, 1)

                def scale_rows(u, h, j):
                    act.wait_ge(factors_in, h + 1)
                    wait(act, summed, u - 1)
                    for e in range(G):
                        nc.scalar.activation(scaled[:, j % 2, e, :], rows[:, j, e, 0:D], ACT.Copy, scale=fsrc[:, j // HB, j % HB, e:e + 1]
                                             ).then_inc(scaled_in, 1)

                def roots(h, b):
                    act.wait_ge(squared, h + 1)
                    nc.scalar.activation(root[:, b, :, :], q[:, b, :, :], ACT.Ln).then_inc(logq_in, 1)
                    act.wait_ge(logq_in, h + 1)
                    nc.scalar.activation(root[:, b, :, :], root[:, b, :, :], ACT.Exp, scale=0.5).then_inc(root_in, 1)

                def logs(h, b):
                    act.wait_ge(z_in, h + 1)
                    nc.scalar.activation(la[:, b, :, :], z[:, b, :, :], ACT.Ln, bias=1.0, scale=1.0)
                    nc.scalar.activation(lb[:, b, :, :], z[:, b, :, :], ACT.Ln, bias=1.0, scale=-1.0).then_inc(logs_in, 1)

                for u in range(AHEAD):
                    indices(u, u)
                copy_hot(0, 0)
                for u, i, j, h, p in ticks(act):
                    copy_hot(u + 1, (j + 1) % RB)
                    indices(u + AHEAD, (j + AHEAD) % RB)
                    if reached(u, LAG):
                        scale_rows(u - LAG, h - 1 if p >= LAG - HB else h - 2, (j - LAG) % RB)
                    if p == HB - 1:
                        roots(h, j // HB)
                    if p == 0 and reached(u, HB):
                        logs(*group_before(h, j // HB))
                logs(BALL_PAIRS // HB - 1, NH - 1)
                for u in range(BALL_PAIRS - LAG, BALL_PAIRS):
                    scale_rows(u, u // HB, u % RB)

            @block.vector
            def _(dve):
                A, B, C = Linked(dve, cha, 9), Linked(dve, chb, 5), Linked(dve, chc, 7)
                V = nc.vector

                def one_hot(u, j):
                    wait(dve, summed, u + 1 - RB)
                    one_hots(nc, k, u, j, hot, hot_ready)

                def inner(u, i, j):
                    dve.wait_ge(gathered[j], i * 16 * G + 16 * G)
                    dve.wait_ge(expanded, u + 1)
                    for e in range(G):
                        wait(dve, product_in, u * G - G + e + 1)
                        last = V.tensor_tensor_reduce(out=junk[:, e, :], in0=rows[:, j, e, 0:D], in1=base[j % 2][:, e, :], scale=1.0, scalar=0.0,
                                                      op0=ALU.mult, op1=ALU.add, accum_out=dot[:, j // HB, j % HB, e:e + 1])
                        last.then_inc(product_in, 1)
                    V.tensor_copy(dst2[:, j // HB, j % HB, :], turn[j % 2][:, :, P]).then_inc(dst2_in, 1)

                def before_root(h, b):
                    A.start(h)
                    src2 = rows[:, b * HB:(b + 1) * HB, :, D]
                    dve.wait_ge(dst2_in, h * HB + HB)
                    A(V.scalar_tensor_tensor(gap[:, b, :, :], dot[:, b, :, :], -2.0, src2, ALU.mult, ALU.add))
                    A(V.tensor_tensor(prod2[:, b, :, :], dst2[:, b, :, :], src2, ALU.mult))
                    A(V.tensor_tensor(q[:, b, :, :], gap[:, b, :, :], dst2[:, b, :, :], ALU.add))
                    A(V.scalar_tensor_tensor(den[:, b, :, :], dot[:, b, :, :], -2.0, prod2[:, b, :, :], ALU.mult, ALU.add))
                    A(V.tensor_scalar(q[:, b, :, :], q[:, b, :, :], 0.0, None, ALU.max))
                    A(V.tensor_scalar(den[:, b, :, :], den[:, b, :, :], 1.0, 0.0, ALU.add, ALU.max))
                    A(V.tensor_tensor(q[:, b, :, :], q[:, b, :, :], den[:, b, :, :], ALU.mult))
                    V.tensor_scalar(q[:, b, :, :], q[:, b, :, :], ROOT_MIN, None, ALU.max).then_inc(squared, 1)
                    A(V.tensor_scalar(den[:, b, :, :], den[:, b, :, :], MIN_NORM, None, ALU.max))
                    A(V.reciprocal(rden[:, b, :, :], den[:, b, :, :]))

                def after_root(h, b):
                    B.start(h)
                    dve.wait_ge(root_in, h + 1)
                    B(V.reciprocal(rroot[:, b, :, :], root[:, b, :, :]))
                    B(V.tensor_tensor(rroot[:, b, :, :], rroot[:, b, :, :], q[:, b, :, :], ALU.mult))
                    B(V.tensor_tensor(root[:, b, :, :], root[:, b, :, :], rroot[:, b, :, :], ALU.add))
                    B(V.scalar_tensor_tensor(sn[:, b, :, :], root[:, b, :, :], 0.5, rden[:, b, :, :], ALU.mult, ALU.mult))
                    B(V.tensor_scalar(sn[:, b, :, :], sn[:, b, :, :], MIN_NORM, None, ALU.max))
                    V.tensor_scalar(z[:, b, :, :], sn[:, b, :, :], Z_MAX, None, ALU.min).then_inc(z_in, 1)

                def factors(h, b):
                    C.start(h)
                    dve.wait_ge(logs_in, h + 1)
                    weight = k.ew_t[:, bass.DynSlice(h * (HB * G), HB * G)].rearrange("p (u e) -> p u e", e=G)
                    C(V.tensor_tensor(g[:, b, :, :], la[:, b, :, :], lb[:, b, :, :], ALU.subtract))
                    C(V.reciprocal(rroot[:, b, :, :], sn[:, b, :, :]))
                    C(V.tensor_tensor(g[:, b, :, :], g[:, b, :, :], rroot[:, b, :, :], ALU.mult))
                    C(V.scalar_tensor_tensor(g[:, b, :, :], g[:, b, :, :], 0.5, rden[:, b, :, :], ALU.mult, ALU.mult))
                    C(V.tensor_tensor(g[:, b, :, :], g[:, b, :, :], weight, ALU.mult))
                    C(V.tensor_scalar(kb[:, b, :, :], dst2[:, b, :, :], -1.0, 1.0, ALU.mult, ALU.add))
                    C(V.scalar_tensor_tensor(fdst[:, b, :, :], gap[:, b, :, :], 1.0, g[:, b, :, :], ALU.add, ALU.mult))
                    V.tensor_tensor(fsrc[:, b, :, :], g[:, b, :, :], kb[:, b, :, :], ALU.mult).then_inc(factors_in, 1)

                one_hot(0, 0)
                one_hot(1, 1)
                for u, i, j, h, p in ticks(dve):
                    one_hot(u + 2, (j + 2) % RB)
                    inner(u, i, j)
                    if reached(u, LAG + 1):
                        accumulate(nc, k, dve, u - LAG - 1, seg[(j - LAG - 1) % 2], AW, summed, added)
                    if p == HB - 1:
                        before_root(h, j // HB)
                    if reached(u, HB):
                        if p == 0:
                            after_root(*group_before(h, j // HB))
                        if p == 1:
                            factors(*group_before(h, j // HB))
                after_root(BALL_PAIRS // HB - 1, NH - 1)
                factors(BALL_PAIRS // HB - 1, NH - 1)
                for u in range(BALL_PAIRS - LAG - 1, BALL_PAIRS):
                    accumulate(nc, k, dve, u, seg[u % 2], AW, summed, added)

            @block.tensor
            def _(pe):
                mm = nc.tensor.matmul

                def turn_hot(u, j):
                    pe.wait_ge(hot_ready, u + 1)
                    wait(pe, dst2_in, u - 1)
                    for e in range(G):
                        last = nc.tensor.transpose(turn[j % 2][:, e, 0:P], hot[:, j, e, :], k.ident[:, :])
                    last.then_inc(turned, 1)

                def expand(u, j):
                    w = window(k, pe, u)
                    pe.wait_ge(hotT_in, u + 1)
                    wait(pe, product_in, u * G - G)
                    for e in range(G):
                        x = at(k.xs, w)
                        mm(turn[j % 2][:, e, P:P + 1], hotT[:, j % 2, e, :], x[:, D:AW], start=True, stop=True)
                        last = mm(base[j % 2][:, e, :], hotT[:, j % 2, e, :], x[:, 0:D], start=True, stop=True)
                    last.then_inc(expanded, 1)

                def segment(u, j):
                    pe.wait_ge(scaled_in, u * G + G)
                    wait(pe, added, u - 1)
                    for e in range(G):
                        mm(seg[j % 2][:, 0:D], hot[:, j, e, :], scaled[:, j % 2, e, :], start=(e == 0), stop=False)
                        last = mm(seg[j % 2][:, D:AW], hot[:, j, e, :], fdst[:, j // HB, j % HB, e:e + 1], start=False, stop=(e == G - 1))
                    last.then_inc(summed, 1)

                turn_hot(0, 0)
                for u, i, j, h, p in ticks(pe):
                    turn_hot(u + 1, (j + 1) % RB)
                    expand(u, j)
                    if reached(u, LAG):
                        segment(u - LAG, (j - LAG) % RB)
                for u in range(BALL_PAIRS - LAG, BALL_PAIRS):
                    segment(u, u % RB)


def nodes_ball(nc, k, sb, ps, sem):
    ctx = ExitStack()
    with ctx:
        def tmp(name, shape, dt=FP32):
            return ctx.enter_context(nc.sbuf_tensor(name, shape, dt))
        mx = tmp("n2_mx", [P, W, D])
        uT = tmp("n2_uT", [P, 2, D])
        junk = tmp("n2_junk", [P, 2, D])
        bball = tmp("n2_bball", [P, D])
        part = tmp("n2_part", [P, 2, D])
        S = {n: tmp("n2_" + n, [P, W]) for n in (
            "s2", "xm", "il", "r", "un", "t1", "t2", "q", "y2", "xy", "den", "c1", "c2", "xn2", "mb", "mxn2", "xn", "mxn", "z", "la",
            "lb", "f", "d1", "d2", "hn2", "r2", "al", "sr", "e")}
        bs = {n: tmp("n2_b" + n, [P, 1]) for n in ("n2", "n", "t", "y2")}
        turn = [ctx.enter_context(nc.psum_tensor(f"n2_turn{b}", [P, D], FP32)) for b in range(2)]
        prod = [ctx.enter_context(nc.psum_tensor(f"n2_prod{b}", [P, 512], FP32)) for b in range(2)]
        (ch, args_ready, function_in, combined, s2_in, u_in, turned, uT_in, multiplied, mx_in, h_in, relu_in, r2_in, xn2_in, hn2_in, part_in) = (
            sem("n2_" + n) for n in ("ch", "args_ready", "function_in", "combined", "s2_in", "u_in", "turned", "uT_in", "multiplied",
                                     "mx_in", "h_in", "relu_in", "r2_in", "xn2_in", "hn2_in", "part_in"))

        def v(name):
            return S[name][:, :]

        with nc.Block() as block:
            @block.vector
            def _(dve):
                link = Chain(dve, ch)
                V = nc.vector

                def tt(out, a, b, op):
                    link(V.tensor_tensor(v(out), v(a), v(b), op))

                def ts(out, a, s1, s2, op0, op1=None):
                    link(V.tensor_scalar(v(out), v(a), s1, s2, op0, op1) if op1 is not None else V.tensor_scalar(v(out), v(a), s1, None, op0))

                def rec(out, a):
                    link(V.reciprocal(v(out), v(a)))

                def by_scalar(n):
                    dve.sem_inc(args_ready, 1)
                    dve.wait_ge(function_in, n)

                def artanh2(out, a, n):
                    ts("z", a, Z_MAX, None, ALU.min)
                    by_scalar(n)
                    tt(out, "la", "lb", ALU.subtract)

                x2 = k.xs[:, :, D]
                for w in range(W):
                    V.scalar_tensor_tensor(k.agg[:, w, 0:D], k.xs[:, w, 0:D], k.agg[:, w, D:AW], k.agg[:, w, 0:D], ALU.mult, ALU.subtract
                                           ).then_inc(combined, 1)
                    dve.wait_ge(combined, w + 1)
                    wait(dve, part_in, w - 1)
                    V.tensor_tensor_reduce(out=part[:, w % 2, :], in0=k.xs[:, w, 0:D], in1=k.agg[:, w, 0:D], scale=1.0, scalar=0.0,
                                           op0=ALU.mult, op1=ALU.add, accum_out=S["xm"][:, w:w + 1]).then_inc(part_in, 1)
                link(V.tensor_scalar(v("il"), x2, -1.0, 1.0, ALU.mult, ALU.add))
                link(V.tensor_copy(v("t2"), v("il")))
                ts("il", "il", MIN_NORM, None, ALU.max)
                rec("il", "il")
                ts("r", "il", 2.0, MIN_NORM, ALU.mult, ALU.max)
                rec("il", "r")
                ts("il", "il", 2.0, None, ALU.mult)
                dve.wait_ge(s2_in, W)
                by_scalar(1)
                tt("un", "un", "il", ALU.mult)
                ts("un", "un", MIN_NORM, None, ALU.max)
                tt("r", "r", "un", ALU.mult)
                by_scalar(2)
                tt("q", "q", "il", ALU.mult)
                rec("un", "un")
                tt("q", "q", "un", ALU.mult)
                tt("y2", "q", "q", ALU.mult)
                tt("y2", "y2", "s2", ALU.mult)
                tt("xy", "q", "xm", ALU.mult)
                ts("xy", "xy", -2.0, 1.0, ALU.mult, ALU.add)
                link(V.tensor_tensor(v("den"), x2, v("y2"), ALU.mult))
                tt("den", "den", "xy", ALU.add)
                ts("den", "den", MIN_NORM, None, ALU.max)
                rec("den", "den")
                tt("c1", "xy", "y2", ALU.add)
                tt("c1", "c1", "den", ALU.mult)
                tt("c2", "t2", "q", ALU.mult)
                tt("c2", "c2", "den", ALU.mult)
                for w in range(W):
                    V.tensor_scalar(part[:, w % 2, :], k.agg[:, w, 0:D], S["c2"][:, w:w + 1], None, ALU.mult).then_inc(combined, 1)
                    dve.wait_ge(combined, W + w + 1)
                    V.scalar_tensor_tensor(k.agg[:, w, 0:D], k.xs[:, w, 0:D], S["c1"][:, w:w + 1], part[:, w % 2, :], ALU.mult, ALU.subtract
                                           ).then_inc(u_in, 1)
                link(V.tensor_tensor_reduce(out=part[:, 0, :], in0=k.bias2[:, :], in1=k.bias2[:, :], scale=1.0, scalar=0.0,
                                            op0=ALU.mult, op1=ALU.add, accum_out=bs["n2"][:, :]))
                by_scalar(3)
                link(V.tensor_scalar(bs["n"][:, :], bs["n"][:, :], MIN_NORM, None, ALU.max))
                by_scalar(4)
                link(V.reciprocal(bs["n"][:, :], bs["n"][:, :]))
                link(V.tensor_tensor(bs["t"][:, :], bs["t"][:, :], bs["n"][:, :], ALU.mult))
                link(V.tensor_scalar(bball[:, :], k.bias2[:, :], bs["t"][:, 0:1], None, ALU.mult))
                link(V.tensor_tensor(bs["y2"][:, :], bs["t"][:, :], bs["t"][:, :], ALU.mult))
                link(V.tensor_tensor(bs["y2"][:, :], bs["y2"][:, :], bs["n2"][:, :], ALU.mult))
                for w in range(W):
                    dve.wait_ge(mx_in, w + 1)
                    dve.wait_ge(part_in, W + w - 1)
                    V.tensor_tensor_reduce(out=part[:, w % 2, :], in0=mx[:, w, :], in1=bball[:, :], scale=1.0, scalar=0.0,
                                           op0=ALU.mult, op1=ALU.add, accum_out=S["mb"][:, w:w + 1]).then_inc(part_in, 1)
                dve.wait_ge(part_in, 2 * W)
                by_scalar(5)
                ts("xn", "xn", MIN_NORM, None, ALU.max)
                ts("mxn", "mxn", MIN_NORM, None, ALU.max)
                artanh2("f", "xn", 6)
                rec("xn", "xn")
                tt("f", "f", "xn", ALU.mult)
                tt("f", "f", "mxn", ALU.mult)
                by_scalar(7)
                rec("mxn", "mxn")
                tt("f", "f", "mxn", ALU.mult)
                tt("xn2", "f", "f", ALU.mult)
                tt("xn2", "xn2", "mxn2", ALU.mult)
                tt("xy", "f", "mb", ALU.mult)
                ts("xy", "xy", 2.0, 1.0, ALU.mult, ALU.add)
                link(V.scalar_tensor_tensor(v("den"), v("xn2"), bs["y2"][:, 0:1], v("xy"), ALU.mult, ALU.add))
                ts("den", "den", MIN_NORM, None, ALU.max)
                rec("den", "den")
                link(V.scalar_tensor_tensor(v("d1"), v("xy"), bs["y2"][:, 0:1], v("f"), ALU.add, ALU.mult))
                tt("d1", "d1", "den", ALU.mult)
                ts("d2", "xn2", -1.0, 1.0, ALU.mult, ALU.add)
                tt("d2", "d2", "den", ALU.mult)
                for w in range(W):
                    V.tensor_scalar(part[:, w % 2, :], bball[:, :], S["d2"][:, w:w + 1], None, ALU.mult).then_inc(combined, 1)
                    dve.wait_ge(combined, 2 * W + w + 1)
                    V.scalar_tensor_tensor(mx[:, w, :], mx[:, w, :], S["d1"][:, w:w + 1], part[:, w % 2, :], ALU.mult, ALU.add).then_inc(h_in, 1)
                dve.wait_ge(r2_in, W)
                by_scalar(8)
                ts("xn", "xn", MIN_NORM, None, ALU.max)
                artanh2("al", "xn", 9)
                rec("xn", "xn")
                link(V.scalar_tensor_tensor(v("al"), v("al"), 0.5, v("xn"), ALU.mult, ALU.mult))
                tt("mxn", "al", "sr", ALU.mult)
                ts("mxn", "mxn", MIN_NORM, None, ALU.max)
                by_scalar(10)
                rec("mxn", "mxn")
                tt("e", "e", "mxn", ALU.mult)
                tt("e", "e", "al", ALU.mult)
                tt("xn", "e", "sr", ALU.mult)
                ts("xn", "xn", MIN_NORM, None, ALU.max)
                rec("xn", "xn")
                ts("xn", "xn", 1.0 - BALL_EPS, 1.0, ALU.mult, ALU.min)
                tt("e", "e", "xn", ALU.mult)
                for w in range(W):
                    V.scalar_tensor_tensor(k.xs[:, w, 0:D], k.agg[:, w, 0:D], S["e"][:, w:w + 1], k.xs[:, w, 0:D], ALU.mult, ALU.add).then_inc(combined, 1)
                    dve.wait_ge(combined, 3 * W + w + 1)
                    last = V.bn_stats(k.stats[:, w, :], k.xs[:, w, 0:D])
                link(last)
                link(V.memset(k.agg[:, :, :], 0.0))

            @block.tensor
            def _(pe):
                for w in range(W):
                    b = w % 2
                    pe.wait_ge(u_in, w + 1)
                    wait(pe, uT_in, w - 1)
                    for c in range(DC):
                        last = nc.tensor.transpose(turn[b][:, c * P:(c + 1) * P], k.agg[:, w, c * P:(c + 1) * P], k.ident[:, :])
                    last.then_inc(turned, 1)
                    pe.wait_ge(uT_in, w + 1)
                    wait(pe, mx_in, w - 1)
                    for c in range(DC):
                        last = nc.tensor.matmul(prod[b][:, 0:D], uT[:, b, c * P:(c + 1) * P], k.w2l[:, c, :], start=(c == 0), stop=(c == DC - 1))
                    last.then_inc(multiplied, 1)

            @block.scalar
            def _(act):
                function = nc.scalar.activation

                def square_sum(w, row, name):
                    return function(junk[:, w % 2, :], row, ACT.Square, accum_out=S[name][:, w:w + 1])

                for w in range(W):
                    act.wait_ge(combined, w + 1)
                    wait(act, s2_in, w - 1)
                    square_sum(w, k.agg[:, w, 0:D], "s2").then_inc(s2_in, 1)
                act.wait_ge(args_ready, 1)
                function(v("un"), v("s2"), ACT.Sqrt).then_inc(function_in, 1)
                act.wait_ge(args_ready, 2)
                function(v("q"), v("r"), ACT.Tanh, scale=0.5).then_inc(function_in, 1)
                for w in range(W):
                    act.wait_ge(u_in, w + 1)
                    act.wait_ge(mx_in, w) if w else act.wait_ge(s2_in, W)
                    square_sum(w, k.agg[:, w, 0:D], "xn2").then_inc(xn2_in, 1)
                    act.wait_ge(turned, w + 1)
                    wait(act, multiplied, w - 1)
                    function(uT[:, w % 2, :], turn[w % 2][:, :], ACT.Copy).then_inc(uT_in, 1)
                    act.wait_ge(multiplied, w + 1)
                    function(mx[:, w, :], prod[w % 2][:, 0:D], ACT.Copy)
                    act.wait_ge(xn2_in, w + 1)
                    square_sum(w, prod[w % 2][:, 0:D], "mxn2").then_inc(mx_in, 1)
                act.wait_ge(args_ready, 3)
                function(bs["n"][:, :], bs["n2"][:, :], ACT.Sqrt).then_inc(function_in, 1)
                act.wait_ge(args_ready, 4)
                function(bs["t"][:, :], bs["n"][:, :], ACT.Tanh).then_inc(function_in, 1)
                act.wait_ge(args_ready, 5)
                function(v("xn"), v("xn2"), ACT.Sqrt)
                function(v("mxn"), v("mxn2"), ACT.Sqrt).then_inc(function_in, 1)
                act.wait_ge(args_ready, 6)
                function(v("la"), v("z"), ACT.Ln, bias=1.0, scale=1.0)
                function(v("lb"), v("z"), ACT.Ln, bias=1.0, scale=-1.0).then_inc(function_in, 1)
                act.wait_ge(args_ready, 7)
                function(v("f"), v("f"), ACT.Tanh, scale=0.5).then_inc(function_in, 1)
                for w in range(W):
                    act.wait_ge(h_in, w + 1)
                    wait(act, hn2_in, w - 1)
                    square_sum(w, mx[:, w, :], "hn2").then_inc(hn2_in, 1)
                    function(k.agg[:, w, 0:D], mx[:, w, :], ACT.Relu).then_inc(relu_in, 1)
                for w in range(W):
                    act.wait_ge(relu_in, w + 1)
                    wait(act, r2_in, w - 1) if w else act.wait_ge(hn2_in, W)
                    square_sum(w, k.agg[:, w, 0:D], "r2").then_inc(r2_in, 1)
                act.wait_ge(args_ready, 8)
                function(v("xn"), v("hn2"), ACT.Sqrt)
                function(v("sr"), v("r2"), ACT.Sqrt).then_inc(function_in, 1)
                act.wait_ge(args_ready, 9)
                function(v("la"), v("z"), ACT.Ln, bias=1.0, scale=1.0)
                function(v("lb"), v("z"), ACT.Ln, bias=1.0, scale=-1.0).then_inc(function_in, 1)
                act.wait_ge(args_ready, 10)
                function(v("e"), v("mxn"), ACT.Tanh).then_inc(function_in, 1)
    layernorm(nc, k, sem, "n2", k.w13, k.b13, 2 * D, k.p_table)


def edges_gate(nc, k, sb, ps, sem):
    ctx = ExitStack()
    with ctx:
        def tmp(name, shape, dt=FP32):
            return ctx.enter_context(nc.sbuf_tensor(name, shape, dt))
        rows = tmp("l3_rows", [P, R, G, 2 * D])
        attr = tmp("l3_attr", [P, R, G, P])
        stack = tmp("l3_stack", [P, 2, G, P], FP32R)
        hot = tmp("l3_hot", [P, R, G, P], FP32R)
        hidT = tmp("l3_hidT", [P, 2, DC, G, P])
        gsum = tmp("l3_gsum", [P, 2, G, D])
        gate = tmp("l3_gate", [P, 2, G, D])
        msg = tmp("l3_msg", [P, 2, G, D])
        high = tmp("l3_high", [P, 2, G, D], FP32R)
        low = tmp("l3_low", [P, 2, G, D], FP32R)
        bias_hl = tmp("l3_bias", [P, G, D], FP32R)
        w_high = tmp("l3_w_high", [P, 2 * D], FP32R)
        w_low = tmp("l3_w_low", [P, 2 * D], FP32R)
        idx = tmp("l3_idx", [P, R, G], I32)
        split_bias(nc, k, "l3", sem, k.b2, bias_hl, G)
        w_split = sem("l3_w_split")
        with nc.Block() as block:
            @block.scalar
            def _(act):
                nc.scalar.activation(w_high[:, :], k.we3[:, :], ACT.Copy).then_inc(w_split, 1)

            @block.vector
            def _(dve):
                dve.wait_ge(w_split, 1)
                nc.vector.tensor_tensor(w_low[:, :], k.we3[:, :], w_high[:, :].bitcast(FP32), ALU.subtract)
        p_hid, p_gate, p_core = (
            [ctx.enter_context(nc.psum_tensor(f"l3_{n}{j}", [P, G, D], FP32)) for j in range(2)] for n in ("p_hid", "p_gate", "p_core"))
        seg = [ctx.enter_context(nc.psum_tensor(f"l3_seg{j}", [P, 512], FP32)) for j in range(2)]
        gathered = [sem(f"l3_gathered{j}") for j in range(R)]
        attr_in = [sem(f"l3_attr_in{j}") for j in range(R)]
        (idx_set, issued, stack_high, stacked, hot_ready, hid_made, gate_made, hid_in, gsum_in, gate_in, core_made, msg_ready, high_in,
         low_in, summed, added) = (sem("l3_" + n) for n in (
             "idx_set", "issued", "stack_high", "stacked", "hot_ready", "hid_made", "gate_made", "hid_in", "gsum_in", "gate_in",
             "core_made", "msg_ready", "high_in", "low_in", "summed", "added"))
        with nc.Block() as block:
            @block.sync
            def _(sp):
                def load(u, j):
                    wait(sp, stacked, u + 1 - R)
                    t = sp.value_load(k.tile_row[0:1, bass.DynSlice(u * G, 1)], min_val=0, max_val=T - G)
                    for half in range(2):
                        sp.dma_start(attr[half * DE3:(half + 1) * DE3, j, :, :], k.ea3[bass.DynSlice(t, G), :, :].rearrange("g p e -> p g e")
                                     ).then_inc(attr_in[j], 16)

                for u, i, j in pairs(sp):
                    load(u, j)
                load(PAIRS, 0)

            @block.gpsimd
            def _(pool):
                for u, i, j in pairs(pool):
                    gather_pair(nc, pool, u, j, idx, idx_set, issued, rows, k.p_table, gathered)

            @block.scalar
            def _(act):
                AHEAD = 3
                F = nc.scalar.activation

                def indices(u, j):
                    wait(act, hid_made, u + 1 - R)
                    wait(act, gsum_in, u + 1 - R)
                    set_indices(nc, k, idx, u, j, idx_set)

                def stack_up(u, i, j):
                    act.wait_ge(attr_in[j], i * 32 + 32)
                    wait(act, gate_made, u - 1)
                    F(stack[:, j % 2, :, :], attr[:, j, :, :], ACT.Copy).then_inc(stack_high, 1)

                def split_high(u, b):
                    act.wait_ge(msg_ready, u + 1)
                    wait(act, summed, u - 1)
                    F(high[:, b, :, :], msg[:, b, :, :], ACT.Copy).then_inc(high_in, 1)

                for u in range(AHEAD):
                    indices(u, u)
                stack_up(0, 0, 0)
                for u, i, j in pairs(act):
                    b = j % 2
                    stack_up(u + 1, i + (j + 1) // R, (j + 1) % R)
                    act.wait_ge(hid_made, u + 1)
                    wait(act, core_made, u - 1)
                    F(hidT[:, b, :, :, :], p_hid[b][:, :, :].rearrange("p c (g e) -> p c g e", e=P), ACT.Relu).then_inc(hid_in, 1)
                    indices(u + AHEAD, (j + AHEAD) % R)
                    act.wait_ge(gsum_in, u + 1)
                    wait(act, msg_ready, u - 1)
                    F(gate[:, b, :, :], gsum[:, b, :, :], ACT.Sigmoid).then_inc(gate_in, 1)
                    if reached(u, 1):
                        split_high(u - 1, 1 - b)
                split_high(PAIRS - 1, (PAIRS - 1) % 2)

            @block.vector
            def _(dve):
                V = nc.vector

                def stack_low(u, j):
                    dve.wait_ge(stack_high, u + 1)
                    V.tensor_tensor(stack[DE3:P, j % 2, :, :], attr[DE3:P, j, :, :], stack[DE3:P, j % 2, :, :].bitcast(FP32), ALU.subtract
                                    ).then_inc(stacked, 1)

                def message(u, b):
                    dve.wait_ge(core_made, u + 1)
                    dve.wait_ge(gate_in, u + 1)
                    wait(dve, low_in, u - 1)
                    V.tensor_tensor(msg[:, b, :, :], p_core[b][:, :, :], gate[:, b, :, :], ALU.mult).then_inc(msg_ready, 1)

                def split_low(u, b):
                    dve.wait_ge(high_in, u + 1)
                    wait(dve, summed, u - 1)
                    V.tensor_tensor(low[:, b, :, :], msg[:, b, :, :], high[:, b, :, :].bitcast(FP32), ALU.subtract).then_inc(low_in, 1)

                stack_low(0, 0)
                for u, i, j in pairs(dve):
                    b = j % 2
                    stack_low(u + 1, (j + 1) % R)
                    if reached(u, 2):
                        split_low(u - 2, b)
                    wait(dve, summed, u + 1 - R)
                    one_hots(nc, k, u, j, hot, hot_ready)
                    dve.wait_ge(gate_made, u + 1)
                    wait(dve, gate_in, u - 1)
                    V.tensor_tensor(gsum[:, b, :, :], p_gate[b][:, :, :], rows[:, j, :, D:2 * D], ALU.add).then_inc(gsum_in, 1)
                    if reached(u, 1):
                        message(u - 1, 1 - b)
                    if reached(u, 3):
                        accumulate(nc, k, dve, u - 3, seg[1 - b], D, summed, added)
                message(PAIRS - 1, 1)
                split_low(PAIRS - 2, 0)
                split_low(PAIRS - 1, 1)
                for u in range(PAIRS - 3, PAIRS):
                    accumulate(nc, k, dve, u, seg[u % 2], D, summed, added)

            @block.tensor
            def _(pe):
                mm = nc.tensor.matmul

                def hidden(u, i, j):
                    b = j % 2
                    pe.wait_ge(gathered[j], i * 16 * G + 16 * G)
                    pe.wait_ge(stacked, u + 1)
                    wait(pe, hid_in, u - 1)
                    for c in range(DC):
                        f = slice(c * P, (c + 1) * P)
                        for e in range(G):
                            mm(p_hid[b][:, c, e * P:(e + 1) * P], rows[:, j, e, f], k.ident[:, :], is_transpose=True, start=(e == 0), stop=False)
                        for part in (w_high, w_low):
                            last = mm(p_hid[b][:, c, :], part[:, f], stack[:, b, :, :], start=False, stop=(part is w_low))
                    last.then_inc(hid_made, 1)

                def gates(u, j):
                    b = j % 2
                    wait(pe, gsum_in, u - 1)
                    for e in range(G):
                        for part in (w_high, w_low):
                            last = mm(p_gate[b][:, e, :], stack[:, b, e, :], part[:, D:2 * D], start=(part is w_high), stop=(part is w_low))
                    last.then_inc(gate_made, 1)

                def times_w2(u, b):
                    pe.wait_ge(hid_in, u + 1)
                    wait(pe, msg_ready, u - 1)
                    mm(p_core[b][:, :, :], k.ones_r[:, :], bias_hl[:, :, :], start=True, stop=False)
                    for e in range(G):
                        for c in range(DC):
                            last = mm(p_core[b][:, e, :], hidT[:, b, c, e, :], k.w2[:, c, :], start=False, stop=(e == G - 1 and c == DC - 1))
                    last.then_inc(core_made, 1)

                def segment(u, j):
                    b = j % 2
                    pe.wait_ge(hot_ready, u + 1)
                    pe.wait_ge(high_in, u + 1)
                    pe.wait_ge(low_in, u + 1)
                    wait(pe, added, u - 1)
                    for e in range(G):
                        for n, part in enumerate((high, low)):
                            last = mm(seg[b][:, 0:D], hot[:, j, e, :], part[:, b, e, :], start=(e == 0 and n == 0), stop=(e == G - 1 and n == 1))
                    last.then_inc(summed, 1)

                for u, i, j in pairs(pe):
                    hidden(u, i, j)
                    gates(u, j)
                    if reached(u, 1):
                        times_w2(u - 1, (j - 1) % 2)
                    if reached(u, 2):
                        segment(u - 2, (j - 2) % R)
                times_w2(PAIRS - 1, 1)
                segment(PAIRS - 2, R - 2)
                segment(PAIRS - 1, R - 1)


def nodes_gate(nc, k, sb, ps, sem):
    ctx = ExitStack()
    with ctx:
        mv = ctx.enter_context(nc.sbuf_tensor("n3a_mv", [P, W, 2], FP32))
        rstd = ctx.enter_context(nc.sbuf_tensor("n3a_rstd", [P, W], FP32))
        ch, var_in, root_in = (sem("n3_" + n) for n in ("ch", "var_in", "root_in"))
        with nc.Block() as block:
            @block.scalar
            def _(act):
                act.wait_ge(var_in, 1)
                nc.scalar.activation(rstd[:, :], rstd[:, :], ACT.Sqrt).then_inc(root_in, 1)

            @block.vector
            def _(dve):
                V = nc.vector
                link = Chain(dve, ch)
                for w in link.loop(W, 1):
                    link(V.tensor_tensor(at(k.agg, w, D), at(k.agg, w, D), at(k.xs, w, D), ALU.add))
                    V.bn_stats(at(k.stats, w), at(k.agg, w, D))
                link(V.memset(rstd[:, :], LN_EPS))
                for w in range(W):
                    last = V.bn_aggr(mv[:, w, :], k.stats[:, w, :])
                link(last)
                V.tensor_tensor(rstd[:, :], mv[:, :, 1], rstd[:, :], ALU.add).then_inc(var_in, 1)
                dve.wait_ge(root_in, 1)
                link(V.reciprocal(rstd[:, :], rstd[:, :]))
                for w in link.loop(W, 4):
                    link(V.tensor_scalar(at(k.agg, w, D), at(k.agg, w, D), mv[:, bass.DynSlice(w, 1), 0], col(rstd, w), ALU.subtract, ALU.mult))
                    link(V.tensor_tensor(at(k.agg, w, D), at(k.agg, w, D), k.gamma[:, :], ALU.mult))
                    link(V.tensor_tensor(at(k.agg, w, D), at(k.agg, w, D), k.beta[:, :], ALU.add))
                    link(V.tensor_tensor(at(k.xs, w, D), at(k.xs, w, D), at(k.agg, w, D), ALU.add))
                    V.bn_stats(at(k.stats, w), at(k.xs, w, D))
    layernorm(nc, k, sem, "n3", None, None, 0, None)


def finish(nc, k, sem, src):
    out_stored = sem("out_stored")
    with nc.Block() as block:
        @block.sync
        def _(sp):
            sp.dma_start(k.out[0:(W - 1) * P, :].rearrange("(w p) f -> p w f", p=P), src[:, 0:W - 1, 0:D]).then_inc(out_stored, 16)
            sp.dma_start(k.out[(W - 1) * P:N, :], src[0:TAIL, W - 1, 0:D]).then_inc(out_stored, 16)
            sp.wait_ge(out_stored, 32)


def gnn_kernel(nc, args, out):
    k = Parts(args, out)
    ctx = ExitStack()
    with ctx:
        def sb(name, shape, dt):
            return ctx.enter_context(nc.sbuf_tensor(name, shape, dt))

        def ps(name, shape, dt):
            return ctx.enter_context(nc.psum_tensor(name, shape, dt))

        live = []

        def sem(name):
            live.append(nc.alloc_semaphore(name))
            return live[-1]

        def phase(build, *more):
            build(nc, k, *more)
            nc.clear_and_free_semaphores(live)
            nc.all_engine_barrier()
            live.clear()
        k.h = nc.dram_tensor("h_table", (W * P, D), FP32).ap()
        k.x2_table = nc.dram_tensor("x2_table", (W * P, AW), FP32).ap()
        k.p_table = nc.dram_tensor("p_table", (W * P, 2 * D), FP32).ap()
        phase(setup, sb, ps, sem)
        phase(edges_mean, sb, ps, sem)
        phase(nodes_mean, sb, ps, sem)
        phase(edges_spline, sb, ps, sem)
        phase(nodes_spline, sb, ps, sem)
        phase(norms, sem)
        phase(edges_ball, sb, ps, sem)
        phase(nodes_ball, sb, ps, sem)
        phase(edges_gate, sb, ps, sem)
        phase(nodes_gate, sb, ps, sem)
        phase(finish, sem, k.xs)


def kernel(x, src, dst, edge_attr_384, edge_attr_64, edge_weight, L0_gnn_W_l, L0_gnn_W_r, L0_gnn_b_r, L1_gnn_W_edge,
           L1_gnn_b_edge, L1_gnn_W_node, L1_gnn_b_node, L1_gnn_base_weight, L1_gnn_spline_weight, L1_gnn_spline_scaler,
           L2_gnn_weight, L2_gnn_bias, L3_gnn_W1, L3_gnn_b1, L3_gnn_W2, L3_gnn_b2, L3_gnn_Wg, L3_gnn_bg, L3_gnn_gamma,
           L3_gnn_beta):
    import numpy as np
    import concourse.bacc as bacc
    from concourse.bass_utils import run_bass_kernel_spmd

    ins = {
        "x": x, "src": src, "dst": dst, "edge_weight": edge_weight,
        "wl_t": np.asarray(L0_gnn_W_l).T, "wr_t": np.asarray(L0_gnn_W_r).T, "b_r": L0_gnn_b_r,
        "wn_t": np.asarray(L1_gnn_W_node).T, "b_node": L1_gnn_b_node, "we_t": np.asarray(L1_gnn_W_edge).T, "b_edge": L1_gnn_b_edge,
        "ea1": np.asarray(edge_attr_384).reshape(T, P, KC1, P).transpose(0, 3, 2, 1),
        "base_t": np.asarray(L1_gnn_base_weight).T, "scaler_t": np.asarray(L1_gnn_spline_scaler).T,
        "spline_t": np.asarray(L1_gnn_spline_weight).transpose(2, 1, 0),
        "w2l_t": np.asarray(L2_gnn_weight).T, "l2_bias": L2_gnn_bias,
        "ea3": np.asarray(edge_attr_64).reshape(T, P, DE3).transpose(0, 2, 1),
        "w1": L3_gnn_W1, "b1": L3_gnn_b1, "w2_in": L3_gnn_W2, "b2_in": L3_gnn_b2, "wg": L3_gnn_Wg, "bg": L3_gnn_bg,
        "gamma_in": L3_gnn_gamma, "beta_in": L3_gnn_beta,
    }
    nc = bacc.Bacc("TRN2", target_bir_lowering=False, num_devices=1)
    arrays, args = {}, {}
    for name, a in ins.items():
        a = np.ascontiguousarray(a)
        arrays[f"in_{name}"] = a
        args[name] = nc.dram_tensor(f"in_{name}", a.shape, mybir.dt.from_np(a.dtype), kind="ExternalInput").ap()
    out = nc.dram_tensor("out_0", (N, D), FP32, kind="ExternalOutput").ap()
    gnn_kernel(nc, args, out)
    r = run_bass_kernel_spmd(nc, [arrays], core_ids=[0])
    return r.results[0]["out_0"]
```

```python
from contextlib import ExitStack

import concourse.bass as bass
from concourse import mybir

FP32 = mybir.dt.float32
FP32R = mybir.dt.float32r
I32 = mybir.dt.int32
ALU = mybir.AluOpType
ACT = mybir.ActivationFunctionType

P = 128
N = 2500
E = 80000
D = 256
DC = D // P
DE1 = 384
KC1 = DE1 // P
DE3 = 64
W = -(-N // P)
TAIL = N - (W - 1) * P
T = E // P
G = 2
NG = -(-T // G)
PAIRS = NG + W - 1
R = 4
HB = 4
NH = 4
RB = NH * HB
BALL_PAIRS = -(-PAIRS // RB) * RB
assert PAIRS % R == 0
SC = -(-BALL_PAIRS * G // P)
SP_ = SC * P
WORD = 16
WBITS = (W - 1).bit_length()
WPAIRS = SP_ // G - WORD + 1
assert WBITS + WORD - 1 <= 24 and WORD % R == 0 and RB % WORD == 0 and WPAIRS >= BALL_PAIRS
AW = D + 1
LN_EPS = 1e-5
INPUTS = ("x", "src", "dst", "edge_weight", "wl_t", "wr_t", "b_r", "wn_t", "b_node", "we_t", "b_edge", "ea1", "base_t", "scaler_t",
          "spline_t", "w2l_t", "l2_bias", "ea3", "w1", "b1", "w2_in", "b2_in", "wg", "bg", "gamma_in", "beta_in")
NB = 7


def rounds(eng, n):
    yield 0
    with eng.Fori(1, n) as i:
        yield i


def wait(eng, sem, value):
    if not isinstance(value, int) or value > 0:
        eng.wait_ge(sem, value)


class Chain:

    def __init__(self, eng, sem):
        self.eng, self.sem, self.n, self.r = eng, sem, 0, 0

    def __call__(self, ins):
        self.count(ins)
        self.wait(0)

    def count(self, ins):
        ins.then_inc(self.sem, 1)
        self.n += 1

    def wait(self, behind):
        self.eng.wait_ge(self.sem, self.r + self.n - behind)

    def loop(self, count, per):
        base = self.n
        with self.eng.Fori(0, count) as i:
            self.r, self.n = i * per + base, 0
            yield i
            assert self.n == per, self.n
        self.r, self.n = 0, base + count * per


class Parts:

    def __init__(self, args, out):
        (self.x, self.src, self.dst, self.edge_weight, self.wl_t, self.wr_t, self.b_r, self.wn_t, self.b_node, self.we_t,
         self.b_edge, self.ea1, self.base_t, self.scaler_t, self.spline_t, self.w2l_t, self.l2_bias, self.ea3, self.w1, self.b1,
         self.w2_in, self.b2_in, self.wg, self.bg, self.gamma_in, self.beta_in) = (args[name] for name in INPUTS)
        self.out = out


def at(t, i, width=None):
    cols = slice(None) if width is None else slice(0, width)
    if isinstance(i, int):
        return t[:, i, cols]
    return t[:, bass.DynSlice(i, 1), cols].rearrange("p o f -> p (o f)")


def col(t, i):
    return t[:, bass.DynSlice(i, 1)]


def setup(nc, k, sb, early, sem):
    k.iota = sb("iota", [P, P], FP32)
    k.ident = sb("ident", [P, P], FP32)
    k.ones = sb("ones", [P, P], FP32)
    k.xs = sb("xs", [P, W, AW], FP32)
    k.stats = sb("stats", [P, W, 6], FP32)
    k.agg = sb("agg", [P, W, AW], FP32)
    k.src_t = sb("src_t", [P, SP_], I32)
    k.rel_t = sb("rel_t", [P, SP_], FP32)
    k.ew_t = sb("ew_t", [P, SP_], FP32)
    k.tile_row = sb("tile_row", [1, SP_], I32)
    k.win_row = sb("win_row", [1, WPAIRS], I32)
    k.w2l, k.w2 = (sb(n, [P, DC, D], FP32) for n in ("w2l", "w2"))
    k.ones_r = sb("ones_r", [P, P], FP32R)
    k.w13 = sb("w13", [P, DC, 2 * D], FP32)
    k.we3 = sb("we3", [P, 2 * D], FP32)
    k.br, k.bn, k.be, k.bias2, k.b2, k.gamma, k.beta = (
        sb(n, [P, D], FP32) for n in ("br", "bn", "be", "bias2", "b2b", "gamma", "beta"))
    k.b13 = sb("b13", [P, 2 * D], FP32)
    k.wl, k.wr, k.wn, k.wbase, k.scaler = (early(n, [P, DC, D], FP32) for n in ("wl", "wr", "wn", "wbase", "scaler"))
    k.we = early("we", [P, KC1, D], FP32)
    k.wsp = early("wsp", [P, NB, DC, D], FP32)
    weights = [(k.wl, k.wl_t), (k.wr, k.wr_t), (k.wn, k.wn_t), (k.we, k.we_t), (k.wbase, k.base_t), (k.scaler, k.scaler_t),
               (k.w2l, k.w2l_t), (k.w2, k.w2_in), (k.w13[:, :, 0:D], k.w1[0:D, :]), (k.w13[:, :, D:2 * D], k.wg[0:D, :])]
    biases = [(k.br[:, :], k.b_r), (k.bn[:, :], k.b_node), (k.be[:, :], k.b_edge), (k.bias2[:, :], k.l2_bias), (k.b2[:, :], k.b2_in),
              (k.gamma[:, :], k.gamma_in), (k.beta[:, :], k.beta_in), (k.b13[:, 0:D], k.b1), (k.b13[:, D:2 * D], k.bg)]

    QT = -(-(NG - 1) // P)
    TP = (NG - 1) // QT
    assert TP * QT == NG - 1
    ctx = ExitStack()
    def tmp(name, shape, dt):
        return ctx.enter_context(nc.sbuf_tensor(name, shape, dt))
    with ctx:
        dst_tiles = tmp("dst_tiles", [TP, QT, G * P], I32)
        last_win = tmp("last_win", [TP, QT], I32)
        last_pos = tmp("last_pos", [TP, QT], FP32)
        tile_id = tmp("tile_id", [TP, QT], FP32)
        step_row = tmp("step_row", [P, SP_], FP32)
        col_id = tmp("col_id", [P, SC], I32)
        pair_i = tmp("pair_i", [P, SC], I32)
        id_f = tmp("id_f", [P, SC], FP32)
        pair_f = tmp("pair_f", [P, SC], FP32)
        first = tmp("first", [P, SC], FP32)
        bad = tmp("bad", [P, SC], FP32)
        part = tmp("part", [P, 1], FP32)
        passed = tmp("passed", [TP, QT, SP_], FP32)
        tile_f = tmp("tile_f", [1, SP_], FP32)
        win_f = tmp("win_f", [1, SP_], FP32)
        word_f = tmp("word_f", [1, WPAIRS], FP32)
        moves = tmp("moves", [1, WPAIRS + WORD - 2], FP32)
        tcol_f = tmp("tcol_f", [P, SC], FP32)
        tcol = tmp("tcol", [P, SC], I32)
        wcol = tmp("wcol", [P, SC], FP32)
        dst_s = tmp("dst_s", [P, SC, P], I32)
        src_s = tmp("src_s", [P, SC, P], I32)
        ew_s = tmp("ew_s", [P, SC, P], FP32)
        conv = tmp("conv", [P, 3, SC, P], FP32)
        pcount = ctx.enter_context(nc.psum_tensor("pcount", [P, 2, 512], FP32))
        ptile = ctx.enter_context(nc.psum_tensor("ptile", [P, SC], FP32))
        ptr = ctx.enter_context(nc.psum_tensor("ptr", [P, 3, P], FP32))
        loaded = sem("setup_loaded")
        xs_zero = sem("xs_zero")
        dst_loaded = sem("dst_loaded")
        iotas = sem("iotas")
        passed_ready = sem("passed_ready")
        counted = sem("counted")
        tcol_ready = sem("tcol_ready")
        rows_in = sem("rows_in")
        conv_ready = sem("conv_ready")
        turned = sem("turned")
        taken = sem("taken")
        ch = sem("setup_chain")
        with nc.Block() as block:
            @block.sync
            def _(sp):
                sp.dma_start(dst_tiles[:, :, :], k.dst[0:(NG - 1) * G * P].rearrange("(p q e) -> p q e", q=QT, e=G * P)).then_inc(dst_loaded, 16)
                sp.dma_start(k.xs[:, 0:W - 1, 0:D], k.x[0:(W - 1) * P, :].rearrange("(w p) f -> p w f", p=P)).then_inc(loaded, 16)
                sp.wait_ge(xs_zero, 1)
                sp.dma_start(k.xs[0:TAIL, W - 1, 0:D], k.x[(W - 1) * P:N, :]).then_inc(loaded, 16)
                n = 2
                for dst, src in weights:
                    sp.dma_start(dst[:, :, :], src.rearrange("(c p) o -> p c o", p=P)).then_inc(loaded, 16)
                    n += 1
                for kk in range(NB):
                    sp.dma_start(k.wsp[:, kk, :, :], k.spline_t[kk].rearrange("(c p) o -> p c o", p=P)).then_inc(loaded, 16)
                    n += 1
                for half in range(2):
                    for cols, src in ((slice(0, D), k.w1), (slice(D, 2 * D), k.wg)):
                        sp.dma_start(k.we3[half * DE3:(half + 1) * DE3, cols], src[D:D + DE3, :]).then_inc(loaded, 16)
                        n += 1
                for dst, src in biases:
                    sp.dma_start(dst, src[None, :].broadcast_to([P, D])).then_inc(loaded, 16)
                    n += 1
                sp.wait_ge(loaded, 16 * n)

            @block.gpsimd
            def _(pool):
                nc.gpsimd.iota(k.iota[:, :], [[1, P]], base=0, channel_multiplier=0, allow_small_or_imprecise_dtypes=True).then_inc(iotas, 1)
                nc.gpsimd.iota(part[:, :], [[1, 1]], base=0, channel_multiplier=1, allow_small_or_imprecise_dtypes=True).then_inc(iotas, 1)
                nc.gpsimd.iota(tile_id[:, :], [[1, QT]], base=0, channel_multiplier=QT, allow_small_or_imprecise_dtypes=True).then_inc(iotas, 1)
                nc.gpsimd.iota(step_row[:, :], [[1, SP_ // G], [0, G]], base=0, channel_multiplier=0, allow_small_or_imprecise_dtypes=True
                               ).then_inc(iotas, 1)
                nc.gpsimd.iota(col_id[:, :], [[P, SC]], base=0, channel_multiplier=1).then_inc(iotas, 1)
                pool.wait_ge(tcol_ready, 1)
                n = 0
                for c in range(SC):
                    for rows, table in ((dst_s, k.dst), (src_s, k.src), (ew_s, k.edge_weight)):
                        nc.gpsimd.indirect_dma_start(rows[:, c, :], None, table.rearrange("(t e) -> t e", e=P),
                                                     bass.IndirectOffsetOnAxis(tcol[:, c:c + 1], 0)).then_inc(rows_in, 16)
                        n += 1
                pool.wait_ge(rows_in, 16 * n)

            @block.vector
            def _(dve):
                link = Chain(dve, ch)
                nc.vector.memset(k.xs[:, W - 1, :], 0.0).then_inc(xs_zero, 1)
                nc.vector.memset(k.ones[:, :], 1.0)
                link(nc.vector.memset(k.agg[:, :, :], 0.0))
                dve.wait_ge(iotas, 5)
                nc.vector.tensor_scalar(k.ident[:, :], k.iota[:, :], part[:, 0:1], None, ALU.is_equal)
                dve.wait_ge(dst_loaded, 16)
                link(nc.vector.tensor_scalar(last_win[:, :], dst_tiles[:, :, G * P - 1], 7, None, ALU.logical_shift_right))
                link(nc.vector.tensor_copy(last_pos[:, :], last_win[:, :]))
                link(nc.vector.tensor_tensor(last_pos[:, :], last_pos[:, :], tile_id[:, :], ALU.add))
                for q in range(QT):
                    last = nc.vector.tensor_scalar(passed[:, q, :], step_row[0:TP, :], last_pos[:, q:q + 1], None, ALU.is_gt)
                last.then_inc(passed_ready, 1)
                dve.wait_ge(counted, 1)
                link(nc.vector.tensor_scalar(pair_i[:, :], col_id[:, :], G.bit_length() - 1, None, ALU.logical_shift_right))
                link(nc.vector.tensor_copy(pair_f[:, :], pair_i[:, :]))
                link(nc.vector.tensor_copy(id_f[:, :], col_id[:, :]))
                link(nc.vector.scalar_tensor_tensor(id_f[:, :], pair_f[:, :], -float(G), id_f[:, :], ALU.mult, ALU.add))
                link(nc.vector.tensor_scalar(first[:, :], ptile[:, :], float(G), None, ALU.mult))
                link(nc.vector.scalar_tensor_tensor(tcol_f[:, :], first[:, :], float(T - G), id_f[:, :], ALU.min, ALU.add))
                nc.vector.tensor_copy(tcol[:, :], tcol_f[:, :]).then_inc(tcol_ready, 1)
                link(nc.vector.tensor_tensor(bad[:, :], tcol_f[:, :], first[:, :], ALU.is_lt))
                link(nc.vector.tensor_tensor(wcol[:, :], pair_f[:, :], ptile[:, :], ALU.subtract))
                link(nc.vector.tensor_scalar(wcol[:, :], wcol[:, :], float(P), None, ALU.mult))
                link(nc.vector.scalar_tensor_tensor(wcol[:, :], bad[:, :], float(W * P), wcol[:, :], ALU.mult, ALU.add))
                half = SP_ // 2
                for h in range(2):
                    cols = slice(h * half, (h + 1) * half)
                    nc.vector.tensor_scalar(tile_f[:, cols], pcount[0:1, h, 0:half], float(G), float(T - G), ALU.mult, ALU.min)
                    link(nc.vector.tensor_tensor(win_f[:, cols], step_row[0:1, cols], pcount[0:1, h, 0:half], ALU.subtract))
                nc.vector.tensor_copy(k.tile_row[:, :], tile_f[:, :])
                link(nc.vector.tensor_scalar(win_f[:, :], win_f[:, :], float(W - 1), None, ALU.min))
                by_pair = win_f[:, :].rearrange("p (u g) -> p u g", g=G)[:, :, 0]
                nc.vector.tensor_tensor(moves[:, :], by_pair[:, 1:WPAIRS + WORD - 1], by_pair[:, 0:WPAIRS + WORD - 2], ALU.subtract)
                link(nc.vector.tensor_copy(word_f[:, :], by_pair[:, 0:WPAIRS]))
                for n in range(WORD - 1):
                    link(nc.vector.scalar_tensor_tensor(word_f[:, :], moves[:, n:n + WPAIRS], float(2 ** (WBITS + n)), word_f[:, :],
                                                        ALU.mult, ALU.add))
                link(nc.vector.tensor_copy(k.win_row[:, :], word_f[:, :]))
                dve.wait_ge(rows_in, 16 * 3 * SC)
                for c in range(SC):
                    nc.vector.tensor_copy(conv[:, 0, c, :], src_s[:, c, :])
                    nc.vector.tensor_scalar(conv[:, 1, c, :], dst_s[:, c, :], wcol[:, c:c + 1], None, ALU.subtract)
                    nc.vector.tensor_copy(conv[:, 2, c, :], ew_s[:, c, :]).then_inc(conv_ready, 1)
                for c in range(SC):
                    cols = slice(c * P, (c + 1) * P)
                    dve.wait_ge(turned, c + 1)
                    nc.vector.tensor_copy(k.src_t[:, cols], ptr[:, 0, :])
                    nc.vector.tensor_copy(k.rel_t[:, cols], ptr[:, 1, :])
                    nc.vector.tensor_copy(k.ew_t[:, cols], ptr[:, 2, :]).then_inc(taken, 1)

            @block.tensor
            def _(pe):
                pe.wait_ge(passed_ready, 1)
                for h in range(2):
                    for q in range(QT):
                        nc.tensor.matmul(pcount[:, h, 0:SP_ // 2], k.ones[0:TP, :], passed[:, q, h * SP_ // 2:(h + 1) * SP_ // 2],
                                         start=(q == 0), stop=(q == QT - 1))
                for c in range(SC):
                    for q in range(QT):
                        last = nc.tensor.matmul(ptile[:, c:c + 1], passed[:, q, c * P:(c + 1) * P], k.ones[0:TP, 0:1],
                                                start=(q == 0), stop=(q == QT - 1))
                last.then_inc(counted, 1)
                for c in range(SC):
                    pe.wait_ge(conv_ready, c + 1)
                    if c:
                        pe.wait_ge(taken, c)
                    for t in range(3):
                        last = nc.tensor.transpose(ptr[:, t, :], conv[:, t, c, :], k.ident[:, :])
                    last.then_inc(turned, 1)


def pairs(eng, n=PAIRS, slots=R):
    for i in rounds(eng, n // slots):
        for j in range(slots):
            yield i * slots + j, i, j


def reached(u, n):
    return not isinstance(u, int) or u >= n


def table_cols(t, u):
    return t[:, bass.DynSlice(u * G, G)]


class Windows:

    def __init__(self, k, eng, lag):
        self.k, self.eng, self.lag = k, eng, lag

    def __call__(self, u, j):
        place = 0 if isinstance(u, int) else j % WORD
        if place == 0:
            self.word = self.eng.value_load(self.k.win_row[0:1, bass.DynSlice(u - self.lag, 1)], min_val=0, max_val=2 ** (WBITS + WORD - 1) - 1)
            w = self.word & (2 ** WBITS - 1)
        else:
            w = self.w + ((self.word >> (WBITS + place - 1)) & 1)
        self.w = self.eng.snap(w).with_bounds(min_val=0, max_val=W - 1)
        return self.w


def set_indices(nc, k, idx, u, j, idx_set):
    nc.scalar.activation(idx[:, j, :], table_cols(k.src_t, u), ACT.Copy).then_inc(idx_set, 1)


def gather_pair(nc, pool, u, j, idx, idx_set, issued, rows, table, gathered):
    pool.wait_ge(idx_set, u + 1)
    pool.sem_inc(issued, 1)
    for e in range(G):
        nc.gpsimd.indirect_dma_start(rows[:, j, e, :], None, table, bass.IndirectOffsetOnAxis(idx[:, j, e:e + 1], 0)
                                     ).then_inc(gathered[j], 16)


def one_hots(nc, k, u, j, hot, hot_ready):
    for e in range(G):
        last = nc.vector.tensor_scalar(hot[:, j, e, :], k.iota[:, :], col(k.rel_t, u * G + e), None, ALU.is_equal)
    last.then_inc(hot_ready, 1)


def accumulate(nc, k, dve, u, w, seg, width, summed, added):
    dve.wait_ge(summed, u + 1)
    wait(dve, added, u)
    nc.vector.tensor_tensor(at(k.agg, w, width), at(k.agg, w, width), seg[:, 0:width], ALU.add).then_inc(added, 1)


def edges_mean(nc, k, sb, ps, sem):
    LAG = 2
    ctx = ExitStack()
    with ctx:
        rows = ctx.enter_context(nc.sbuf_tensor("l0_rows", [P, R, G, AW], FP32))
        hot = ctx.enter_context(nc.sbuf_tensor("l0_hot", [P, R, G, P], FP32))
        idx = ctx.enter_context(nc.sbuf_tensor("l0_idx", [P, R, G], I32))
        seg = [ctx.enter_context(nc.psum_tensor(f"l0_seg{j}", [P, 512], FP32)) for j in range(R)]
        gathered = [sem(f"l0_gathered{j}") for j in range(R)]
        ones_set, idx_set, issued, hot_ready, summed, added = (
            sem("l0_" + n) for n in ("ones_set", "idx_set", "issued", "hot_ready", "summed", "added"))
        with nc.Block() as block:
            @block.gpsimd
            def _(pool):
                pool.wait_ge(ones_set, 1)
                for u, i, j in pairs(pool):
                    gather_pair(nc, pool, u, j, idx, idx_set, issued, rows[:, :, :, 0:D], k.x, gathered)

            @block.scalar
            def _(act):
                for u, i, j in pairs(act):
                    wait(act, summed, u + 1 - R)
                    set_indices(nc, k, idx, u, j, idx_set)

            @block.vector
            def _(dve):
                there = Windows(k, dve, LAG)
                nc.vector.memset(rows[:, :, :, D:AW], 1.0).then_inc(ones_set, 1)
                for u, i, j in pairs(dve):
                    one_hots(nc, k, u, j, hot, hot_ready)
                    if reached(u, LAG):
                        accumulate(nc, k, dve, u - LAG, there(u, j), seg[(j - LAG) % R], AW, summed, added)
                for u in range(PAIRS - LAG, PAIRS):
                    accumulate(nc, k, dve, u, there(u + LAG, 0), seg[u % R], AW, summed, added)

            @block.tensor
            def _(pe):
                for u, i, j in pairs(pe):
                    wait(pe, added, u + 1 - R)
                    pe.wait_ge(hot_ready, u + 1)
                    pe.wait_ge(gathered[j], i * 16 * G + 16 * G)
                    for e in range(G):
                        last = nc.tensor.matmul(seg[j][:, 0:AW], hot[:, j, e, :], rows[:, j, e, :], start=(e == 0), stop=(e == G - 1))
                    last.then_inc(summed, 1)


def nodes_mean(nc, k, sb, ps, sem):
    ctx = ExitStack()
    with ctx:
        def tmp(name, shape, dt=FP32):
            return ctx.enter_context(nc.sbuf_tensor(name, shape, dt))
        rc = tmp("n0_rc", [P, W])
        mean = tmp("n0_mean", [P, 2, D])
        row = tmp("n0_row", [P, 2, D])
        opT = tmp("n0_opT", [P, 2, 2 * DC, P])
        turn = [ctx.enter_context(nc.psum_tensor(f"n0_turn{b}", [P, 2 * DC, P], FP32)) for b in range(2)]
        prod = [ctx.enter_context(nc.psum_tensor(f"n0_prod{b}", [P, 512], FP32)) for b in range(2)]
        mean_ready, brought, turned, copied, multiplied, biased, xs_in, ch = (
            sem("n0_" + n) for n in ("mean_ready", "brought", "turned", "copied", "multiplied", "biased", "xs_in", "ch"))
        with nc.Block() as block:
            @block.vector
            def _(dve):
                link = Chain(dve, ch)
                V = nc.vector
                link(V.tensor_scalar(rc[:, :], k.agg[:, :, D], 1.0, None, ALU.max))
                link(V.reciprocal(rc[:, :], rc[:, :]))

                def take(w, b):
                    dve.wait_ge(biased, w + 1)
                    dve.wait_ge(multiplied, w + 1)
                    V.tensor_tensor(at(k.xs, w, D), at(k.xs, w, D), prod[b][:, 0:D], ALU.add).then_inc(xs_in, 1)
                    dve.wait_ge(xs_in, w + 1)
                    V.bn_stats(at(k.stats, w), at(k.xs, w, D))

                for i in rounds(dve, W // 2):
                    for b in range(2):
                        w = i * 2 + b
                        wait(dve, turned, w - 1)
                        V.tensor_scalar(mean[:, b, :], at(k.agg, w, D), col(rc, w), None, ALU.mult).then_inc(mean_ready, 1)
                        dve.wait_ge(brought, w + 1)
                        V.tensor_tensor(at(k.xs, w, D), at(k.xs, w, D), k.br[:, :], ALU.add).then_inc(biased, 1)
                        if not isinstance(i, int) or w >= 1:
                            take(w - 1, 1 - b)
                take(W - 1, 1)
                link(V.memset(k.agg[:, :, :], 0.0))

            @block.tensor
            def _(pe):
                def turn_rows(w, b):
                    pe.wait_ge(mean_ready, w + 1)
                    pe.wait_ge(brought, w + 1)
                    wait(pe, copied, w - 1)
                    for n, rows in enumerate((mean, row)):
                        for c in range(DC):
                            last = nc.tensor.transpose(turn[b][:, n * DC + c, :], rows[:, b, c * P:(c + 1) * P], k.ident[:, :])
                    last.then_inc(turned, 1)

                def multiply(w, b):
                    pe.wait_ge(copied, w + 1)
                    wait(pe, xs_in, w - 1)
                    for c in range(2 * DC):
                        last = nc.tensor.matmul(prod[b][:, 0:D], opT[:, b, c, :], (k.wl if c < DC else k.wr)[:, c % DC, :],
                                                start=(c == 0), stop=(c == 2 * DC - 1))
                    last.then_inc(multiplied, 1)

                turn_rows(0, 0)
                for i in rounds(pe, W // 2 - 1):
                    for b in range(2):
                        w = i * 2 + b
                        turn_rows(w + 1, 1 - b)
                        multiply(w, b)
                turn_rows(W - 1, 1)
                multiply(W - 2, 0)
                multiply(W - 1, 1)

            @block.gpsimd
            def _(pool):
                for i in rounds(pool, W // 2):
                    for b in range(2):
                        w = i * 2 + b
                        wait(pool, turned, w - 1)
                        nc.gpsimd.tensor_copy(row[:, b, :], at(k.xs, w, D)).then_inc(brought, 1)

            @block.scalar
            def _(act):
                for i in rounds(act, W // 2):
                    for b in range(2):
                        w = i * 2 + b
                        act.wait_ge(turned, w + 1)
                        wait(act, multiplied, w - 1)
                        nc.scalar.activation(opT[:, b, :, :], turn[b][:, :, :], ACT.Copy).then_inc(copied, 1)
        layernorm(nc, k, sem, "n0", k.wn, k.bn, D, k.h)


def layernorm(nc, k, sem, tag, weight, bias, width, table):
    ctx = ExitStack()
    with ctx:
        def tmp(name, shape, dt=FP32):
            return ctx.enter_context(nc.sbuf_tensor(tag + name, shape, dt))
        rstd = tmp("_rstd", [P, W])
        mv = tmp("_mv", [P, W, 2])
        ch, rooted, normed = (sem(f"{tag}_{n}") for n in ("lch", "rooted", "normed"))
        with nc.Block() as block:
            @block.scalar
            def _(act):
                act.wait_ge(ch, 2)
                nc.scalar.activation(rstd[:, :], rstd[:, :], ACT.Sqrt).then_inc(rooted, 1)

            @block.vector
            def _(dve):
                link = Chain(dve, ch)
                for w in range(W):
                    last = nc.vector.bn_aggr(mv[:, w, :], k.stats[:, w, :])
                link(last)
                link(nc.vector.tensor_scalar(rstd[:, :], mv[:, :, 1], LN_EPS, None, ALU.add))
                dve.wait_ge(rooted, 1)
                link(nc.vector.reciprocal(rstd[:, :], rstd[:, :]))
                for w in range(W):
                    nc.vector.tensor_scalar(k.xs[:, w, 0:D], k.xs[:, w, 0:D], mv[:, w, 0:1], rstd[:, w:w + 1], ALU.subtract, ALU.mult
                                            ).then_inc(normed, 1)
    if weight is not None:
        project(nc, k, sem, tag, weight, bias, width, table)


def project(nc, k, sem, tag, weight, bias, width, table):
    ctx = ExitStack()
    with ctx:
        def tmp(name, shape, dt=FP32):
            return ctx.enter_context(nc.sbuf_tensor(tag + name, shape, dt))
        opT = tmp("_lnT", [P, 2, DC, P])
        row = tmp("_lrow", [P, 2, D])
        made = tmp("_made", [P, W, width])
        turn = [ctx.enter_context(nc.psum_tensor(f"{tag}_lturn{b}", [P, DC, P], FP32)) for b in range(2)]
        prod = [ctx.enter_context(nc.psum_tensor(f"{tag}_lprod{b}", [P, 512], FP32)) for b in range(2)]
        brought, turned, copied, multiplied, added, stored = (
            sem(f"{tag}_{n}") for n in ("lbrought", "lturned", "lcopied", "lmult", "ladded", "stored"))
        with nc.Block() as block:
            @block.scalar
            def _(act):
                with act.Fori(0, W // 2) as i:
                    for b in range(2):
                        act.wait_ge(turned, i * 2 + b + 1)
                        nc.scalar.activation(opT[:, b, :, :], turn[b][:, :, :], ACT.Copy).then_inc(copied, 1)

            @block.vector
            def _(dve):
                with dve.Fori(0, W // 2) as i:
                    for b in range(2):
                        w = i * 2 + b
                        dve.wait_ge(multiplied, w + 1)
                        nc.vector.tensor_tensor(at(made, w), prod[b][:, 0:width], bias[:, 0:width], ALU.add).then_inc(added, 1)

            @block.gpsimd
            def _(pool):
                for i in rounds(pool, W // 2):
                    for b in range(2):
                        w = i * 2 + b
                        wait(pool, turned, w - 1)
                        nc.gpsimd.tensor_copy(row[:, b, :], at(k.xs, w, D)).then_inc(brought, 1)

            @block.tensor
            def _(pe):
                for i in rounds(pe, W // 2):
                    for b in range(2):
                        w = i * 2 + b
                        wait(pe, copied, w - 1)
                        pe.wait_ge(brought, w + 1)
                        for c in range(DC):
                            last = nc.tensor.transpose(turn[b][:, c, :], row[:, b, c * P:(c + 1) * P], k.ident[:, :])
                        last.then_inc(turned, 1)
                        pe.wait_ge(copied, w + 1)
                        wait(pe, added, w - 1)
                        for c in range(DC):
                            last = nc.tensor.matmul(prod[b][:, 0:width], opT[:, b, c, :], weight[:, c, :], start=(c == 0), stop=(c == DC - 1))
                        last.then_inc(multiplied, 1)

            @block.sync
            def _(sp):
                sp.wait_ge(added, W)
                sp.dma_start(table.rearrange("(w p) f -> p w f", p=P), made[:, :, :]).then_inc(stored, 16)
                sp.wait_ge(stored, 16)


def split_bias(nc, k, tag, sem, bias, bias_hl, copies):
    high = sem(tag + "_bias_high")
    done, cleared = sem(tag + "_bias_done"), sem(tag + "_bias_cleared")
    with nc.sbuf_tensor(tag + "_bias_hi", [P, D], FP32R) as hi, nc.Block() as block:
        @block.scalar
        def _(act):
            nc.scalar.activation(k.ones_r[:, :], k.ones[:, :], ACT.Copy)
            nc.scalar.activation(hi[:, :], bias[:, :], ACT.Copy).then_inc(high, 1)
            act.wait_ge(cleared, 1)
            for g in range(copies):
                last = nc.scalar.activation(bias_hl[0:1, g, :], bias[0:1, :], ACT.Copy)
            last.then_inc(done, 1)

        @block.vector
        def _(dve):
            nc.vector.memset(bias_hl[:, :, :].bitcast(FP32), 0.0).then_inc(cleared, 1)
            dve.wait_ge(high, 1)
            dve.wait_ge(cleared, 1)
            for g in range(copies):
                last = nc.vector.tensor_tensor(bias_hl[32:33, g, :], bias[32:33, :], hi[32:33, :].bitcast(FP32), ALU.subtract)
            last.then_inc(done, 1)


def edges_spline(nc, k, sb, ps, sem):
    ctx = ExitStack()
    with ctx:
        def tmp(name, shape, dt=FP32):
            return ctx.enter_context(nc.sbuf_tensor(name, shape, dt))
        rows = tmp("l1_rows", [P, R, G, D])
        attr = tmp("l1_attr", [P, R, G, KC1, P])
        hot = tmp("l1_hot", [P, R, G, P], FP32R)
        msg = tmp("l1_msg", [P, R, G, D])
        high = tmp("l1_high", [P, 2, G, D], FP32R)
        low = tmp("l1_low", [P, 2, G, D], FP32R)
        bias = tmp("l1_bias", [P, G, D])
        edge = tmp("l1_edge", [P, 2, G, D])
        idx = tmp("l1_idx", [P, R, G], I32)
        prod = [ctx.enter_context(nc.psum_tensor(f"l1_prod{j}", [P, G, D], FP32)) for j in range(R)]
        seg = [ctx.enter_context(nc.psum_tensor(f"l1_seg{j}", [P, 512], FP32)) for j in range(2)]
        gathered = [sem(f"l1_gathered{j}") for j in range(R)]
        attr_in = [sem(f"l1_attr_in{j}") for j in range(R)]
        bias_set, idx_set, issued, hot_ready, multiplied, edge_in, msg_ready, high_in, low_in, summed, added = (
            sem("l1_" + n) for n in ("bias_set", "idx_set", "issued", "hot_ready", "multiplied", "edge_in", "msg_ready", "high_in", "low_in", "summed", "added"))
        with nc.Block() as block:
            @block.sync
            def _(sp):
                for u, i, j in pairs(sp):
                    wait(sp, multiplied, u + 1 - R)
                    t = sp.value_load(k.tile_row[0:1, bass.DynSlice(u * G, 1)], min_val=0, max_val=T - G)
                    sp.dma_start(attr[:, j, :, :, :], k.ea1[bass.DynSlice(t, G), :, :, :].rearrange("g p c e -> p g c e")
                                 ).then_inc(attr_in[j], 16)

            @block.gpsimd
            def _(pool):
                for u, i, j in pairs(pool):
                    gather_pair(nc, pool, u, j, idx, idx_set, issued, rows, k.h, gathered)

            @block.scalar
            def _(act):
                AHEAD = 2

                def split_high(u, j):
                    act.wait_ge(msg_ready, u + 1)
                    wait(act, summed, u - 1)
                    nc.scalar.activation(high[:, j % 2, :, :], msg[:, j, :, :], ACT.Copy).then_inc(high_in, 1)

                for u, i, j in pairs(act):
                    wait(act, msg_ready, u + 1 - R)
                    set_indices(nc, k, idx, u, j, idx_set)
                    if reached(u, AHEAD):
                        split_high(u - AHEAD, (j - AHEAD) % R)
                for u in range(PAIRS - AHEAD, PAIRS):
                    split_high(u, u % R)

            @block.vector
            def _(dve):
                there = Windows(k, dve, 3)

                for e in range(G):
                    last = nc.vector.tensor_copy(bias[:, e, :], k.be[:, :])
                last.then_inc(bias_set, 1)
                dve.wait_ge(bias_set, 1)

                def biased(u, j):
                    dve.wait_ge(multiplied, u + 1)
                    nc.vector.tensor_tensor(edge[:, j % 2, :, :], prod[j][:, :, :], bias[:, :, :], ALU.add).then_inc(edge_in, 1)

                def message(u, i, j):
                    dve.wait_ge(edge_in, u + 1)
                    dve.wait_ge(gathered[j], i * 16 * G + 16 * G)
                    nc.vector.tensor_tensor(msg[:, j, :, :], edge[:, j % 2, :, :], rows[:, j, :, :], ALU.mult).then_inc(msg_ready, 1)

                def split_low(u, j):
                    dve.wait_ge(high_in, u + 1)
                    wait(dve, summed, u - 1)
                    dve.wait_ge(msg_ready, u + 1)
                    nc.vector.tensor_tensor(low[:, j % 2, :, :], msg[:, j, :, :], high[:, j % 2, :, :].bitcast(FP32), ALU.subtract
                                            ).then_inc(low_in, 1)

                for u, i, j in pairs(dve):
                    biased(u, j)
                    one_hots(nc, k, u, j, hot, hot_ready)
                    message(u, i, j)
                    if reached(u, 1):
                        split_low(u - 1, (j - 1) % R)
                    if reached(u, 3):
                        accumulate(nc, k, dve, u - 3, there(u, j), seg[(j - 3) % 2], D, summed, added)
                split_low(PAIRS - 1, R - 1)
                for u in range(PAIRS - 3, PAIRS):
                    accumulate(nc, k, dve, u, there(u + 3, 0), seg[u % 2], D, summed, added)

            @block.tensor
            def _(pe):
                mm = nc.tensor.matmul

                def products(u, i, j):
                    pe.wait_ge(attr_in[j], i * 16 + 16)
                    wait(pe, edge_in, u + 1 - R)
                    for e in range(G):
                        for c in range(KC1):
                            last = mm(prod[j][:, e, :], attr[:, j, e, c, :], k.we[:, c, :], start=(c == 0), stop=(c == KC1 - 1))
                    last.then_inc(multiplied, 1)

                def segment(u, j):
                    pe.wait_ge(low_in, u + 1)
                    pe.wait_ge(high_in, u + 1)
                    pe.wait_ge(hot_ready, u + 1)
                    wait(pe, added, u - 1)
                    for e in range(G):
                        for n, part in enumerate((high, low)):
                            last = mm(seg[j % 2][:, 0:D], hot[:, j, e, :], part[:, j % 2, e, :], start=(e == 0 and n == 0), stop=(e == G - 1 and n == 1))
                    last.then_inc(summed, 1)

                for u, i, j in pairs(pe):
                    products(u, i, j)
                    if reached(u, 2):
                        segment(u - 2, (j - 2) % R)
                segment(PAIRS - 2, R - 2)
                segment(PAIRS - 1, R - 1)


def nodes_spline(nc, k, sb, ps, sem):
    ctx = ExitStack()
    with ctx:
        def tmp(name, shape, dt=FP32):
            return ctx.enter_context(nc.sbuf_tensor(name, shape, dt))
        centre = tmp("n1_centre", [P, NB])
        row = tmp("n1_row", [P, 2, D])
        aggT = tmp("n1_aggT", [P, 2, D])
        siluT = tmp("n1_siluT", [P, 2, D])
        near = tmp("n1_near", [P, 2, NB, D])
        far = tmp("n1_far", [P, 2, NB, D])
        sq = tmp("n1_sq", [P, 2, NB, D])
        sqn = tmp("n1_sqn", [P, 2, NB, D])
        basis = tmp("n1_basis", [P, 2, NB, D])
        turn = [ctx.enter_context(nc.psum_tensor(f"n1_turn{b}", [P, D], FP32)) for b in range(2)]
        prod = [ctx.enter_context(nc.psum_tensor(f"n1_prod{b}", [P, 512], FP32)) for b in range(2)]
        (brought, turned, aggT_in, silu_in, dist_in, near_in, far_in, sq_in, near_used, cube_in, basis_in, multiplied, xs_in, centred, ch,
         scaled) = (sem("n1_" + n) for n in (
             "brought", "turned", "aggT_in", "silu_in", "dist_in", "near_in", "far_in", "sq_in", "near_used", "cube_in", "basis_in",
             "multiplied", "xs_in", "centred", "ch", "scaled"))
        with nc.Block() as block:
            @block.gpsimd
            def _(pool):
                for i in rounds(pool, W // 2):
                    for b in range(2):
                        w = i * 2 + b
                        wait(pool, turned, w - 1)
                        nc.gpsimd.tensor_copy(row[:, b, :], at(k.agg, w, D)).then_inc(brought, 1)

            @block.scalar
            def _(act):
                act.wait_ge(centred, 1)
                for i in rounds(act, W // 2):
                    for b in range(2):
                        w = i * 2 + b
                        act.wait_ge(turned, w + 1)
                        wait(act, near_used, w - 1)
                        for n in range(NB):
                            last = nc.scalar.activation(near[:, b, n, :], turn[b][:, :], ACT.Abs, bias=centre[:, n:n + 1], scale=2.0)
                        last.then_inc(dist_in, 1)
                        act.wait_ge(near_in, w + 1)
                        nc.scalar.activation(sq[:, b, :, :], far[:, b, :, :], ACT.Square)
                        nc.scalar.activation(sqn[:, b, :, :], near[:, b, :, :], ACT.Square).then_inc(sq_in, 1)
                        wait(act, multiplied, w - 1)
                        nc.scalar.activation(siluT[:, b, :], turn[b][:, :], ACT.Silu).then_inc(silu_in, 1)

            @block.vector
            def _(dve):
                link = Chain(dve, ch)
                link(nc.vector.tensor_scalar(centre[:, :], k.iota[:, 0:NB], -1.0, 3.0, ALU.mult, ALU.add))
                nc.vector.tensor_copy(centre[:, :], centre[:, :]).then_inc(centred, 1)
                for n in range(NB):
                    last = nc.vector.scalar_tensor_tensor(k.wsp[:, n, :, :], k.wsp[:, n, :, :], 1.0 / 6.0, k.scaler[:, :, :], ALU.mult, ALU.mult)
                last.then_inc(scaled, 1)

                def take(w, b):
                    dve.wait_ge(multiplied, w + 1)
                    nc.vector.tensor_tensor(at(k.xs, w, D), at(k.xs, w, D), prod[b][:, 0:D], ALU.add).then_inc(xs_in, 1)
                    dve.wait_ge(xs_in, w + 1)
                    nc.vector.bn_stats(at(k.stats, w), at(k.xs, w, D))

                def clip(w, b):
                    dve.wait_ge(dist_in, w + 1)
                    nc.vector.tensor_scalar(far[:, b, :, :], near[:, b, :, :], 2.0, 2.0, ALU.min, ALU.subtract).then_inc(far_in, 1)
                    dve.wait_ge(far_in, w + 1)
                    nc.vector.tensor_scalar(near[:, b, :, :], near[:, b, :, :], 1.0, 1.0, ALU.min, ALU.subtract).then_inc(near_in, 1)

                def combine(w, b):
                    dve.wait_ge(sq_in, w + 1)
                    nc.vector.scalar_tensor_tensor(sqn[:, b, :, :], sqn[:, b, :, :], 4.0, near[:, b, :, :], ALU.mult, ALU.mult).then_inc(near_used, 1)
                    nc.vector.tensor_tensor(sq[:, b, :, :], sq[:, b, :, :], far[:, b, :, :], ALU.mult).then_inc(cube_in, 1)
                    dve.wait_ge(cube_in, w + 1)
                    wait(dve, multiplied, w - 1)
                    nc.vector.tensor_tensor(basis[:, b, :, :], sqn[:, b, :, :], sq[:, b, :, :], ALU.subtract).then_inc(basis_in, 1)

                clip(0, 0)
                for i in rounds(dve, W // 2 - 1):
                    for b in range(2):
                        w = i * 2 + b
                        clip(w + 1, 1 - b)
                        combine(w, b)
                        if not isinstance(i, int) or w >= 1:
                            take(w - 1, 1 - b)
                clip(W - 1, 1)
                combine(W - 2, 0)
                take(W - 3, 1)
                combine(W - 1, 1)
                take(W - 2, 0)
                take(W - 1, 1)
                link(nc.vector.memset(k.agg[:, :, :], 0.0))

            @block.tensor
            def _(pe):
                pe.wait_ge(scaled, 1)

                def turn_rows(w, b):
                    pe.wait_ge(brought, w + 1)
                    wait(pe, silu_in, w - 1)
                    wait(pe, dist_in, w - 1)
                    for c in range(DC):
                        last = nc.tensor.transpose(turn[b][:, c * P:(c + 1) * P], row[:, b, c * P:(c + 1) * P], k.ident[:, :])
                    last.then_inc(turned, 1)

                def multiply(w, b):
                    pe.wait_ge(silu_in, w + 1)
                    wait(pe, xs_in, w - 1)
                    for c in range(DC):
                        nc.tensor.matmul(prod[b][:, 0:D], siluT[:, b, c * P:(c + 1) * P], k.wbase[:, c, :], start=(c == 0), stop=False)
                    pe.wait_ge(basis_in, w + 1)
                    for n in range(NB):
                        for c in range(DC):
                            last = nc.tensor.matmul(prod[b][:, 0:D], basis[:, b, n, c * P:(c + 1) * P], k.wsp[:, n, c, :],
                                                    start=False, stop=(n == NB - 1 and c == DC - 1))
                    last.then_inc(multiplied, 1)

                turn_rows(0, 0)
                turn_rows(1, 1)
                for i in rounds(pe, W // 2 - 1):
                    for b in range(2):
                        w = i * 2 + b
                        turn_rows(w + 2, b)
                        multiply(w, b)
                multiply(W - 2, 0)
                multiply(W - 1, 1)
    layernorm(nc, k, sem, "n1", None, None, 0, None)


MIN_NORM = 1e-15
BALL_EPS = 1e-5
Z_MAX = 1.0 - 1e-7
ROOT_MIN = 2.0 ** -60


class Linked:

    def __init__(self, eng, sem, per):
        self.eng, self.sem, self.per = eng, sem, per

    def start(self, h):
        self.base, self.n = h * self.per, 0

    def __call__(self, ins):
        ins.then_inc(self.sem, 1)
        self.n += 1
        assert self.n <= self.per

    def wait(self):
        self.eng.wait_ge(self.sem, self.base + self.n)


def norms(nc, k, sem):
    normed, stored = sem("x2_normed"), sem("x2_stored")
    with nc.sbuf_tensor("x2_junk", [P, 2, D], FP32) as junk, nc.Block() as block:
        @block.scalar
        def _(act):
            for w in range(W):
                wait(act, normed, w - 1)
                nc.scalar.activation(junk[:, w % 2, :], k.xs[:, w, 0:D], ACT.Square, accum_out=k.xs[:, w, D:AW]).then_inc(normed, 1)

        @block.sync
        def _(sp):
            sp.wait_ge(normed, W)
            sp.dma_start(k.x2_table.rearrange("(w p) f -> p w f", p=P), k.xs[:, :, :]).then_inc(stored, 16)
            sp.wait_ge(stored, 16)


def edges_ball(nc, k, sb, ps, sem):
    LAG = 2 * HB + 3
    ctx = ExitStack()
    with ctx:
        def tmp(name, shape, dt=FP32):
            return ctx.enter_context(nc.sbuf_tensor(name, shape, dt))
        rows = tmp("l2_rows", [P, RB, G, AW])
        hot = tmp("l2_hot", [P, RB, G, P])
        x_high = tmp("l2_x_high", [P, W, AW + 1], FP32R)
        x_low = tmp("l2_x_low", [P, W, AW + 1], FP32R)
        hotT = tmp("l2_hotT", [P, 4, G, P], FP32R)
        scaled = tmp("l2_scaled", [P, 2, G, AW])
        junk = tmp("l2_junk", [P, 2, G, D])
        apart = tmp("l2_apart", [P, 2, G, P])
        idx = tmp("l2_idx", [P, RB, G], I32)
        dot, dst2, gap, q, den, rden, prod2, root, rroot, sn, z, la, lb, g, kb, fsrc, fdst = (
            tmp("l2_" + n, [P, NH, HB, G]) for n in ("dot", "dst2", "gap", "q", "den", "rden", "prod2", "root", "rroot", "sn", "z",
                                                     "la", "lb", "g", "kb", "fsrc", "fdst"))
        x_split = sem("l2_x_split")
        with nc.Block() as block:
            @block.scalar
            def _(act):
                act.wait_ge(x_split, 1)
                for w in range(W):
                    nc.scalar.activation(x_high[:, w, 0:AW], k.xs[:, w, :], ACT.Copy).then_inc(x_split, 1)

            @block.vector
            def _(dve):
                nc.vector.memset(x_low[:, :, AW:].bitcast(FP32), 0.0)
                nc.vector.memset(x_high[:, :, AW:].bitcast(FP32), 0.0).then_inc(x_split, 1)
                for w in range(W):
                    dve.wait_ge(x_split, w + 2)
                    nc.vector.tensor_tensor(x_low[:, w, 0:AW], k.xs[:, w, :], x_high[:, w, 0:AW].bitcast(FP32), ALU.subtract)
        turn = [ctx.enter_context(nc.psum_tensor(f"l2_turn{j}", [P, G, D], FP32)) for j in range(2)]
        base = [ctx.enter_context(nc.psum_tensor(f"l2_base{j}", [P, G, 512], FP32)) for j in range(2)]
        seg = [ctx.enter_context(nc.psum_tensor(f"l2_seg{j}", [P, 512], FP32)) for j in range(2)]
        gathered = [sem(f"l2_gathered{j}") for j in range(RB)]
        (idx_set, issued, hot_ready, turned, hotT_in, expanded, product_in, apart_in, dst2_in, scaled_in, summed, added, squared, logq_in, root_in,
         z_in, logs_in, factors_in, before_done, after_done) = (sem("l2_" + n) for n in (
             "idx_set", "issued", "hot_ready", "turned", "hotT_in", "expanded", "product_in", "apart_in", "dst2_in", "scaled_in", "summed", "added",
             "squared", "logq_in", "root_in", "z_in", "logs_in", "factors_in", "before_done", "after_done"))

        def ticks(eng):
            for u, i, j in pairs(eng, BALL_PAIRS, RB):
                yield u, i, j, i * NH + j // HB, j % HB

        with nc.Block() as block:
            @block.gpsimd
            def _(pool):
                for u, i, j, h, _ in ticks(pool):
                    gather_pair(nc, pool, u, j, idx, idx_set, issued, rows, k.x2_table, gathered)

            @block.scalar
            def _(act):
                act.preload_act_table_set("natural_log_exp_and_others")
                AHEAD = 4

                def indices(u, j):
                    wait(act, scaled_in, u * G + (1 - RB) * G)
                    set_indices(nc, k, idx, u, j, idx_set)

                def distances(u, j):
                    for e in range(G):
                        last = nc.scalar.activation(apart[:, j % 2, e, :], k.iota[:, :], ACT.Abs, bias=col(k.rel_t, u * G + e), scale=-1.0)
                    last.then_inc(apart_in, 1)

                def one_hot(u, j):
                    act.wait_ge(apart_in, u + 1)
                    nc.scalar.activation(hot[:, j, :, :], apart[:, j % 2, :, :], ACT.Relu, bias=1.0, scale=-1.0).then_inc(hot_ready, 1)

                def copy_hot(u, j):
                    act.wait_ge(turned, u + 1)
                    wait(act, expanded, u - 3)
                    nc.scalar.activation(hotT[:, j % 4, :, :], turn[j % 2][:, :, 0:P], ACT.Copy).then_inc(hotT_in, 1)

                def scale_rows(u, h, j):
                    act.wait_ge(factors_in, h + 1)
                    wait(act, summed, u - 1)
                    nc.scalar.activation(scaled[:, j % 2, :, D], fdst[:, j // HB, j % HB, :], ACT.Copy)
                    for e in range(G):
                        nc.scalar.activation(scaled[:, j % 2, e, 0:D], rows[:, j, e, 0:D], ACT.Copy, scale=fsrc[:, j // HB, j % HB, e:e + 1]
                                             ).then_inc(scaled_in, 1)

                def roots(h, b):
                    act.wait_ge(squared, h + 1)
                    nc.scalar.activation(root[:, b, :, :], q[:, b, :, :], ACT.Ln).then_inc(logq_in, 1)
                    act.wait_ge(logq_in, h + 1)
                    nc.scalar.activation(root[:, b, :, :], root[:, b, :, :], ACT.Exp, scale=0.5).then_inc(root_in, 1)

                def logs(h, b):
                    act.wait_ge(z_in, h + 1)
                    nc.scalar.activation(la[:, b, :, :], z[:, b, :, :], ACT.Ln, bias=1.0, scale=1.0)
                    nc.scalar.activation(lb[:, b, :, :], z[:, b, :, :], ACT.Ln, bias=1.0, scale=-1.0).then_inc(logs_in, 1)

                for u in range(AHEAD):
                    indices(u, u)
                distances(0, 0)
                distances(1, 1)
                one_hot(0, 0)
                copy_hot(0, 0)
                distances(2, 2)
                one_hot(1, 1)
                copy_hot(1, 1)
                distances(3, 3)
                one_hot(2, 2)
                for u, i, j, h, p in ticks(act):
                    if reached(u, LAG):
                        scale_rows(u - LAG, h + (p - LAG) // HB, (j - LAG) % RB)
                    one_hot(u + 3, (j + 3) % RB)
                    copy_hot(u + 2, (j + 2) % RB)
                    distances(u + 4, (j + 4) % RB)
                    indices(u + AHEAD, (j + AHEAD) % RB)
                    if p == 2 and reached(u, HB):
                        roots(h - 1, (j // HB - 1) % NH)
                    if p == 1 and reached(u, 2 * HB):
                        logs(h - 2, (j // HB - 2) % NH)
                last_group = BALL_PAIRS // HB - 1
                logs(last_group - 1, (last_group - 1) % NH)
                roots(last_group, last_group % NH)
                logs(last_group, last_group % NH)
                for u in range(BALL_PAIRS - LAG, BALL_PAIRS):
                    scale_rows(u, u // HB, u % RB)

            @block.vector
            def _(dve):
                before, after = Linked(dve, before_done, 15), Linked(dve, after_done, 6)
                there = Windows(k, dve, LAG + 1)
                V = nc.vector

                def inner(u, i, j, e):
                    if e == 0:
                        dve.wait_ge(gathered[j], i * 16 * G + 16 * G)
                        dve.wait_ge(expanded, u + 1)
                        wait(dve, product_in, u * G - G)
                    V.tensor_tensor_reduce(out=junk[:, j % 2, e, :], in0=rows[:, j, e, 0:D], in1=base[j % 2][:, e, 0:D], scale=1.0, scalar=0.0,
                                           op0=ALU.mult, op1=ALU.add, accum_out=dot[:, j // HB, j % HB, e:e + 1]).then_inc(product_in, 1)

                def take_dst2(j):
                    V.tensor_copy(dst2[:, j // HB, j % HB, :], base[j % 2][:, :, D]).then_inc(dst2_in, 1)

                def small(p, n, h, b):
                    link = after if p == 3 else before
                    def f(t):
                        return t[:, b, :, :]
                    src2 = rows[:, b * HB:(b + 1) * HB, :, D]
                    if (p, n) in ((0, 0), (3, 0)):
                        link.start(h)
                    else:
                        link.wait()
                    if (p, n) == (0, 0):
                        dve.wait_ge(product_in, h * (HB * G) + HB * G)
                        link(V.scalar_tensor_tensor(f(gap), f(dot), -2.0, src2, ALU.mult, ALU.add))
                    elif (p, n) == (0, 1):
                        dve.wait_ge(dst2_in, h * HB + HB)
                        link(V.tensor_tensor(f(prod2), f(dst2), src2, ALU.mult))
                    elif (p, n) == (0, 2):
                        link(V.tensor_tensor(f(q), f(gap), f(dst2), ALU.add))
                    elif (p, n) == (0, 3):
                        link(V.scalar_tensor_tensor(f(den), f(dot), -2.0, f(prod2), ALU.mult, ALU.add))
                    elif (p, n) == (0, 4):
                        link(V.tensor_scalar(f(q), f(q), 0.0, None, ALU.max))
                    elif (p, n) == (0, 5):
                        link(V.tensor_scalar(f(den), f(den), 1.0, 0.0, ALU.add, ALU.max))
                    elif (p, n) == (1, 0):
                        link(V.tensor_tensor(f(q), f(q), f(den), ALU.mult))
                    elif (p, n) == (1, 1):
                        V.tensor_scalar(f(q), f(q), ROOT_MIN, None, ALU.max).then_inc(squared, 1)
                    elif (p, n) == (1, 2):
                        link(V.tensor_scalar(f(den), f(den), MIN_NORM, None, ALU.max))
                    elif (p, n) == (1, 3):
                        link(V.reciprocal(f(rden), f(den)))
                    elif (p, n) == (1, 4):
                        link(V.tensor_scalar(f(kb), f(dst2), -1.0, 1.0, ALU.mult, ALU.add))
                    elif (p, n) == (2, 0):
                        dve.wait_ge(root_in, h + 1)
                        link(V.reciprocal(f(rroot), f(root)))
                    elif (p, n) == (2, 1):
                        link(V.tensor_tensor(f(rroot), f(rroot), f(q), ALU.mult))
                    elif (p, n) == (2, 2):
                        link(V.tensor_tensor(f(root), f(root), f(rroot), ALU.add))
                    elif (p, n) == (2, 3):
                        link(V.scalar_tensor_tensor(f(sn), f(root), 0.5, f(rden), ALU.mult, ALU.mult))
                    elif (p, n) == (2, 4):
                        link(V.tensor_scalar(f(sn), f(sn), MIN_NORM, None, ALU.max))
                    elif (p, n) == (2, 5):
                        V.tensor_scalar(f(z), f(sn), Z_MAX, None, ALU.min).then_inc(z_in, 1)
                    elif (p, n) == (3, 0):
                        link(V.reciprocal(f(rroot), f(sn)))
                    elif (p, n) == (3, 1):
                        dve.wait_ge(logs_in, h + 1)
                        link(V.tensor_tensor(f(g), f(la), f(lb), ALU.subtract))
                    elif (p, n) == (3, 2):
                        link(V.tensor_tensor(f(g), f(g), f(rroot), ALU.mult))
                    elif (p, n) == (3, 3):
                        link(V.scalar_tensor_tensor(f(g), f(g), 0.5, f(rden), ALU.mult, ALU.mult))
                    elif (p, n) == (3, 4):
                        weight = k.ew_t[:, bass.DynSlice(h * (HB * G), HB * G)].rearrange("p (u e) -> p u e", e=G)
                        link(V.tensor_tensor(f(g), f(g), weight, ALU.mult))
                    elif (p, n) == (3, 5):
                        link(V.scalar_tensor_tensor(f(fdst), f(gap), 1.0, f(g), ALU.add, ALU.mult))
                        V.tensor_tensor(f(fsrc), f(g), f(kb), ALU.mult).then_inc(factors_in, 1)

                for u, i, j, h, p in ticks(dve):
                    def between(n):
                        part, back = ((0, 1), (1, 1), (3, 2), (2, 1))[p]
                        if reached(u, back * HB):
                            small(part, n, h - back, (j // HB - back) % NH)
                    between(0)
                    inner(u, i, j, 0)
                    between(1)
                    inner(u, i, j, 1)
                    between(2)
                    take_dst2(j)
                    between(3)
                    if reached(u, LAG + 1):
                        accumulate(nc, k, dve, u - LAG - 1, there(u, j), seg[(j - LAG - 1) % 2], AW, summed, added)
                    between(4)
                    between(5)
                last_group = BALL_PAIRS // HB - 1
                for part, h in ((0, last_group), (1, last_group), (3, last_group - 1), (2, last_group), (3, last_group)):
                    for n in range(6):
                        small(part, n, h, h % NH)
                for u in range(BALL_PAIRS - LAG - 1, BALL_PAIRS):
                    accumulate(nc, k, dve, u, there(u + LAG + 1, 0), seg[u % 2], AW, summed, added)

            @block.tensor
            def _(pe):
                mm = nc.tensor.matmul
                here = Windows(k, pe, 0)

                def turn_hot(u, j):
                    pe.wait_ge(hot_ready, u + 1)
                    wait(pe, hotT_in, u - 1)
                    for e in range(G):
                        last = nc.tensor.transpose(turn[j % 2][:, e, 0:P], hot[:, j, e, :], k.ident[:, :])
                    last.then_inc(turned, 1)

                def expand(u, j, w):
                    pe.wait_ge(hotT_in, u + 1)
                    wait(pe, dst2_in, u - 1)
                    for e in range(G):
                        mm(base[j % 2][:, e, 0:AW + 1], hotT[:, j % 4, e, :], at(x_high, w), start=True, stop=False)
                        last = mm(base[j % 2][:, e, 0:AW + 1], hotT[:, j % 4, e, :], at(x_low, w), start=False, stop=True)
                    last.then_inc(expanded, 1)

                def segment(u, j):
                    pe.wait_ge(scaled_in, u * G + G)
                    wait(pe, added, u - 1)
                    for e in range(G):
                        last = mm(seg[j % 2][:, 0:AW], hot[:, j, e, :], scaled[:, j % 2, e, :], start=(e == 0), stop=(e == G - 1))
                    last.then_inc(summed, 1)

                turn_hot(0, 0)
                turn_hot(1, 1)
                for u, i, j, h, p in ticks(pe):
                    turn_hot(u + 2, (j + 2) % RB)
                    expand(u, j, here(u, j))
                    if reached(u, LAG):
                        segment(u - LAG, (j - LAG) % RB)
                for u in range(BALL_PAIRS - LAG, BALL_PAIRS):
                    segment(u, u % RB)


def nodes_ball(nc, k, sb, ps, sem):
    ctx = ExitStack()
    with ctx:
        def tmp(name, shape, dt=FP32):
            return ctx.enter_context(nc.sbuf_tensor(name, shape, dt))
        mx = tmp("n2_mx", [P, W, D])
        uT = tmp("n2_uT", [P, 2, D])
        junk = tmp("n2_junk", [P, 2, D])
        bball = tmp("n2_bball", [P, D])
        part = tmp("n2_part", [P, 2, D])
        S = {n: tmp("n2_" + n, [P, W]) for n in (
            "s2", "xm", "il", "r", "un", "t1", "t2", "q", "y2", "xy", "den", "c1", "c2", "xn2", "mb", "mxn2", "xn", "mxn", "z", "la",
            "lb", "f", "d1", "d2", "hn2", "r2", "al", "sr", "e")}
        bs = {n: tmp("n2_b" + n, [P, 1]) for n in ("n2", "n", "t", "y2")}
        turn = [ctx.enter_context(nc.psum_tensor(f"n2_turn{b}", [P, D], FP32)) for b in range(2)]
        prod = [ctx.enter_context(nc.psum_tensor(f"n2_prod{b}", [P, 512], FP32)) for b in range(2)]
        (ch, args_ready, function_in, combined, s2_in, u_in, turned, uT_in, multiplied, mx_in, h_in, relu_in, r2_in, xn2_in, hn2_in, part_in) = (
            sem("n2_" + n) for n in ("ch", "args_ready", "function_in", "combined", "s2_in", "u_in", "turned", "uT_in", "multiplied",
                                     "mx_in", "h_in", "relu_in", "r2_in", "xn2_in", "hn2_in", "part_in"))

        def v(name):
            return S[name][:, :]

        with nc.Block() as block:
            @block.vector
            def _(dve):
                link = Chain(dve, ch)
                V = nc.vector

                def tt(out, a, b, op):
                    link(V.tensor_tensor(v(out), v(a), v(b), op))

                def ts(out, a, s1, s2, op0, op1=None):
                    link(V.tensor_scalar(v(out), v(a), s1, s2, op0, op1) if op1 is not None else V.tensor_scalar(v(out), v(a), s1, None, op0))

                def rec(out, a):
                    link(V.reciprocal(v(out), v(a)))

                def by_scalar(n):
                    dve.sem_inc(args_ready, 1)
                    dve.wait_ge(function_in, n)

                def artanh2(out, a, n):
                    ts("z", a, Z_MAX, None, ALU.min)
                    by_scalar(n)
                    tt(out, "la", "lb", ALU.subtract)

                x2 = k.xs[:, :, D]
                for w in range(W):
                    V.scalar_tensor_tensor(k.agg[:, w, 0:D], k.xs[:, w, 0:D], k.agg[:, w, D:AW], k.agg[:, w, 0:D], ALU.mult, ALU.subtract
                                           ).then_inc(combined, 1)
                    dve.wait_ge(combined, w + 1)
                    wait(dve, part_in, w - 1)
                    V.tensor_tensor_reduce(out=part[:, w % 2, :], in0=k.xs[:, w, 0:D], in1=k.agg[:, w, 0:D], scale=1.0, scalar=0.0,
                                           op0=ALU.mult, op1=ALU.add, accum_out=S["xm"][:, w:w + 1]).then_inc(part_in, 1)
                link(V.tensor_scalar(v("il"), x2, -1.0, 1.0, ALU.mult, ALU.add))
                link(V.tensor_copy(v("t2"), v("il")))
                ts("il", "il", MIN_NORM, None, ALU.max)
                rec("il", "il")
                ts("r", "il", 2.0, MIN_NORM, ALU.mult, ALU.max)
                rec("il", "r")
                ts("il", "il", 2.0, None, ALU.mult)
                dve.wait_ge(s2_in, W)
                by_scalar(1)
                tt("un", "un", "il", ALU.mult)
                ts("un", "un", MIN_NORM, None, ALU.max)
                tt("r", "r", "un", ALU.mult)
                by_scalar(2)
                tt("q", "q", "il", ALU.mult)
                rec("un", "un")
                tt("q", "q", "un", ALU.mult)
                tt("y2", "q", "q", ALU.mult)
                tt("y2", "y2", "s2", ALU.mult)
                tt("xy", "q", "xm", ALU.mult)
                ts("xy", "xy", -2.0, 1.0, ALU.mult, ALU.add)
                link(V.tensor_tensor(v("den"), x2, v("y2"), ALU.mult))
                tt("den", "den", "xy", ALU.add)
                ts("den", "den", MIN_NORM, None, ALU.max)
                rec("den", "den")
                tt("c1", "xy", "y2", ALU.add)
                tt("c1", "c1", "den", ALU.mult)
                tt("c2", "t2", "q", ALU.mult)
                tt("c2", "c2", "den", ALU.mult)
                for w in range(W):
                    V.tensor_scalar(part[:, w % 2, :], k.agg[:, w, 0:D], S["c2"][:, w:w + 1], None, ALU.mult).then_inc(combined, 1)
                    dve.wait_ge(combined, W + w + 1)
                    V.scalar_tensor_tensor(k.agg[:, w, 0:D], k.xs[:, w, 0:D], S["c1"][:, w:w + 1], part[:, w % 2, :], ALU.mult, ALU.subtract
                                           ).then_inc(u_in, 1)
                link(V.tensor_tensor_reduce(out=part[:, 0, :], in0=k.bias2[:, :], in1=k.bias2[:, :], scale=1.0, scalar=0.0,
                                            op0=ALU.mult, op1=ALU.add, accum_out=bs["n2"][:, :]))
                by_scalar(3)
                link(V.tensor_scalar(bs["n"][:, :], bs["n"][:, :], MIN_NORM, None, ALU.max))
                by_scalar(4)
                link(V.reciprocal(bs["n"][:, :], bs["n"][:, :]))
                link(V.tensor_tensor(bs["t"][:, :], bs["t"][:, :], bs["n"][:, :], ALU.mult))
                link(V.tensor_scalar(bball[:, :], k.bias2[:, :], bs["t"][:, 0:1], None, ALU.mult))
                link(V.tensor_tensor(bs["y2"][:, :], bs["t"][:, :], bs["t"][:, :], ALU.mult))
                link(V.tensor_tensor(bs["y2"][:, :], bs["y2"][:, :], bs["n2"][:, :], ALU.mult))
                for w in range(W):
                    dve.wait_ge(mx_in, w + 1)
                    dve.wait_ge(part_in, W + w - 1)
                    V.tensor_tensor_reduce(out=part[:, w % 2, :], in0=mx[:, w, :], in1=bball[:, :], scale=1.0, scalar=0.0,
                                           op0=ALU.mult, op1=ALU.add, accum_out=S["mb"][:, w:w + 1]).then_inc(part_in, 1)
                dve.wait_ge(part_in, 2 * W)
                by_scalar(5)
                ts("xn", "xn", MIN_NORM, None, ALU.max)
                ts("mxn", "mxn", MIN_NORM, None, ALU.max)
                artanh2("f", "xn", 6)
                rec("xn", "xn")
                tt("f", "f", "xn", ALU.mult)
                tt("f", "f", "mxn", ALU.mult)
                by_scalar(7)
                rec("mxn", "mxn")
                tt("f", "f", "mxn", ALU.mult)
                tt("xn2", "f", "f", ALU.mult)
                tt("xn2", "xn2", "mxn2", ALU.mult)
                tt("xy", "f", "mb", ALU.mult)
                ts("xy", "xy", 2.0, 1.0, ALU.mult, ALU.add)
                link(V.scalar_tensor_tensor(v("den"), v("xn2"), bs["y2"][:, 0:1], v("xy"), ALU.mult, ALU.add))
                ts("den", "den", MIN_NORM, None, ALU.max)
                rec("den", "den")
                link(V.scalar_tensor_tensor(v("d1"), v("xy"), bs["y2"][:, 0:1], v("f"), ALU.add, ALU.mult))
                tt("d1", "d1", "den", ALU.mult)
                ts("d2", "xn2", -1.0, 1.0, ALU.mult, ALU.add)
                tt("d2", "d2", "den", ALU.mult)
                for w in range(W):
                    V.tensor_scalar(part[:, w % 2, :], bball[:, :], S["d2"][:, w:w + 1], None, ALU.mult).then_inc(combined, 1)
                    dve.wait_ge(combined, 2 * W + w + 1)
                    V.scalar_tensor_tensor(mx[:, w, :], mx[:, w, :], S["d1"][:, w:w + 1], part[:, w % 2, :], ALU.mult, ALU.add).then_inc(h_in, 1)
                dve.wait_ge(r2_in, W)
                by_scalar(8)
                ts("xn", "xn", MIN_NORM, None, ALU.max)
                artanh2("al", "xn", 9)
                rec("xn", "xn")
                link(V.scalar_tensor_tensor(v("al"), v("al"), 0.5, v("xn"), ALU.mult, ALU.mult))
                tt("mxn", "al", "sr", ALU.mult)
                ts("mxn", "mxn", MIN_NORM, None, ALU.max)
                by_scalar(10)
                rec("mxn", "mxn")
                tt("e", "e", "mxn", ALU.mult)
                tt("e", "e", "al", ALU.mult)
                tt("xn", "e", "sr", ALU.mult)
                ts("xn", "xn", MIN_NORM, None, ALU.max)
                rec("xn", "xn")
                ts("xn", "xn", 1.0 - BALL_EPS, 1.0, ALU.mult, ALU.min)
                tt("e", "e", "xn", ALU.mult)
                for w in range(W):
                    V.scalar_tensor_tensor(k.xs[:, w, 0:D], k.agg[:, w, 0:D], S["e"][:, w:w + 1], k.xs[:, w, 0:D], ALU.mult, ALU.add).then_inc(combined, 1)
                    dve.wait_ge(combined, 3 * W + w + 1)
                    last = V.bn_stats(k.stats[:, w, :], k.xs[:, w, 0:D])
                link(last)
                link(V.memset(k.agg[:, :, :], 0.0))

            @block.tensor
            def _(pe):
                for w in range(W + 1):
                    if w < W:
                        pe.wait_ge(u_in, w + 1)
                        wait(pe, uT_in, w - 1)
                        for c in range(DC):
                            last = nc.tensor.transpose(turn[w % 2][:, c * P:(c + 1) * P], k.agg[:, w, c * P:(c + 1) * P], k.ident[:, :])
                        last.then_inc(turned, 1)
                    if w:
                        b = (w - 1) % 2
                        pe.wait_ge(uT_in, w)
                        wait(pe, mx_in, w - 2)
                        for c in range(DC):
                            last = nc.tensor.matmul(prod[b][:, 0:D], uT[:, b, c * P:(c + 1) * P], k.w2l[:, c, :], start=(c == 0), stop=(c == DC - 1))
                        last.then_inc(multiplied, 1)

            @block.scalar
            def _(act):
                function = nc.scalar.activation

                def square_sum(w, row, name):
                    return function(junk[:, w % 2, :], row, ACT.Square, accum_out=S[name][:, w:w + 1])

                for w in range(W):
                    act.wait_ge(combined, w + 1)
                    wait(act, s2_in, w - 1)
                    square_sum(w, k.agg[:, w, 0:D], "s2").then_inc(s2_in, 1)
                act.wait_ge(args_ready, 1)
                function(v("un"), v("s2"), ACT.Sqrt).then_inc(function_in, 1)
                act.wait_ge(args_ready, 2)
                function(v("q"), v("r"), ACT.Tanh, scale=0.5).then_inc(function_in, 1)
                for w in range(W + 1):
                    if w < W:
                        act.wait_ge(turned, w + 1)
                        wait(act, multiplied, w - 1)
                        function(uT[:, w % 2, :], turn[w % 2][:, :], ACT.Copy).then_inc(uT_in, 1)
                        act.wait_ge(mx_in, w - 1) if w > 1 else act.wait_ge(s2_in, W)
                        square_sum(w, k.agg[:, w, 0:D], "xn2").then_inc(xn2_in, 1)
                    if w:
                        act.wait_ge(multiplied, w)
                        function(mx[:, w - 1, :], prod[(w - 1) % 2][:, 0:D], ACT.Copy)
                        act.wait_ge(xn2_in, w)
                        square_sum(w - 1, prod[(w - 1) % 2][:, 0:D], "mxn2").then_inc(mx_in, 1)
                act.wait_ge(args_ready, 3)
                function(bs["n"][:, :], bs["n2"][:, :], ACT.Sqrt).then_inc(function_in, 1)
                act.wait_ge(args_ready, 4)
                function(bs["t"][:, :], bs["n"][:, :], ACT.Tanh).then_inc(function_in, 1)
                act.wait_ge(args_ready, 5)
                function(v("xn"), v("xn2"), ACT.Sqrt)
                function(v("mxn"), v("mxn2"), ACT.Sqrt).then_inc(function_in, 1)
                act.wait_ge(args_ready, 6)
                function(v("la"), v("z"), ACT.Ln, bias=1.0, scale=1.0)
                function(v("lb"), v("z"), ACT.Ln, bias=1.0, scale=-1.0).then_inc(function_in, 1)
                act.wait_ge(args_ready, 7)
                function(v("f"), v("f"), ACT.Tanh, scale=0.5).then_inc(function_in, 1)
                for w in range(W):
                    act.wait_ge(h_in, w + 1)
                    wait(act, hn2_in, w - 1)
                    square_sum(w, mx[:, w, :], "hn2").then_inc(hn2_in, 1)
                    function(k.agg[:, w, 0:D], mx[:, w, :], ACT.Relu).then_inc(relu_in, 1)
                for w in range(W):
                    act.wait_ge(relu_in, w + 1)
                    wait(act, r2_in, w - 1) if w else act.wait_ge(hn2_in, W)
                    square_sum(w, k.agg[:, w, 0:D], "r2").then_inc(r2_in, 1)
                act.wait_ge(args_ready, 8)
                function(v("xn"), v("hn2"), ACT.Sqrt)
                function(v("sr"), v("r2"), ACT.Sqrt).then_inc(function_in, 1)
                act.wait_ge(args_ready, 9)
                function(v("la"), v("z"), ACT.Ln, bias=1.0, scale=1.0)
                function(v("lb"), v("z"), ACT.Ln, bias=1.0, scale=-1.0).then_inc(function_in, 1)
                act.wait_ge(args_ready, 10)
                function(v("e"), v("mxn"), ACT.Tanh).then_inc(function_in, 1)
    layernorm(nc, k, sem, "n2", k.w13, k.b13, 2 * D, k.p_table)


def edges_gate(nc, k, sb, ps, sem):
    ctx = ExitStack()
    with ctx:
        def tmp(name, shape, dt=FP32):
            return ctx.enter_context(nc.sbuf_tensor(name, shape, dt))
        rows = tmp("l3_rows", [P, R, G, 2 * D])
        attr = tmp("l3_attr", [P, R, G, P])
        stack = tmp("l3_stack", [P, 2, G, P], FP32R)
        hot = tmp("l3_hot", [P, R, G, P], FP32R)
        hidT = tmp("l3_hidT", [P, 2, DC, G, P])
        gsum = tmp("l3_gsum", [P, 2, G, D])
        gate = tmp("l3_gate", [P, 2, G, D])
        msg = tmp("l3_msg", [P, 2, G, D])
        high = tmp("l3_high", [P, 2, G, D], FP32R)
        low = tmp("l3_low", [P, 2, G, D], FP32R)
        bias_hl = tmp("l3_bias", [P, G, D], FP32R)
        w_high = tmp("l3_w_high", [P, 2 * D], FP32R)
        w_low = tmp("l3_w_low", [P, 2 * D], FP32R)
        idx = tmp("l3_idx", [P, R, G], I32)
        split_bias(nc, k, "l3", sem, k.b2, bias_hl, G)
        w_split = sem("l3_w_split")
        with nc.Block() as block:
            @block.scalar
            def _(act):
                nc.scalar.activation(w_high[:, :], k.we3[:, :], ACT.Copy).then_inc(w_split, 1)

            @block.vector
            def _(dve):
                dve.wait_ge(w_split, 1)
                nc.vector.tensor_tensor(w_low[:, :], k.we3[:, :], w_high[:, :].bitcast(FP32), ALU.subtract)
        p_hid, p_gate, p_core = (
            [ctx.enter_context(nc.psum_tensor(f"l3_{n}{j}", [P, G, D], FP32)) for j in range(2)] for n in ("p_hid", "p_gate", "p_core"))
        seg = [ctx.enter_context(nc.psum_tensor(f"l3_seg{j}", [P, 512], FP32)) for j in range(2)]
        gathered = [sem(f"l3_gathered{j}") for j in range(R)]
        attr_in = [sem(f"l3_attr_in{j}") for j in range(R)]
        (idx_set, issued, stack_high, stacked, hot_ready, hid_made, gate_made, hid_in, gsum_in, gate_in, core_made, msg_ready, high_in,
         low_in, summed, added) = (sem("l3_" + n) for n in (
             "idx_set", "issued", "stack_high", "stacked", "hot_ready", "hid_made", "gate_made", "hid_in", "gsum_in", "gate_in",
             "core_made", "msg_ready", "high_in", "low_in", "summed", "added"))
        with nc.Block() as block:
            @block.sync
            def _(sp):
                def load(u, j):
                    wait(sp, stacked, u + 1 - R)
                    t = sp.value_load(k.tile_row[0:1, bass.DynSlice(u * G, 1)], min_val=0, max_val=T - G)
                    for half in range(2):
                        sp.dma_start(attr[half * DE3:(half + 1) * DE3, j, :, :], k.ea3[bass.DynSlice(t, G), :, :].rearrange("g p e -> p g e")
                                     ).then_inc(attr_in[j], 16)

                for u, i, j in pairs(sp):
                    load(u, j)
                load(PAIRS, 0)

            @block.gpsimd
            def _(pool):
                for u, i, j in pairs(pool):
                    gather_pair(nc, pool, u, j, idx, idx_set, issued, rows, k.p_table, gathered)

            @block.scalar
            def _(act):
                AHEAD = 3
                F = nc.scalar.activation

                def indices(u, j):
                    wait(act, hid_made, u + 1 - R)
                    wait(act, gsum_in, u + 1 - R)
                    set_indices(nc, k, idx, u, j, idx_set)

                def stack_up(u, i, j):
                    act.wait_ge(attr_in[j], i * 32 + 32)
                    wait(act, gate_made, u - 1)
                    F(stack[:, j % 2, :, :], attr[:, j, :, :], ACT.Copy).then_inc(stack_high, 1)

                def split_high(u, b):
                    act.wait_ge(msg_ready, u + 1)
                    wait(act, summed, u - 1)
                    F(high[:, b, :, :], msg[:, b, :, :], ACT.Copy).then_inc(high_in, 1)

                for u in range(AHEAD):
                    indices(u, u)
                stack_up(0, 0, 0)
                for u, i, j in pairs(act):
                    b = j % 2
                    stack_up(u + 1, i + (j + 1) // R, (j + 1) % R)
                    act.wait_ge(hid_made, u + 1)
                    wait(act, core_made, u - 1)
                    F(hidT[:, b, :, :, :], p_hid[b][:, :, :].rearrange("p c (g e) -> p c g e", e=P), ACT.Relu).then_inc(hid_in, 1)
                    indices(u + AHEAD, (j + AHEAD) % R)
                    act.wait_ge(gsum_in, u + 1)
                    wait(act, msg_ready, u - 1)
                    F(gate[:, b, :, :], gsum[:, b, :, :], ACT.Sigmoid).then_inc(gate_in, 1)
                    if reached(u, 1):
                        split_high(u - 1, 1 - b)
                split_high(PAIRS - 1, (PAIRS - 1) % 2)

            @block.vector
            def _(dve):
                V = nc.vector
                there = Windows(k, dve, 3)

                def stack_low(u, j):
                    dve.wait_ge(stack_high, u + 1)
                    V.tensor_tensor(stack[DE3:P, j % 2, :, :], attr[DE3:P, j, :, :], stack[DE3:P, j % 2, :, :].bitcast(FP32), ALU.subtract
                                    ).then_inc(stacked, 1)

                def message(u, b):
                    dve.wait_ge(core_made, u + 1)
                    dve.wait_ge(gate_in, u + 1)
                    wait(dve, low_in, u - 1)
                    V.tensor_tensor(msg[:, b, :, :], p_core[b][:, :, :], gate[:, b, :, :], ALU.mult).then_inc(msg_ready, 1)

                def split_low(u, b):
                    dve.wait_ge(high_in, u + 1)
                    wait(dve, summed, u - 1)
                    V.tensor_tensor(low[:, b, :, :], msg[:, b, :, :], high[:, b, :, :].bitcast(FP32), ALU.subtract).then_inc(low_in, 1)

                stack_low(0, 0)
                for u, i, j in pairs(dve):
                    b = j % 2
                    stack_low(u + 1, (j + 1) % R)
                    if reached(u, 2):
                        split_low(u - 2, b)
                    one_hots(nc, k, u, j, hot, hot_ready)
                    dve.wait_ge(gate_made, u + 1)
                    wait(dve, gate_in, u - 1)
                    V.tensor_tensor(gsum[:, b, :, :], p_gate[b][:, :, :], rows[:, j, :, D:2 * D], ALU.add).then_inc(gsum_in, 1)
                    if reached(u, 1):
                        message(u - 1, 1 - b)
                    if reached(u, 3):
                        accumulate(nc, k, dve, u - 3, there(u, j), seg[1 - b], D, summed, added)
                message(PAIRS - 1, 1)
                split_low(PAIRS - 2, 0)
                split_low(PAIRS - 1, 1)
                for u in range(PAIRS - 3, PAIRS):
                    accumulate(nc, k, dve, u, there(u + 3, 0), seg[u % 2], D, summed, added)

            @block.tensor
            def _(pe):
                mm = nc.tensor.matmul

                def hidden(u, i, j):
                    b = j % 2
                    pe.wait_ge(gathered[j], i * 16 * G + 16 * G)
                    pe.wait_ge(stacked, u + 1)
                    wait(pe, hid_in, u - 1)
                    for c in range(DC):
                        f = slice(c * P, (c + 1) * P)
                        for e in range(G):
                            mm(p_hid[b][:, c, e * P:(e + 1) * P], rows[:, j, e, f], k.ident[:, :], is_transpose=True, start=(e == 0), stop=False)
                        for part in (w_high, w_low):
                            last = mm(p_hid[b][:, c, :], part[:, f], stack[:, b, :, :], start=False, stop=(part is w_low))
                    last.then_inc(hid_made, 1)

                def gates(u, j):
                    b = j % 2
                    wait(pe, gsum_in, u - 1)
                    for e in range(G):
                        for part in (w_high, w_low):
                            last = mm(p_gate[b][:, e, :], stack[:, b, e, :], part[:, D:2 * D], start=(part is w_high), stop=(part is w_low))
                    last.then_inc(gate_made, 1)

                def times_w2(u, b):
                    pe.wait_ge(hid_in, u + 1)
                    wait(pe, msg_ready, u - 1)
                    mm(p_core[b][:, :, :], k.ones_r[:, :], bias_hl[:, :, :], start=True, stop=False)
                    for e in range(G):
                        for c in range(DC):
                            last = mm(p_core[b][:, e, :], hidT[:, b, c, e, :], k.w2[:, c, :], start=False, stop=(e == G - 1 and c == DC - 1))
                    last.then_inc(core_made, 1)

                def segment(u, j):
                    b = j % 2
                    pe.wait_ge(hot_ready, u + 1)
                    pe.wait_ge(high_in, u + 1)
                    pe.wait_ge(low_in, u + 1)
                    wait(pe, added, u - 1)
                    for e in range(G):
                        for n, part in enumerate((high, low)):
                            last = mm(seg[b][:, 0:D], hot[:, j, e, :], part[:, b, e, :], start=(e == 0 and n == 0), stop=(e == G - 1 and n == 1))
                    last.then_inc(summed, 1)

                for u, i, j in pairs(pe):
                    hidden(u, i, j)
                    gates(u, j)
                    if reached(u, 1):
                        times_w2(u - 1, (j - 1) % 2)
                    if reached(u, 2):
                        segment(u - 2, (j - 2) % R)
                times_w2(PAIRS - 1, 1)
                segment(PAIRS - 2, R - 2)
                segment(PAIRS - 1, R - 1)


def nodes_gate(nc, k, sb, ps, sem):
    ctx = ExitStack()
    with ctx:
        mv = ctx.enter_context(nc.sbuf_tensor("n3a_mv", [P, W, 2], FP32))
        rstd = ctx.enter_context(nc.sbuf_tensor("n3a_rstd", [P, W], FP32))
        ch, var_in, root_in = (sem("n3_" + n) for n in ("ch", "var_in", "root_in"))
        with nc.Block() as block:
            @block.scalar
            def _(act):
                act.wait_ge(var_in, 1)
                nc.scalar.activation(rstd[:, :], rstd[:, :], ACT.Sqrt).then_inc(root_in, 1)

            @block.vector
            def _(dve):
                V = nc.vector
                link = Chain(dve, ch)
                for w in link.loop(W // 2, 2):
                    for b in range(2):
                        link.count(V.tensor_tensor(at(k.agg, w * 2 + b, D), at(k.agg, w * 2 + b, D), at(k.xs, w * 2 + b, D), ALU.add))
                    for b in range(2):
                        link.wait(1 - b)
                        V.bn_stats(at(k.stats, w * 2 + b), at(k.agg, w * 2 + b, D))
                link(V.memset(rstd[:, :], LN_EPS))
                for w in range(W):
                    last = V.bn_aggr(mv[:, w, :], k.stats[:, w, :])
                link(last)
                V.tensor_tensor(rstd[:, :], mv[:, :, 1], rstd[:, :], ALU.add).then_inc(var_in, 1)
                dve.wait_ge(root_in, 1)
                link(V.reciprocal(rstd[:, :], rstd[:, :]))
                for i in link.loop(W // 2, 8):
                    both = [(i * 2 + b, b) for b in range(2)]
                    for w, b in both:
                        link.count(V.tensor_scalar(at(k.agg, w, D), at(k.agg, w, D), mv[:, bass.DynSlice(w, 1), 0], col(rstd, w), ALU.subtract, ALU.mult))
                    for w, b in both:
                        link.wait(1)
                        link.count(V.tensor_tensor(at(k.agg, w, D), at(k.agg, w, D), k.gamma[:, :], ALU.mult))
                    for w, b in both:
                        link.wait(1)
                        link.count(V.tensor_tensor(at(k.agg, w, D), at(k.agg, w, D), k.beta[:, :], ALU.add))
                    for w, b in both:
                        link.wait(1)
                        link.count(V.tensor_tensor(at(k.xs, w, D), at(k.xs, w, D), at(k.agg, w, D), ALU.add))
                    for w, b in both:
                        link.wait(1 - b)
                        V.bn_stats(at(k.stats, w), at(k.xs, w, D))
    layernorm(nc, k, sem, "n3", None, None, 0, None)


def finish(nc, k, sem, src):
    out_stored = sem("out_stored")
    with nc.Block() as block:
        @block.sync
        def _(sp):
            sp.dma_start(k.out[0:(W - 1) * P, :].rearrange("(w p) f -> p w f", p=P), src[:, 0:W - 1, 0:D]).then_inc(out_stored, 16)
            sp.dma_start(k.out[(W - 1) * P:N, :], src[0:TAIL, W - 1, 0:D]).then_inc(out_stored, 16)
            sp.wait_ge(out_stored, 32)


def gnn_kernel(nc, args, out):
    k = Parts(args, out)
    ctx = ExitStack()
    with ctx:
        def sb(name, shape, dt):
            return ctx.enter_context(nc.sbuf_tensor(name, shape, dt))

        def ps(name, shape, dt):
            return ctx.enter_context(nc.psum_tensor(name, shape, dt))

        live = []

        def sem(name):
            live.append(nc.alloc_semaphore(name))
            return live[-1]

        def phase(build, *more):
            build(nc, k, *more)
            nc.clear_and_free_semaphores(live)
            nc.all_engine_barrier()
            live.clear()
        k.h = nc.dram_tensor("h_table", (W * P, D), FP32).ap()
        k.x2_table = nc.dram_tensor("x2_table", (W * P, AW), FP32).ap()
        k.p_table = nc.dram_tensor("p_table", (W * P, 2 * D), FP32).ap()
        first_layers = ExitStack()
        with first_layers:
            phase(setup, sb, lambda *tensor: first_layers.enter_context(nc.sbuf_tensor(*tensor)), sem)
            phase(edges_mean, sb, ps, sem)
            phase(nodes_mean, sb, ps, sem)
            phase(edges_spline, sb, ps, sem)
            phase(nodes_spline, sb, ps, sem)
        phase(norms, sem)
        phase(edges_ball, sb, ps, sem)
        phase(nodes_ball, sb, ps, sem)
        phase(edges_gate, sb, ps, sem)
        phase(nodes_gate, sb, ps, sem)
        phase(finish, sem, k.xs)


def kernel(x, src, dst, edge_attr_384, edge_attr_64, edge_weight, L0_gnn_W_l, L0_gnn_W_r, L0_gnn_b_r, L1_gnn_W_edge,
           L1_gnn_b_edge, L1_gnn_W_node, L1_gnn_b_node, L1_gnn_base_weight, L1_gnn_spline_weight, L1_gnn_spline_scaler,
           L2_gnn_weight, L2_gnn_bias, L3_gnn_W1, L3_gnn_b1, L3_gnn_W2, L3_gnn_b2, L3_gnn_Wg, L3_gnn_bg, L3_gnn_gamma,
           L3_gnn_beta):
    import numpy as np
    import concourse.bacc as bacc
    from concourse.bass_utils import run_bass_kernel_spmd

    ins = {
        "x": x, "src": src, "dst": dst, "edge_weight": edge_weight,
        "wl_t": np.asarray(L0_gnn_W_l).T, "wr_t": np.asarray(L0_gnn_W_r).T, "b_r": L0_gnn_b_r,
        "wn_t": np.asarray(L1_gnn_W_node).T, "b_node": L1_gnn_b_node, "we_t": np.asarray(L1_gnn_W_edge).T, "b_edge": L1_gnn_b_edge,
        "ea1": np.asarray(edge_attr_384).reshape(T, P, KC1, P).transpose(0, 3, 2, 1),
        "base_t": np.asarray(L1_gnn_base_weight).T, "scaler_t": np.asarray(L1_gnn_spline_scaler).T,
        "spline_t": np.asarray(L1_gnn_spline_weight).transpose(2, 1, 0),
        "w2l_t": np.asarray(L2_gnn_weight).T, "l2_bias": L2_gnn_bias,
        "ea3": np.asarray(edge_attr_64).reshape(T, P, DE3).transpose(0, 2, 1),
        "w1": L3_gnn_W1, "b1": L3_gnn_b1, "w2_in": L3_gnn_W2, "b2_in": L3_gnn_b2, "wg": L3_gnn_Wg, "bg": L3_gnn_bg,
        "gamma_in": L3_gnn_gamma, "beta_in": L3_gnn_beta,
    }
    nc = bacc.Bacc("TRN2", target_bir_lowering=False, num_devices=1)
    arrays, args = {}, {}
    for name, a in ins.items():
        a = np.ascontiguousarray(a)
        arrays[f"in_{name}"] = a
        args[name] = nc.dram_tensor(f"in_{name}", a.shape, mybir.dt.from_np(a.dtype), kind="ExternalInput").ap()
    out = nc.dram_tensor("out_0", (N, D), FP32, kind="ExternalOutput").ap()
    gnn_kernel(nc, args, out)
    r = run_bass_kernel_spmd(nc, [arrays], core_ids=[0])
    return r.results[0]["out_0"]
```
